# Optimizing a Trainium2 kernel written in Bass

```python
import numpy as np
import jax
import jax.numpy as jnp

def _softmax(x, axis=-1):
    return jax.nn.softmax(x, axis=axis)

def _gelu(x):
    return jax.nn.gelu(x, approximate=True)

def _silu(x):
    return jax.nn.silu(x)

def _sigmoid(x):
    return jax.nn.sigmoid(x)

def _layernorm(x, axis=-1, eps=1e-05):
    m = jnp.mean(x, axis=axis, keepdims=True)
    v = jnp.var(x, axis=axis, keepdims=True)
    return (x - m) / jnp.sqrt(v + eps)

def _scatter_add(tgt, idx, src, axis=0):
    return tgt.at[idx].add(src)

def _segment_sum(src, seg, n):
    return jax.ops.segment_sum(src, seg, n)
kernel_name = 'mk_sandwich_d2_jaxref_r8_f27ae2'

def setup_inputs(seed: int=0):
    np.random.seed(seed)
    _w = jnp.asarray

    def _L0_attn_setup():
        import jax, jax.numpy as jnp
        import numpy as np
        NUM_HEADS = 16
        HIDDEN = 128
        HEAD_DIM = HIDDEN // NUM_HEADS
        GROUP_SIZE = 32

        def _attention(q, k, v, head_dim):
            scores = jnp.einsum('bghqd,bghkd->bghqk', q, k) / head_dim ** 0.5
            w = jax.nn.softmax(scores, axis=-1)
            return jnp.einsum('bghqk,bghkd->bghqd', w, v)
        key = jax.random.key(seed)
        k1, k2, k3 = jax.random.split(key, 3)
        hidden_states = jax.random.normal(k1, (2, 1024, HIDDEN), dtype=jnp.float32)
        w_qkv = jax.random.normal(k2, (3 * HIDDEN, HIDDEN), dtype=jnp.float32) * 0.02
        b_qkv = jax.random.normal(k3, (3 * HIDDEN,), dtype=jnp.float32) * 0.02
        return {'hidden_states': hidden_states, 'w_qkv': w_qkv, 'b_qkv': b_qkv}
    _L0_attn_in = _L0_attn_setup()

    def _L0_ffn_setup():
        import jax, jax.numpy as jnp
        import numpy as np
        NUM_NOD = 6
        MAX_PREV = 5
        NUM_EDGE = 20
        D = 128
        H = 8
        LN_EPS = 1e-06

        def _layernorm(x, g, b):
            mu = jnp.mean(x, axis=-1, keepdims=True)
            var = jnp.mean(jnp.square(x - mu), axis=-1, keepdims=True)
            return (x - mu) * jax.lax.rsqrt(var + LN_EPS) * g + b

        def _mha(q, k, v, wq, wk, wv, wo):
            B, S, d = q.shape
            dh = d // H
            qh = (q @ wq).reshape(B, S, H, dh)
            kh = (k @ wk).reshape(B, S, H, dh)
            vh = (v @ wv).reshape(B, S, H, dh)
            scores = jnp.einsum('bqhd,bkhd->bhqk', qh, kh) / jnp.sqrt(jnp.asarray(dh, q.dtype))
            attn = jax.nn.softmax(scores, axis=-1)
            ctx = jnp.einsum('bhqk,bkhd->bqhd', attn, vh).reshape(B, S, d)
            return ctx @ wo
        key = jax.random.key(seed)
        ks = jax.random.split(key, 12)
        B, S = (8, 128)
        scale = 1.0 / np.sqrt(D)
        return {'inputs': jax.random.normal(ks[0], (B, S, D), jnp.float32), 'ew': jax.random.uniform(ks[1], (NUM_NOD, 3), jnp.float32), 'act_w': jax.random.uniform(ks[2], (NUM_NOD,), jnp.float32), 'We': jax.random.normal(ks[3], (NUM_EDGE, D, D), jnp.float32) * scale, 'be': jnp.zeros((NUM_EDGE, D), jnp.float32), 'Wq': jax.random.normal(ks[4], (NUM_NOD, D, D), jnp.float32) * scale, 'Wk': jax.random.normal(ks[5], (NUM_NOD, D, D), jnp.float32) * scale, 'Wv': jax.random.normal(ks[6], (NUM_NOD, D, D), jnp.float32) * scale, 'Wo': jax.random.normal(ks[7], (NUM_NOD, D, D), jnp.float32) * scale, 'ln_g': jnp.ones((D,), jnp.float32), 'ln_b': jnp.zeros((D,), jnp.float32)}
    _L0_ffn_in = _L0_ffn_setup()

    def _L1_attn_setup():
        import jax, jax.numpy as jnp
        import numpy as np
        NUM_HEADS = 16
        EMBED_DIM = 128
        HEAD_DIM = EMBED_DIM // NUM_HEADS
        ROPE_BASE = 10000.0

        def _split_heads(x):
            B, T, _ = x.shape
            return x.reshape(B, T, NUM_HEADS, HEAD_DIM).transpose(0, 2, 1, 3)

        def _rope(q, k):
            T = q.shape[-2]
            half = HEAD_DIM // 2
            dtype = q.dtype
            pos = jnp.arange(T, dtype=dtype)[:, None]
            idx = jnp.arange(half, dtype=dtype)[None, :]
            inv_freq = 1.0 / ROPE_BASE ** (idx / jnp.asarray(half, dtype))
            angles = pos * inv_freq
            sin = jnp.sin(angles)[None, None]
            cos = jnp.cos(angles)[None, None]

            def rot(x):
                x1, x2 = jnp.split(x, 2, axis=-1)
                return jnp.concatenate([x1 * cos - x2 * sin, x1 * sin + x2 * cos], axis=-1)
            return (rot(q), rot(k))
        key = jax.random.key(seed)
        ks = jax.random.split(key, 5)
        B, T, D = (2, 256, EMBED_DIM)
        s = 1.0 / np.sqrt(D)
        return {'x': jax.random.normal(ks[0], (B, T, D), jnp.float32), 'wq_w': jax.random.normal(ks[1], (D, D), jnp.float32) * s, 'wq_b': jnp.zeros((D,), jnp.float32), 'wk_w': jax.random.normal(ks[2], (D, D), jnp.float32) * s, 'wk_b': jnp.zeros((D,), jnp.float32), 'wv_w': jax.random.normal(ks[3], (D, D), jnp.float32) * s, 'wv_b': jnp.zeros((D,), jnp.float32), 'wo_w': jax.random.normal(ks[4], (D, D), jnp.float32) * s, 'wo_b': jnp.zeros((D,), jnp.float32)}
    _L1_attn_in = _L1_attn_setup()

    def _L1_ffn_setup():
        import jax, jax.numpy as jnp
        import numpy as np
        B, S, D, F, E, R = (4, 256, 128, 512, 8, 4)
        key = jax.random.key(seed)
        ks = jax.random.split(key, 8)
        s_in = 1.0 / np.sqrt(D)
        s_ff = 1.0 / np.sqrt(F)
        return {'hidden_states': jax.random.normal(ks[0], (B, S, D), jnp.float32), 'gate_W': jax.random.normal(ks[1], (E, D), jnp.float32) * s_in, 'gate_b': jnp.zeros((E,), jnp.float32), 'wi_W': jax.random.normal(ks[2], (F, D), jnp.float32) * s_in, 'wi_b': jnp.zeros((F,), jnp.float32), 'wo_W': jax.random.normal(ks[3], (D, F), jnp.float32) * s_ff, 'wo_b': jnp.zeros((D,), jnp.float32), 'lora_A': jax.random.normal(ks[4], (E, R, D), jnp.float32) * s_in, 'lora_B': jax.random.normal(ks[5], (E, F, R), jnp.float32) * 0.02}
    _L1_ffn_in = _L1_ffn_setup()
    _d = {'L0_attn_hidden_states': _L0_attn_in['hidden_states'], 'L0_attn_w_qkv': _L0_attn_in['w_qkv'], 'L0_attn_b_qkv': _L0_attn_in['b_qkv'], 'L0_ffn_ew': _L0_ffn_in['ew'], 'L0_ffn_act_w': _L0_ffn_in['act_w'], 'L0_ffn_We': _L0_ffn_in['We'], 'L0_ffn_be': _L0_ffn_in['be'], 'L0_ffn_Wq': _L0_ffn_in['Wq'], 'L0_ffn_Wk': _L0_ffn_in['Wk'], 'L0_ffn_Wv': _L0_ffn_in['Wv'], 'L0_ffn_Wo': _L0_ffn_in['Wo'], 'L0_ffn_ln_g': _L0_ffn_in['ln_g'], 'L0_ffn_ln_b': _L0_ffn_in['ln_b'], 'L1_attn_wq_w': _L1_attn_in['wq_w'], 'L1_attn_wq_b': _L1_attn_in['wq_b'], 'L1_attn_wk_w': _L1_attn_in['wk_w'], 'L1_attn_wk_b': _L1_attn_in['wk_b'], 'L1_attn_wv_w': _L1_attn_in['wv_w'], 'L1_attn_wv_b': _L1_attn_in['wv_b'], 'L1_attn_wo_w': _L1_attn_in['wo_w'], 'L1_attn_wo_b': _L1_attn_in['wo_b'], 'L1_ffn_gate_W': _L1_ffn_in['gate_W'], 'L1_ffn_gate_b': _L1_ffn_in['gate_b'], 'L1_ffn_wi_W': _L1_ffn_in['wi_W'], 'L1_ffn_wi_b': _L1_ffn_in['wi_b'], 'L1_ffn_wo_W': _L1_ffn_in['wo_W'], 'L1_ffn_wo_b': _L1_ffn_in['wo_b'], 'L1_ffn_lora_A': _L1_ffn_in['lora_A'], 'L1_ffn_lora_B': _L1_ffn_in['lora_B']}
    _x0 = _d['L0_attn_hidden_states']
    _d['L0_attn_hidden_states'] = jax.random.normal(jax.random.fold_in(jax.random.key(seed), 1), (1, 2048, 128), dtype=_x0.dtype)
    del _x0
    return _d

def reference(L0_attn_hidden_states, L0_attn_w_qkv, L0_attn_b_qkv, L0_ffn_ew, L0_ffn_act_w, L0_ffn_We, L0_ffn_be, L0_ffn_Wq, L0_ffn_Wk, L0_ffn_Wv, L0_ffn_Wo, L0_ffn_ln_g, L0_ffn_ln_b, L1_attn_wq_w, L1_attn_wq_b, L1_attn_wk_w, L1_attn_wk_b, L1_attn_wv_w, L1_attn_wv_b, L1_attn_wo_w, L1_attn_wo_b, L1_ffn_gate_W, L1_ffn_gate_b, L1_ffn_wi_W, L1_ffn_wi_b, L1_ffn_wo_W, L1_ffn_wo_b, L1_ffn_lora_A, L1_ffn_lora_B):

    def _L0_attn_ref(hidden_states, w_qkv, b_qkv):
        import jax, jax.numpy as jnp
        import numpy as np
        NUM_HEADS = 16
        HIDDEN = 128
        HEAD_DIM = HIDDEN // NUM_HEADS
        GROUP_SIZE = 32

        def _attention(q, k, v, head_dim):
            scores = jnp.einsum('bghqd,bghkd->bghqk', q, k) / head_dim ** 0.5
            w = jax.nn.softmax(scores, axis=-1)
            return jnp.einsum('bghqk,bghkd->bghqd', w, v)
        b, n, _ = hidden_states.shape
        h, d, G = (NUM_HEADS, HEAD_DIM, GROUP_SIZE)
        ng = n // G
        half = G // 2
        qkv = hidden_states @ w_qkv.T + b_qkv
        qkv = qkv.reshape(b, n, 3, h, d).transpose(2, 0, 3, 1, 4)
        q, k, v = (qkv[0], qkv[1], qkv[2])

        def grp(x):
            return x.reshape(b, h, ng, G, d).transpose(0, 2, 1, 3, 4)
        q, k, v = (grp(q), grp(k), grp(v))
        q1, q2 = (q[:, :, :, :half], q[:, :, :, half:])
        k1, k2 = (k[:, :, :, :half], k[:, :, :, half:])
        v1, v2 = (v[:, :, :, :half], v[:, :, :, half:])
        q2 = jnp.roll(q2, -half, axis=2)
        k2 = jnp.roll(k2, -half, axis=2)
        v2 = jnp.roll(v2, -half, axis=2)
        out1 = _attention(q1, k1, v1, d)
        out2 = _attention(q2, k2, v2, d)
        out = jnp.concatenate([out1, out2], axis=3)
        out = jnp.concatenate([out[:, :, :, :half], jnp.roll(out[:, :, :, half:], half, axis=2)], axis=3)
        out = out.transpose(0, 2, 1, 3, 4).reshape(b, n, h * d)
        return out

    def _L0_ffn_ref(inputs, ew, act_w, We, be, Wq, Wk, Wv, Wo, ln_g, ln_b):
        import jax, jax.numpy as jnp
        import numpy as np
        NUM_NOD = 6
        MAX_PREV = 5
        NUM_EDGE = 20
        D = 128
        H = 8
        LN_EPS = 1e-06

        def _layernorm(x, g, b):
            mu = jnp.mean(x, axis=-1, keepdims=True)
            var = jnp.mean(jnp.square(x - mu), axis=-1, keepdims=True)
            return (x - mu) * jax.lax.rsqrt(var + LN_EPS) * g + b

        def _mha(q, k, v, wq, wk, wv, wo):
            B, S, d = q.shape
            dh = d // H
            qh = (q @ wq).reshape(B, S, H, dh)
            kh = (k @ wk).reshape(B, S, H, dh)
            vh = (v @ wv).reshape(B, S, H, dh)
            scores = jnp.einsum('bqhd,bkhd->bhqk', qh, kh) / jnp.sqrt(jnp.asarray(dh, q.dtype))
            attn = jax.nn.softmax(scores, axis=-1)
            ctx = jnp.einsum('bhqk,bkhd->bqhd', attn, vh).reshape(B, S, d)
            return ctx @ wo
        nodes = {-1: inputs}
        lind = 0
        for c in range(NUM_NOD):
            nsrc = min(c + 1, MAX_PREV)
            snode = c - nsrc
            eq, ek, ev = (lind + nsrc - 1, lind, lind + nsrc // 2)
            in_q, in_k, in_v = (c - 1, snode, snode + nsrc // 2)
            q = ew[c, 0] * (nodes[in_q] @ We[eq] + be[eq])
            k = ew[c, 1] * (nodes[in_k] @ We[ek] + be[ek])
            v = ew[c, 2] * (nodes[in_v] @ We[ev] + be[ev])
            o = _mha(q, k, v, Wq[c], Wk[c], Wv[c], Wo[c])
            nodes[c] = act_w[c] * o + q
            lind += nsrc
        out = nodes[NUM_NOD - 1]
        return _layernorm(out, ln_g, ln_b)

    def _L1_attn_ref(x, wq_w, wq_b, wk_w, wk_b, wv_w, wv_b, wo_w, wo_b):
        import jax, jax.numpy as jnp
        import numpy as np
        NUM_HEADS = 16
        EMBED_DIM = 128
        HEAD_DIM = EMBED_DIM // NUM_HEADS
        ROPE_BASE = 10000.0

        def _split_heads(x):
            B, T, _ = x.shape
            return x.reshape(B, T, NUM_HEADS, HEAD_DIM).transpose(0, 2, 1, 3)

        def _rope(q, k):
            T = q.shape[-2]
            half = HEAD_DIM // 2
            dtype = q.dtype
            pos = jnp.arange(T, dtype=dtype)[:, None]
            idx = jnp.arange(half, dtype=dtype)[None, :]
            inv_freq = 1.0 / ROPE_BASE ** (idx / jnp.asarray(half, dtype))
            angles = pos * inv_freq
            sin = jnp.sin(angles)[None, None]
            cos = jnp.cos(angles)[None, None]

            def rot(x):
                x1, x2 = jnp.split(x, 2, axis=-1)
                return jnp.concatenate([x1 * cos - x2 * sin, x1 * sin + x2 * cos], axis=-1)
            return (rot(q), rot(k))
        B, T, D = x.shape
        q = _split_heads(x @ wq_w + wq_b)
        k = _split_heads(x @ wk_w + wk_b)
        v = _split_heads(x @ wv_w + wv_b)
        q, k = _rope(q, k)
        scale = HEAD_DIM ** (-0.5)
        logits = jnp.einsum('bhqd,bhkd->bhqk', q, k) * scale
        attn = jax.nn.softmax(logits, axis=-1)
        y = jnp.einsum('bhqk,bhkd->bhqd', attn, v)
        y = y.transpose(0, 2, 1, 3).reshape(B, T, D)
        return y @ wo_w + wo_b

    def _L1_ffn_ref(hidden_states, gate_W, gate_b, wi_W, wi_b, wo_W, wo_b, lora_A, lora_B):
        import jax, jax.numpy as jnp
        import numpy as np
        B, S, D, F, E, R = (4, 256, 128, 512, 8, 4)
        x = hidden_states
        logits = jnp.einsum('bsd,ed->bse', x, gate_W) + gate_b
        top1 = jnp.argmax(jax.nn.softmax(logits, axis=-1), axis=-1)
        base = jnp.einsum('bsd,fd->bsf', x, wi_W) + wi_b
        out = jnp.zeros_like(x)
        for i in range(lora_A.shape[0]):
            lora = jnp.einsum('bsr,fr->bsf', jnp.einsum('bsd,rd->bsr', x, lora_A[i]), lora_B[i])
            inter = jax.nn.relu(base + lora)
            expert_out = jnp.einsum('bsf,df->bsd', inter, wo_W) + wo_b
            mask = (top1 == i).astype(x.dtype)[..., None]
            out = out + mask * expert_out
        return out
    x = L0_attn_hidden_states
    x = x + _layernorm(_L0_attn_ref(_layernorm(x, axis=-1), L0_attn_w_qkv, L0_attn_b_qkv), axis=-1)
    x = x + _layernorm(_L0_ffn_ref(_layernorm(x, axis=-1), L0_ffn_ew, L0_ffn_act_w, L0_ffn_We, L0_ffn_be, L0_ffn_Wq, L0_ffn_Wk, L0_ffn_Wv, L0_ffn_Wo, L0_ffn_ln_g, L0_ffn_ln_b), axis=-1)
    x = x + _layernorm(_L1_attn_ref(_layernorm(x, axis=-1), L1_attn_wq_w, L1_attn_wq_b, L1_attn_wk_w, L1_attn_wk_b, L1_attn_wv_w, L1_attn_wv_b, L1_attn_wo_w, L1_attn_wo_b), axis=-1)
    x = x + _layernorm(_L1_ffn_ref(_layernorm(x, axis=-1), L1_ffn_gate_W, L1_ffn_gate_b, L1_ffn_wi_W, L1_ffn_wi_b, L1_ffn_wo_W, L1_ffn_wo_b, L1_ffn_lora_A, L1_ffn_lora_B), axis=-1)
    return x

_drawn_inputs = setup_inputs


def setup_inputs(seed=0):
    import zlib

    import numpy as np

    out = dict(_drawn_inputs(seed))
    spreads = {'L0_ffn_be': (0.0, 0.1),
     'L0_ffn_ln_g': (1.0, 0.2),
     'L0_ffn_ln_b': (0.0, 0.1),
     'L1_attn_wq_b': (0.0, 0.8),
     'L1_attn_wk_b': (0.0, 0.8),
     'L1_attn_wv_b': (0.0, 0.1),
     'L1_attn_wo_b': (0.0, 0.1),
     'L1_ffn_gate_b': (0.0, 2.0),
     'L1_ffn_wi_b': (0.0, 0.1),
     'L1_ffn_wo_b': (0.0, 0.1)}
    factors = {'L0_ffn_Wq': 64.0, 'L0_ffn_Wk': 64.0, 'L1_ffn_gate_W': 2.888, 'L1_ffn_lora_B': 2.787}
    for name, (base, spread) in spreads.items():
        noise = np.random.default_rng([zlib.crc32(name.encode()), seed]).standard_normal(out[name].shape)
        drawn = base * np.exp(spread * noise) if base else spread * noise
        out[name] = jnp.asarray(drawn.astype(out[name].dtype))
    for name, factor in factors.items():
        out[name] = (out[name] * factor).astype(out[name].dtype)
    return out
```

```python
from contextlib import ExitStack

import numpy as np

import concourse.bass as bass
from concourse import mybir

F32 = mybir.dt.float32
BF16 = mybir.dt.bfloat16
U32 = mybir.dt.uint32
ALU = mybir.AluOpType
ACT = mybir.ActivationFunctionType
AX = mybir.AxisListType

P = 128
N = 2048
D = 128
TILES = N // P
BLK = 512
NBLK = N // BLK
QT = BLK // P
M_ROW = 96
K_ROWS = M_ROW + 3
VW = 32
NODES = 6
MAX_PREV = 5
L0_HEADS, L0_DIM, L0_SPAN = 16, 8, 16
NAS_HEADS, NAS_DIM = 8, 16
ROT_HEADS, ROT_DIM = 16, 8
EXPERTS, RANK, FF = 8, 4, 512
FC = FF // P

TERMS = {
    16: ((0, 0, 1, 0, 1, 2), (0, 1, 0, 2, 1, 0)),
    8: ((0, 0, 0, 1, 1, 1, 2, 2, 2), (0, 1, 2, 0, 1, 2, 0, 1, 2)),
}


def node_plan():
    plan, first = [], 0
    for c in range(NODES):
        n = min(c + 1, MAX_PREV)
        src = c - n
        plan.append(dict(eq=first + n - 1, ek=first, ev=first + n // 2, q=c - 1, k=src, v=src + n // 2))
        first += n
    return plan


NODE = node_plan()


def slot_of(node):
    return 0 if node == NODES - 1 else node + 1


def node_col(node, blk=0):
    return slot_of(node) * N + blk * BLK


class Body:

    def __init__(self, kind, node, b0, b1, before, *, with_out, next_q, next_k, next_v, last):
        self.kind, self.node, self.b0, self.b1 = kind, node, b0, b1
        self.heads = NAS_HEADS if kind == "nas" else ROT_HEADS
        self.before = dict(before)
        self.with_out, self.next_q, self.next_k, self.next_v, self.last = with_out, next_q, next_k, next_v, last
        self.jobs = {}
        for h in range(self.heads):
            if h or with_out:
                self.jobs[h, 3] = "fold"
            if not (last and h == self.heads - 1):
                self.jobs[h, 7] = "rows"
        at = {"turn": 0 if with_out else None, "out": 1 if with_out else None,
              "q1": 2 if next_q else None, "q2": 3 if next_q else None,
              "k1": 4 if next_k else None, "k2": 5 if next_k else None,
              "v1": 6 if next_v else None, "v2": 7 if next_v else None}
        self.jobs.update({(h, 5): name for name, h in at.items() if h is not None})
        self.order = {hs: n for n, hs in enumerate(sorted(self.jobs))}
        self.n_jobs = len(self.jobs)
        self.n_splits = int(next_q) + int(next_k)

    def unit(self, b):
        return self.before["unit"] + self.heads * (b - self.b0)

    def job(self, b, h, s):
        return self.before["job"] + self.n_jobs * (b - self.b0) + self.order[h, s]

    def split(self, b):
        return self.before["split"] + self.n_splits * (b - self.b0)

    def body(self, b):
        return self.before["body"] + (b - self.b0)

    def jobs_so_far(self, b, h, s):
        return self.before["job"] + self.n_jobs * (b - self.b0) + sum(k < (h, s) for k in self.jobs)

    def out_of(self, b):
        return (self.node, b - 1) if self.b0 or self.kind == "rot" else (self.node - 1, NBLK - 1)

    def turns_over(self):
        return self.kind == "nas" and self.b1 == NBLK and not self.last

    def pick(self, b, here, there):
        if not self.turns_over():
            return here
        if self.b1 - self.b0 == 1:
            return there
        return here + (b // (NBLK - 1)) * (there - here)


class Serial:

    def __init__(self, kind, node, before, jobs):
        self.kind, self.node, self.before, self.jobs = kind, node, dict(before), jobs


def make_plan():
    plan = []
    count = dict(unit=0, job=0, split=0, body=0)

    def body(kind, node, b0, b1, **kw):
        x = Body(kind, node, b0, b1, count, **kw)
        plan.append(x)
        n = b1 - b0
        count["unit"] += x.heads * n
        count["job"] += x.n_jobs * n
        count["split"] += x.n_splits * n
        count["body"] += n

    def serial(kind, node, jobs):
        plan.append(Serial(kind, node, count, jobs))
        count["job"] += len(jobs)
        count["split"] += sum(name in ("q2", "k2") for name, _ in jobs)

    keys = [(j, b) for b in range(NBLK) for j in ("k1", "k2")]
    queries = [("q1", 0), ("q2", 0)]
    values = [(j, b) for b in range(NBLK) for j in ("v1", "v2")]
    finish = [("fold", NBLK - 1), ("turn", NBLK - 1), ("out", NBLK - 1)]
    serial("nas", 0, queries + keys + values + [("prime", 0)])
    for c in range(NODES):
        end = c == NODES - 1
        kw = dict(next_q=True, next_k=not end, next_v=not end and c > 0, last=False)
        body("nas", c, 0, 1, with_out=c > 1, **kw)
        body("nas", c, 1, NBLK - end, with_out=True, **kw)
        if end:
            body("nas", c, NBLK - 1, NBLK, with_out=True, next_q=False, next_k=False, next_v=False, last=True)
        if c == 0:
            serial("nas", 0, finish)
            serial("nas", 1, values)
    serial("nas", NODES - 1, finish)
    count["body"] = 0
    serial("rot", 0, queries + keys + [("v2", b) for b in range(NBLK)] + [("prime", 0)])
    kw = dict(next_k=False, next_v=False)
    body("rot", 0, 0, 1, with_out=False, next_q=True, last=False, **kw)
    body("rot", 0, 1, NBLK - 1, with_out=True, next_q=True, last=False, **kw)
    body("rot", 0, NBLK - 1, NBLK, with_out=True, next_q=False, last=True, **kw)
    serial("rot", 0, finish)
    return plan


PLAN = make_plan()


def need(eng, semaphore, value):
    if not (isinstance(value, int) and value <= 0):
        eng.wait_ge(semaphore, value)


def each_block(eng, body, emit):
    if body.b1 - body.b0 == 1:
        emit(body.b0)
    else:
        with eng.Fori(body.b0, body.b1) as b:
            emit(b)


def build(nc, A, out):
    with ExitStack() as ctx:
        build_program(nc, ctx, A, out)


def build_program(nc, ctx, A, out):
    def sb(name, shape, dt):
        return ctx.enter_context(nc.sbuf_tensor(name, shape, dt))

    def sem(name):
        return ctx.enter_context(nc.semaphore(name))

    big = sb("big", [P, 6 * N + 4096 + 4096], F32)
    nodes = big[:, 0:6 * N]
    xT = big[:, 0:N]
    tok = big[:, N:2 * N].rearrange("p (t d) -> p t d", d=D)
    att = big[:, 0:N].rearrange("p (t d) -> p t d", d=D)
    qst = big[:, 6 * N:6 * N + 4096].bitcast(BF16)
    probs = big[:, 6 * N + 4096:6 * N + 8192].rearrange("p (i n) -> p i n", i=4)
    q_loc = big[:, N:N + 16 * N // 2].bitcast(BF16)
    kst = sb("kst", [P, 16 * N], BF16)
    vst = sb("vst", [P, 256 * VW], F32)
    v_cols = vst[:, :].rearrange("p (x w) -> p x w", w=VW)
    v_nas = vst[:, :].rearrange("p (a t h w) -> p a t h w", a=2, t=TILES, h=NAS_HEADS)
    v_16 = vst[:, :].rearrange("p (t h w) -> p t h w", t=TILES, h=16)
    x_res = sb("x_res", [P, TILES, D], F32)
    ob = sb("ob", [P, N], F32)
    normed_x = ob[:, :].rearrange("p (t d) -> p t d", d=D)
    o_part = ob[:, 0:1024].rearrange("p (i n) -> p i n", i=2)
    o_tok = ob[:, 1024:1536].rearrange("p (t d) -> p t d", d=D)
    o_chan = ob[:, 1536:2048]
    parts2 = ob[:, 0:1536].bitcast(BF16).rearrange("p (i t n) -> p i t n", i=2, t=3)
    parts = sb("parts", [P, 3, BLK], BF16)
    rest = sb("rest", [P, BLK], F32)
    t_tmp = sb("t_tmp", [P, BLK], F32)
    l_probs = (rest, t_tmp)
    w_q, w_k, w_v, w_o = (sb(f"w_{x}", [P, 2, D], F32) for x in "qkvo")
    ident = sb("ident", [P, P], F32)
    ident_b = sb("ident_b", [P, P], BF16)
    pick_b = sb("pick_b", [P, P], BF16)
    col = sb("col", [P, 64], F32)
    BE, EW, AW, QBE, QEW, RB, LB, FB = 0, 20, 38, 44, 45, 46, 50, 52
    stats = sb("stats", [P, TILES, 6], F32)
    mean_var = sb("mean_var", [P, TILES, 2], F32)
    rstd = sb("rstd", [P, 3, TILES], F32)
    row_max = sb("row_max", [P, 2, 16], F32)
    neg_max = sb("neg_max", [P, 2, 4], F32)
    neg_rest = sb("neg_rest", [P, 2, 4], F32)
    zeros = sb("zeros", [P, 4], F32)
    max_parts = sb("max_parts", [P, 2, 4, 3], BF16)
    sums = sb("sums", [P, QT, NAS_DIM + 1], F32)
    recip = sb("recip", [P, 16], F32)
    v_now = [w[:, 0, :].rearrange("p (h w) -> p h w", w=VW) for w in (w_q, w_k)]
    mask_rows = [parts[:, 0, :], parts[:, 1, :]]
    mask_only = parts[:, 2, :]
    cos, sin = big[:, 2 * N:3 * N], big[:, 3 * N:4 * N]
    rot_a, rot_b, rot_sum = (big[:, 4 * N + i * BLK:4 * N + (i + 1) * BLK] for i in range(3))
    rows = big[:, 4 * N + 3 * BLK:4 * N + 3 * BLK + 384].rearrange("p (i d) -> p i d", d=D)
    M0 = 5 * N
    wi = big[:, M0:M0 + FF]
    wo = big[:, M0 + FF:M0 + 2 * FF].rearrange("p (c d) -> p c d", d=D)
    lora_b = big[0:EXPERTS * RANK, M0 + 2 * FF:M0 + 3 * FF]
    GA = EXPERTS + EXPERTS * RANK
    gate_a = big[:, M0 + 3 * FF:M0 + 3 * FF + GA]
    gate_bias = big[:, M0 + 3 * FF + 64:M0 + 3 * FF + 64 + EXPERTS]
    rank_row = big[:, M0 + 3 * FF + 80:M0 + 3 * FF + 80 + EXPERTS]
    wo_bias = big[:, M0 + 3 * FF + 128:M0 + 3 * FF + 256]
    hid = vst[:, 0:2 * FC * BLK].rearrange("p (i c n) -> p i c n", i=2, c=FC)
    low_T = big[0:EXPERTS * RANK, 3 * N:4 * N]
    G0 = 4 * N
    logits = big[:, G0:G0 + 128].rearrange("p (t e) -> p t e", e=EXPERTS)
    chosen = big[:, G0 + 128:G0 + 256].rearrange("p (t e) -> p t e", e=EXPERTS)
    top = big[:, G0 + 256:G0 + 272]
    low = big[:, G0 + 512:G0 + 1024].rearrange("p (t r) -> p t r", r=EXPERTS * RANK)

    ps = ctx.enter_context(nc.psum_tensor("ps", [P, 8, BLK], F32))
    MAXES, ACC, MISC = 4, 6, 7
    misc = ps[:, MISC, :]
    acc = ps[:, ACC, :]

    scratch = {x: nc.dram_tensor(f"parts_{x}", [3, P, N], BF16, kind="Internal").ap() for x in "qk"}

    def stacked(x, term, dim, heads, c0, c1):
        return scratch[x][term, :, c0:c1].rearrange("(h r) n -> r h n", r=dim)[:, heads, :]

    S = {name: sem(name) for name in """
        x_in const_in small_in w0_in w0_row_in masks_in nas_cols_in norm_rows_in rot_in rot_rows_in mlp_in
        consts_made rows_ready zeros_ready masks_made
        var_ready std_ready normed turned turn_copied
        dve_step
        l_full l_free l_parts_ready l_parts_sent_even l_parts_sent_odd l_q_in l_k_in l_values
        l_scores l_neg l_pool l_maxparts l_rows l_rows_in l_st l_exp l_vnow l_pv l_acc l_turned l_normed
        tile_ready tile_done neg_ready pool_step maxparts_ready st_ready exp_done pv_done acc_copied
        misc_full misc_free high_ready mid_ready rest_ready parts_ready parts_sent
        heads_summed heads_recip heads_normed rot_a_done rot_b_done rot_sum_done
        q_weights_in node_weights_in nas_k_in nas_qa_in nas_qb_in rot_k_in rot_qa_in rot_qb_in
        cell_turned cell_copied gates_ready gates_copied low_ready low_turned low_copied hid_full hid_free
        mlp_full mlp_free pads_ready out_ready rot_swapped rot_high_ready out_in""".split()}

    l_parts_sent = (S["l_parts_sent_even"], S["l_parts_sent_odd"])
    block = ctx.enter_context(nc.Block())
    n_terms = {kind: len(TERMS[dim][0]) for kind, dim in (("nas", NAS_DIM), ("rot", ROT_DIM))}
    dims = {"nas": NAS_DIM, "rot": ROT_DIM}
    heads_of = {"nas": NAS_HEADS, "rot": ROT_HEADS}
    rot_split0 = next(x for x in PLAN if x.kind == "rot").before["split"]

    def node_weights_count(node):
        return 64 + 80 * (node + 1) - 64 * (node == NODES - 1)

    def in_nodes(at):
        if isinstance(at, int):
            return at
        return nc.s_assert_within(at, 0, 6 * N - BLK, skip_runtime_bounds_check_because="blocks 0..3 of slots 0..5")

    def next_block(x, b):
        return in_nodes(x.pick(b, node_col(x.node), node_col(min(x.node + 1, NODES - 1)) - N) + (b + 1) * BLK)


    @block.sync
    def _(sp):
        def load(dst, src, semaphore, **kw):
            sp.dma_start(dst, src, **kw).then_inc(S[semaphore], 16)

        load(x_res[:, :, :], A["x"][0].rearrange("(t p) d -> p t d", p=P), "x_in")
        load(ident[:, :], A["c_ident"], "const_in")
        for w, i in ((w_q, 0), (w_k, 1), (w_v, 2)):
            load(w[:, 0, :], A["w_qkvT"][:, i * D:(i + 1) * D], "w0_in")
        for i in range(2):
            load(col[:, LB + i:LB + i + 1], A["b_qkv"][i * D:(i + 1) * D].rearrange("(p a) -> p a", a=1), "w0_in")
        load(w_o[:, 0, :], A["b_qkv"][2 * D:3 * D].rearrange("(a d) -> a d", a=1).partition_broadcast(P), "w0_in")
        load(t_tmp[:, 0:P], A["c_pick"], "small_in")
        sp.wait_ge(S["consts_made"], 2)
        load(t_tmp[:, :], A["c_mask"], "masks_in")

        terms_q, terms_k = TERMS[L0_DIM]
        for n in range(2 * NBLK):
            x, b = ("k", n) if n < NBLK else ("q", n - NBLK)
            sp.wait_ge(S["l_parts_ready"], n + 1)
            sp.dma_start(scratch[x][:, :, b * BLK:(b + 1) * BLK].rearrange("t p n -> p t n"),
                         parts2[:, n % 2, :, :]).then_inc(l_parts_sent[n % 2], 16)
            if n == NBLK - 1 or n == 2 * NBLK - 1:
                for sent in l_parts_sent:
                    sp.wait_ge(sent, 16 * (n + 1) // 2)
                if n == NBLK - 1:
                    for j, term in enumerate(terms_k):
                        load(kst[8 * j:8 * j + 8, :].rearrange("p (h n) -> p h n", n=N),
                             stacked("k", term, L0_DIM, slice(0, 16), 0, N), "l_k_in")
                else:
                    for j, term in enumerate(terms_q):
                        load(q_loc[8 * j:8 * j + 8, :].rearrange("p (h n) -> p h n", n=N),
                             stacked("q", term, L0_DIM, slice(0, 16), 0, N), "l_q_in")

        sp.wait_ge(S["l_normed"], 16)
        load(col[:, BE:BE + 20], A["be"].rearrange("e d -> d e"), "nas_cols_in", allow_slow_non_contiguous=True)
        load(col[:, EW:EW + 18], A["ew"].rearrange("c g -> (c g)").rearrange("(a n) -> a n", a=1)
             .partition_broadcast(P), "nas_cols_in")
        load(col[:, AW:AW + NODES], A["act_w"].rearrange("(a n) -> a n", a=1).partition_broadcast(P), "nas_cols_in")

        def node_q_weights(b, x, node_here, node_there):
            e, c = NODE[node_here]["eq"], node_here
            if x:
                e, c = x.pick(b, e, NODE[node_there]["eq"]), x.pick(b, c, node_there)
            load(w_q[:, 0, :], A["We"][bass.ds(e, 1)].rearrange("a k n -> (a k) n"), "q_weights_in")
            load(w_q[:, 1, :], A["Wq"][bass.ds(c, 1)].rearrange("a k n -> (a k) n"), "q_weights_in")
            load(col[:, QBE:QBE + 1], A["be"][bass.ds(e, 1), :].rearrange("a d -> d a"), "q_weights_in",
                 allow_slow_non_contiguous=True)
            load(col[:, QEW:QEW + 1], A["ew"][bass.ds(c, 1), 0:1].partition_broadcast(P)
                 .rearrange("p a b -> p (a b)"), "q_weights_in")

        def kv_weights(c):
            load(w_k[:, 0, :], A["We"][NODE[c]["ek"]], "node_weights_in")
            load(w_k[:, 1, :], A["Wk"][c], "node_weights_in")
            load(w_v[:, 0, :], A["We"][NODE[c]["ev"]], "node_weights_in")
            load(w_v[:, 1, :], A["Wv"][c], "node_weights_in")

        node_q_weights(0, None, 0, 0)
        kv_weights(0)

        def send_parts(x, split, ready=None):
            sp.wait_ge(S["parts_ready"], split + 1 if ready is None else ready)
            sp.dma_start(scratch[x][:, :, 0:BLK].rearrange("t p n -> p t n"),
                         parts[:, :, :]).then_inc(S["parts_sent"], 16)
            sp.wait_ge(S["parts_sent"], 16 * (split + 1))

        def stage_queries(kind, half, semaphore):
            d, h2 = dims[kind], heads_of[kind] // 2
            for j, term in enumerate(TERMS[d][0]):
                load(qst[d * j:d * j + d, half * h2 * BLK:(half + 1) * h2 * BLK].rearrange("p (h n) -> p h n", n=BLK),
                     stacked("q", term, d, slice(half * h2, (half + 1) * h2), 0, BLK), semaphore)

        def stage_keys(kind, node, b):
            d, heads = dims[kind], heads_of[kind]
            slots = kst[:, :] if kind == "rot" else kst[:, (node % 2) * 8 * N:(node % 2) * 8 * N + 8 * N]
            for j, term in enumerate(TERMS[d][1]):
                load(slots[d * j:d * j + d, :].rearrange("p (h n) -> p h n", n=N)[:, :, bass.ds(b * BLK, BLK)],
                     stacked("k", term, d, slice(0, heads), 0, BLK), f"{kind}_k_in")

        splits_k = {"nas": 0, "rot": 0}
        for x in PLAN:
            kind = x.kind
            if isinstance(x, Serial):
                if kind == "rot" and x.jobs[0][0] == "q1":
                    sp.wait_ge(S["cell_turned"], 4)
                    load(w_q[:, 0, :], A["wq_w"], "rot_in")
                    load(w_k[:, 0, :], A["wk_w"], "rot_in")
                    load(w_v[:, 0, :], A["wv_w"], "rot_in")
                    load(w_o[:, 0, :], A["wo_w"], "rot_in")
                    for i, name in enumerate(("wq_b", "wk_b")):
                        load(col[:, RB + 2 * i:RB + 2 * i + 1], A[name].rearrange("(p a) -> p a", a=1), "rot_in")
                        load(col[:, RB + 2 * i + 1:RB + 2 * i + 2], A[name + "_swapped"].rearrange("(p a) -> p a", a=1),
                             "rot_in")
                    load(cos, A["c_cos"], "rot_in")
                    load(sin, A["c_sin"], "rot_in")
                    load(rows[:, 0, :], A["wv_b"].rearrange("(a d) -> a d", a=1).partition_broadcast(P), "rot_rows_in")
                    load(rows[:, 1, :], A["wo_b"].rearrange("(a d) -> a d", a=1).partition_broadcast(P), "rot_rows_in")
                    load(wi, A["wi_T"], "mlp_in")
                    load(wo, A["wo_T"].rearrange("(c p) d -> p c d", p=P), "mlp_in")
                    load(lora_b, A["lora_BT"], "mlp_in")
                    load(gate_a[:, 0:EXPERTS], A["gate_T"], "mlp_in")
                    load(gate_a[:, EXPERTS:GA], A["lora_AT"], "mlp_in")
                    load(gate_bias, A["gate_b"].rearrange("(a d) -> a d", a=1).partition_broadcast(P), "mlp_in")
                    load(rank_row, A["c_rank"].partition_broadcast(P), "mlp_in")
                    load(wo_bias, A["ffn_wo_b"].rearrange("(a d) -> a d", a=1).partition_broadcast(P), "mlp_in")
                    load(col[:, FB:FB + FC], A["wi_b"].rearrange("(c p) -> p c", p=P), "mlp_in",
                         allow_slow_non_contiguous=True)
                    sp.wait_ge(S["pads_ready"], 1)
                split = x.before["split"]
                for name, b in x.jobs:
                    if name == "q2":
                        send_parts("q", split)
                        stage_queries(kind, 0, f"{kind}_qa_in")
                        split += 1
                    if name == "k2":
                        if splits_k[kind] == 0:
                            sp.wait_ge(S[f"{kind}_qa_in"], 16 * n_terms[kind])
                        else:
                            sp.wait_ge(S[f"{kind}_k_in"], 16 * n_terms[kind] * splits_k[kind])
                        send_parts("k", split)
                        stage_keys(kind, 0, b)
                        split += 1
                        splits_k[kind] += 1
                continue

            def emit(b, x=x, kind=kind):
                c, g = x.node, x.body(b)
                nt = 16 * n_terms[kind]
                ready = [None if isinstance(b, int) else sp.to_reg(x.split(b) + i) for i in (1, 2)]
                need(sp, S["misc_full"], x.before["job"] + x.n_jobs * (b - x.b0))
                need(sp, S["st_ready"], 8 * x.unit(b))
                stage_queries(kind, 1, f"{kind}_qb_in")
                if kind == "nas":
                    if x.next_q:
                        node_q_weights(b, x, c, min(c + 1, NODES - 1))
                    if x.b0 == 0:
                        if x.next_k:
                            kv_weights(c + 1)
                        load(w_o[:, c % 2, :], A["Wo"][c], "node_weights_in")
                if x.next_q:
                    sp.wait_ge(S[f"{kind}_qb_in"], nt * (g + 1))
                    send_parts("q", x.split(b), ready[0])
                    sp.wait_ge(S["st_ready"], 8 * (x.unit(b) + x.heads // 2))
                    stage_queries(kind, 0, f"{kind}_qa_in")
                if x.next_k:
                    k_before = NBLK * (c + 1) + b
                    sp.wait_ge(S["nas_k_in"], nt * k_before)
                    send_parts("k", x.split(b) + 1, ready[1])
                    stage_keys(kind, c + 1, b)

            each_block(sp, x, emit)
            if kind == "nas" and x.last:
                load(t_tmp[:, 0:D], A["ln_g"].rearrange("(a d) -> a d", a=1).partition_broadcast(P), "norm_rows_in")
                load(t_tmp[:, D:2 * D], A["ln_b"].rearrange("(a d) -> a d", a=1).partition_broadcast(P), "norm_rows_in")

        for b in range(NBLK):
            sp.wait_ge(S["out_ready"], b + 1)
            load(out[0].rearrange("(t p) d -> p t d", p=P)[:, QT * b:QT * (b + 1), :],
                 x_res[:, QT * b:QT * (b + 1), :], "out_in")
        sp.wait_ge(S["out_in"], 16 * NBLK)

    @block.gpsimd
    def _(pool):
        pool.memset(zeros[:, :], 0.0).then_inc(S["zeros_ready"], 1)
        pool.wait_ge(S["zeros_ready"], 1)
        pool.memset(kst[M_ROW:P, :].bitcast(F32), float(np.array([0x3F803F80], np.uint32).view(np.float32)[0])) \
            .then_inc(S["rows_ready"], 1)
        pool.wait_ge(S["rows_ready"], 1)

        def split_max(neg, out3, step_sem, done_sem, n, i):
            pool.tensor_tensor(out3[:, i, :, 0], neg[:, i, :], zeros[:, :], ALU.add).then_inc(S[step_sem], 1)
            pool.wait_ge(S[step_sem], 3 * n + 1)
            pool.tensor_tensor(neg_rest[:, i, :], neg[:, i, :], out3[:, i, :, 0], ALU.subtract).then_inc(S[step_sem], 1)
            pool.wait_ge(S[step_sem], 3 * n + 2)
            pool.tensor_tensor(out3[:, i, :, 1], neg_rest[:, i, :], zeros[:, :], ALU.add) \
                .then_inc(S[step_sem], 1)
            pool.wait_ge(S[step_sem], 3 * n + 3)
            pool.tensor_tensor(out3[:, i, :, 2], neg_rest[:, i, :], out3[:, i, :, 1], ALU.subtract) \
                .then_inc(S[done_sem], 1)

        def local_step(n, i):
            pool.wait_ge(S["l_neg"], n + 1)
            need(pool, S["l_rows"], n - 1)
            split_max(neg_max, max_parts, "l_pool", "l_maxparts", n, i)

        for grp in range(L0_HEADS // 4):
            with pool.Fori(0, TILES // 2) as pair:
                t = 2 * pair
                for i in range(2):
                    if grp == 0:
                        pool.wait_ge(S["l_neg"], t + (i + 1))
                        split_max(neg_max, max_parts, "l_pool", "l_maxparts", t + i, i)
                    else:
                        local_step(grp * TILES + i + t, i)

        def attention_step(u, i):
            pool.wait_ge(S["neg_ready"], u + 1)
            split_max(neg_max, max_parts, "pool_step", "maxparts_ready", u, i)

        for x in PLAN:
            if isinstance(x, Serial):
                if x.jobs[-1][0] == "prime":
                    attention_step(x.before["unit"], 0)
                continue

            def emit(b, x=x):
                for h in range(x.heads):
                    if not (x.last and h == x.heads - 1):
                        attention_step(x.unit(b) + h + 1, (h + 1) % 2)

            each_block(pool, x, emit)

    @block.scalar
    def _(act):
        norms = [0]

        def root():
            act.wait_ge(S["var_ready"], norms[0] + 1)
            act.activation(rstd[:, 1, :], rstd[:, 0, :], ACT.Sqrt).then_inc(S["std_ready"], 1)
            norms[0] += 1

        def copy_turned(layer):
            for b in range(NBLK):
                act.wait_ge(S["turned"], NBLK * layer + b + 1)
                act.activation(xT[:, b * BLK:(b + 1) * BLK], ps[:, b, :], ACT.Copy).then_inc(S["turn_copied"], 1)

        root()
        copy_turned(0)

        act.wait_ge(S["masks_made"], 3)

        def local_step(n, i):
            act.wait_ge(S["l_rows"], n + 1)
            need(act, S["l_st"], n - 1)
            act.activation(mask_rows[i][M_ROW:K_ROWS, :], ps[M_ROW:K_ROWS, 2 + i, :], ACT.Copy) \
                .then_inc(S["l_rows_in"], 1)
            act.wait_ge(S["l_st"], n + 1)
            need(act, S["l_pv"], n - 1)
            act.activation(l_probs[i][:, :], ps[:, i, :], ACT.Exp, scale=float(L0_DIM) ** -0.5) \
                .then_inc(S["l_exp"], 1)

        for grp in range(L0_HEADS // 4):
            n0 = grp * TILES
            local_step(n0, 0)
            local_step(n0 + 1, 1)
            with act.Fori(1, TILES // 2) as pair:
                t = 2 * pair
                local_step(n0 + t, 0)
                local_step(n0 + 1 + t, 1)

        root()
        root()
        copy_turned(1)

        def rows_copy(job, slot):
            act.wait_ge(S["misc_full"], job + 1)
            act.activation(qst[M_ROW:K_ROWS, slot * BLK:(slot + 1) * BLK], misc[M_ROW:K_ROWS, :], ACT.Copy) \
                .then_inc(S["misc_free"], 1)

        def turn_copy(job):
            act.wait_ge(S["misc_full"], job + 1)
            act.activation(o_chan, misc, ACT.Copy).then_inc(S["misc_free"], 1)

        def high_part(job, split):
            act.wait_ge(S["misc_full"], job + 1)
            need(act, S["parts_sent"], 16 * split)
            act.activation(parts[:, 0, :], misc, ACT.Copy).then_inc(S["high_ready"], 1)

        def acc_copy(u, i):
            act.wait_ge(S["pv_done"], 4 * u + 4)
            act.activation(o_part[:, i, :], acc, ACT.Copy).then_inc(S["acc_copied"], 1)

        for x in PLAN:
            kind = x.kind
            if isinstance(x, Serial):
                job, split = x.before["job"], x.before["split"]
                for name, b in x.jobs:
                    if name == "prime":
                        rows_copy(job, 0)
                    if name == "turn":
                        turn_copy(job)
                    if name in ("q2", "k2"):
                        if kind == "nas":
                            high_part(job, split)
                        split += 1
                    job += 1
                if kind == "nas" and x.jobs[0][0] == "fold" and x.node == NODES - 1:
                    for b in range(NBLK):
                        act.wait_ge(S["cell_turned"], b + 1)
                        act.activation(tok[:, QT * b:QT * (b + 1), :].rearrange("p t d -> p (t d)"), ps[:, b, :],
                                       ACT.Copy).then_inc(S["cell_copied"], 1)
                    for _ in range(3):
                        root()
                    copy_turned(2)
                continue

            def emit(b, x=x, kind=kind):
                for h in range(x.heads):
                    u = x.unit(b) + h
                    for s in range(8):
                        act.wait_ge(S["st_ready"], 8 * u + s + 1)
                        if s % 2 == 0:
                            need(act, S["pv_done"], 4 * u + s // 2 - 1)
                        act.activation(probs[:, s % 4, :],
                                       ps[:, 2 * (s % 2):2 * (s % 2) + 2, :].rearrange("p a n -> p (a n)"),
                                       ACT.Exp, scale=float(dims[kind]) ** -0.5).then_inc(S["exp_done"], 1)
                        if s == 1 and h > 0:
                            acc_copy(u - 1, (h - 1) % 2)
                        name = x.jobs.get((h, s))
                        if name == "rows":
                            rows_copy(x.job(b, h, s), (h + 1) % x.heads)
                        if name == "turn":
                            turn_copy(x.job(b, h, s))
                        if name == "q2" and kind == "nas":
                            high_part(x.job(b, h, s), x.split(b))
                        if name == "k2":
                            high_part(x.job(b, h, s), x.split(b) + 1)
                acc_copy(x.unit(b) + x.heads - 1, (x.heads - 1) % 2)

            each_block(act, x, emit)

        root()
        root()
        copy_turned(3)

        for b in range(NBLK):
            act.wait_ge(S["low_turned"], b + 1)
            act.activation(low_T[:, b * BLK:(b + 1) * BLK], ps[0:EXPERTS * RANK, 2 + b, :], ACT.Copy) \
                .then_inc(S["low_copied"], 1)
        act.wait_ge(S["mlp_in"], 16 * 9)
        for b in range(NBLK):
            for c in range(FC):
                i = FC * b + c
                act.wait_ge(S["hid_full"], i + 1)
                need(act, S["mlp_full"], b - 1)
                act.activation(hid[:, b % 2, c, :], ps[:, i % 2, :], ACT.Relu, bias=col[:, FB + c:FB + c + 1]) \
                    .then_inc(S["hid_free"], 1)
        root()

    @block.tensor
    def _(pe):
        def turn_normed(layer):
            for b in range(NBLK):
                pe.wait_ge(S["normed"], NBLK * layer + b + 1)
                for t in range(QT):
                    last = pe.transpose(ps[:, b, t * P:(t + 1) * P], normed_x[:, QT * b + t, :], ident[:, :])
                last.then_inc(S["turned"], 1)

        pe.wait_ge(S["const_in"], 16)
        turn_normed(0)

        pe.wait_ge(S["w0_in"], 16 * 6)
        for n in range(3 * NBLK):
            bank = ps[:, n % 4, :]
            pe.wait_ge(S["turn_copied"], NBLK if n < 4 else NBLK)
            need(pe, S["l_free"], n - 3)
            if n < 2 * NBLK:
                w, b = (w_k, n) if n < NBLK else (w_q, n - NBLK)
                pe.matmul(bank, w[:, 0, :], xT[:, b * BLK:(b + 1) * BLK], start=True, stop=True) \
                    .then_inc(S["l_full"], 1)
            else:
                for t in range(QT):
                    j = QT * (n - 2 * NBLK) + t
                    last = pe.matmul(bank[:, t * P:(t + 1) * P], xT[:, j * P:(j + 1) * P], w_v[:, 0, :],
                                     start=True, stop=True)
                last.then_inc(S["l_full"], 1)

        pe.wait_ge(S["consts_made"], 2)
        pe.wait_ge(S["masks_made"], 3)
        pe.wait_ge(S["l_free"], 3 * NBLK)
        pe.wait_ge(S["l_k_in"], 16 * len(TERMS[L0_DIM][0]))
        pe.wait_ge(S["l_q_in"], 16 * len(TERMS[L0_DIM][0]))
        L_ROWS = L0_DIM * len(TERMS[L0_DIM][0])

        def local_maxes(n, t, grp, i):
            need(pe, S["l_neg"], n - 1)
            pe.matmul(ps[:, MAXES + i, :], pick_b[:, :], mask_only, start=True, stop=False, skip_group_check=True)
            for h in range(4):
                at = bass.ds((4 * grp + h) * N + t * P, P)
                last = pe.matmul(ps[:, MAXES + i, h * P:(h + 1) * P], q_loc[0:L_ROWS, at], kst[0:L_ROWS, at],
                                 start=False, stop=(h == 3), skip_group_check=True)
            last.then_inc(S["l_scores"], 1)

        def local_scores(n, t, grp, i):
            pe.wait_ge(S["l_maxparts"], n + 1)
            need(pe, S["l_rows_in"], n - 1)
            for h in range(4):
                last = pe.matmul(ps[M_ROW:K_ROWS, 2 + i, h * P:(h + 1) * P], max_parts[:, i, h, :], ident_b[:, :],
                                 start=True, stop=True)
            last.then_inc(S["l_rows"], 1)
            pe.wait_ge(S["l_rows_in"], n + 1)
            need(pe, S["l_exp"], n - 1)
            pe.matmul(ps[:, i, :], pick_b[:, :], mask_rows[i], start=True, stop=False, skip_group_check=True)
            for h in range(4):
                at = bass.ds((4 * grp + h) * N + t * P, P)
                last = pe.matmul(ps[:, i, h * P:(h + 1) * P], kst[0:L_ROWS, at], q_loc[0:L_ROWS, at],
                                 start=False, stop=(h == 3), skip_group_check=True)
            last.then_inc(S["l_st"], 1)

        def local_values(n, i):
            pe.wait_ge(S["l_exp"], n + 1)
            pe.wait_ge(S["l_vnow"], n + 1)
            need(pe, S["l_acc"], n - 1)
            for h in range(4):
                last = pe.matmul(ps[VW * h:VW * (h + 1), ACC + i, 0:P], v_now[i][:, h, :],
                                 l_probs[i][:, h * P:(h + 1) * P], start=True, stop=True)
            last.then_inc(S["l_pv"], 1)

        for grp in range(L0_HEADS // 4):
            n0 = grp * TILES
            local_maxes(n0, 0, grp, 0)
            local_maxes(n0 + 1, 1, grp, 1)
            local_scores(n0, 0, grp, 0)

            def two_steps(t, grp=grp, n0=n0):
                for i in range(2):
                    local_maxes(n0 + i + t, t + i, grp, i)
                    local_scores(n0 + i - 1 + t, t + (i - 1), grp, 1 - i)
                    local_values(n0 + i - 2 + t, i)

            if grp == 0:
                two_steps(2)
            with pe.Fori(2 if grp == 0 else 1, TILES // 2) as pair:
                two_steps(2 * pair)
            local_scores(n0 + TILES - 1, TILES - 1, grp, 1)
            local_values(n0 + TILES - 2, 0)
            local_values(n0 + TILES - 1, 1)
            pe.wait_ge(S["l_acc"], n0 + TILES)
            strided = ob[:, :].rearrange("p (b j) -> p j b", j=L0_SPAN)
            for j in range(L0_SPAN):
                if j % 4 == 0:
                    need(pe, S["l_normed"], 4 * (grp - 1) + j // 4 + 1)
                last = pe.transpose(ps[:, j // 4, (j % 4) * P:(j % 4 + 1) * P], strided[:, j, :], ident[:, :])
                if j % 4 == 3:
                    last.then_inc(S["l_turned"], 1)
            pe.wait_ge(S["l_normed"], 4 * (grp + 1))

        turn_normed(1)

        def start_job(job):
            need(pe, S["misc_free"], job)

        def fold(u, i, job):
            pe.wait_ge(S["acc_copied"], u + 1)
            start_job(job)
            for t in range(QT):
                last = pe.transpose(misc[:, t * P:(t + 1) * P], o_part[:, i, t * P:(t + 1) * P], ident[:, :])
            last.then_inc(S["misc_full"], 1)

        def turn(units, job):
            pe.wait_ge(S["heads_normed"], units)
            start_job(job)
            for t in range(QT):
                last = pe.transpose(misc[:, t * P:(t + 1) * P], o_tok[:, t, :], ident[:, :])
            last.then_inc(S["misc_full"], 1)

        def project(w, rhs, job):
            start_job(job)
            pe.matmul(misc, w, rhs, start=True, stop=True).then_inc(S["misc_full"], 1)

        def project_tiles(lhs_tiles, w, job):
            start_job(job)
            for t in range(QT):
                last = pe.matmul(misc[:, t * P:(t + 1) * P], lhs_tiles[:, t * P:(t + 1) * P], w, start=True, stop=True)
            last.then_inc(S["misc_full"], 1)

        def out_job(kind, node, job):
            if kind == "nas":
                pe.wait_ge(S["node_weights_in"], node_weights_count(node))
                project(w_o[:, node % 2, :], o_chan, job)
            else:
                project_tiles(o_chan, w_o[:, 0, :], job)

        def rows_job(u, i, job):
            pe.wait_ge(S["maxparts_ready"], u + 1)
            start_job(job)
            for t in range(QT):
                last = pe.matmul(misc[M_ROW:K_ROWS, t * P:(t + 1) * P], max_parts[:, i, t, :], ident_b[:, :],
                                 start=True, stop=True)
            last.then_inc(S["misc_full"], 1)

        def max_tile(u, i, slot, k_base):
            tile = 16 * u + i
            if not isinstance(tile, int) or tile >= 2:
                pe.wait_ge(S["tile_done"], tile - 1)
            q0 = slot * BLK + (i // 4) * P
            at = k_base + (i % 4) * BLK
            keys = kst[0:M_ROW, at:at + BLK] if isinstance(at, int) else kst[0:M_ROW, bass.ds(at, BLK)]
            pe.matmul(ps[:, MAXES + i % 2, :], qst[0:M_ROW, q0:q0 + P], keys, start=True, stop=True) \
                .then_inc(S["tile_ready"], 1)

        for x in PLAN:
            kind = x.kind
            if isinstance(x, Serial):
                if kind == "rot" and x.jobs[0][0] == "q1":
                    turn_normed(2)
                    pe.wait_ge(S["turn_copied"], NBLK * 3)
                    pe.wait_ge(S["rot_in"], 16 * 8)
                    pe.wait_ge(S["rot_swapped"], 2)
                if kind == "nas" and x.jobs[0][0] == "q1":
                    pe.wait_ge(S["turn_copied"], NBLK * 2)
                    pe.wait_ge(S["q_weights_in"], 64)
                    pe.wait_ge(S["node_weights_in"], 64)
                job = x.before["job"]
                u0 = x.before["unit"]
                for name, b in x.jobs:
                    if name == "fold":
                        fold(u0 - 1, 1, job)
                    if name == "turn":
                        turn(u0, job)
                    if name == "out":
                        out_job(kind, x.node, job)
                    if name in ("q1", "k1") and kind == "rot":
                        project((w_q if name == "q1" else w_k)[:, 0, :], xT[:, b * BLK:(b + 1) * BLK], job)
                    if name in ("q2", "k2") and kind == "rot":
                        project((w_q if name == "q2" else w_k)[:, 1, :], xT[:, b * BLK:(b + 1) * BLK], job)
                    if name == "v2" and kind == "rot":
                        project_tiles(xT[:, b * BLK:(b + 1) * BLK], w_v[:, 0, :], job)
                    if kind == "nas":
                        plan = NODE[x.node]
                        if name == "q1":
                            project(w_q[:, 0, :], xT[:, 0:BLK], job)
                        if name == "q2":
                            at = node_col(0)
                            project(w_q[:, 1, :], nodes[:, at:at + BLK], job)
                        if name == "k1":
                            at = node_col(plan["k"], b)
                            project(w_k[:, 0, :], nodes[:, at:at + BLK], job)
                        if name == "k2":
                            project(w_k[:, 1, :], t_tmp[:, :], job)
                        if name == "v1":
                            at = node_col(plan["v"], b)
                            project(w_v[:, 0, :], nodes[:, at:at + BLK], job)
                        if name == "v2":
                            project_tiles(t_tmp[:, :], w_v[:, 1, :], job)
                    if name == "prime":
                        pe.wait_ge(S["rows_ready"], 1)
                        pe.wait_ge(S[f"{kind}_qa_in"], 16 * n_terms[kind])
                        pe.wait_ge(S[f"{kind}_k_in"], 16 * n_terms[kind] * NBLK)
                        for i in range(16):
                            max_tile(u0, i, 0, 0)
                        for i in range(8):
                            max_tile(u0 + 1, i, 1, N)
                        rows_job(u0, 0, job)
                    job += 1
                if kind == "nas" and x.jobs[0][0] == "fold" and x.node == NODES - 1:
                    pe.wait_ge(S["misc_free"], job)
                    for b in range(NBLK):
                        for t in range(QT):
                            last = pe.transpose(ps[:, b, t * P:(t + 1) * P], xT[:, (QT * b + t) * P:(QT * b + t + 1) * P],
                                                ident[:, :])
                        last.then_inc(S["cell_turned"], 1)
                continue

            def emit(b, x=x, kind=kind):
                c, heads, u0 = x.node, x.heads, x.unit(b)
                nt = 16 * n_terms[kind]
                par = (c % 2) * 8 if kind == "nas" else 0
                values = (lambda t, h: v_nas[:, c % 2, t, h, :]) if kind == "nas" else (lambda t, h: v_16[:, t, h, :])

                def pv_quad(u, h, quad):
                    pe.wait_ge(S["exp_done"], 8 * u + 2 * quad + 2)
                    if quad == 0:
                        need(pe, S["acc_copied"], u)
                    for k in range(4):
                        t = 4 * quad + k
                        last = pe.matmul(acc[VW * k:VW * (k + 1), :], values(t, h),
                                         probs[:, (2 * quad + k // 2) % 4, (k % 2) * BLK:(k % 2 + 1) * BLK],
                                         start=(quad == 0), stop=(quad == 3), skip_group_check=True)
                    last.then_inc(S["pv_done"], 1)

                for h in range(heads):
                    u = u0 + h
                    slot = par + h
                    for s in range(8):
                        if s == 0:
                            pe.wait_ge(S["misc_free"], x.jobs_so_far(b, h, s))
                        if not (isinstance(u, int) and 8 * u + s < 2):
                            pe.wait_ge(S["exp_done"], 8 * u + s - 1)
                        for k in range(2):
                            key0 = slot * N + (2 * s + k) * P
                            last = pe.matmul(ps[:, 2 * (s % 2) + k, :], kst[0:K_ROWS, key0:key0 + P],
                                             qst[0:K_ROWS, h * BLK:(h + 1) * BLK], start=True, stop=True)
                        last.then_inc(S["st_ready"], 1)
                        ahead, first = (1, 8 + 2 * s) if s < 4 else (2, 2 * s - 8)
                        v, hv = u + ahead, h + ahead
                        if not (x.last and hv >= heads):
                            wraps = hv >= heads
                            hv %= heads
                            if first == 0 and hv == 0 and wraps:
                                pe.wait_ge(S[f"{kind}_qa_in"], nt * (x.body(b) + 2))
                                if x.turns_over():
                                    pe.wait_ge(S["nas_k_in"], nt * (NBLK * (c + 1) + b + 1))
                            if first == 0 and hv == heads // 2 and not wraps:
                                pe.wait_ge(S[f"{kind}_qb_in"], nt * (x.body(b) + 1))
                            base = (x.pick(b, par, 8 - par) if wraps else par) + hv
                            for k in range(2):
                                max_tile(v, first + k, hv, base * N)
                        name = x.jobs.get((h, s))
                        if name:
                            job = x.job(b, h, s)
                        if name == "fold":
                            if h:
                                fold(u - 1, (h - 1) % 2, job)
                            else:
                                fold(u - 1, 1, job)
                        if name == "turn":
                            turn(u0, job)
                        if name == "out":
                            out_job(kind, x.out_of(b)[0], job)
                        if name == "rows":
                            rows_job(u + 1, (h + 1) % 2, job)
                        if name in ("q1", "q2") and kind == "rot":
                            project(w_q[:, 0 if name == "q1" else 1, :], xT[:, bass.ds((b + 1) * BLK, BLK)], job)
                        if kind == "nas":
                            if name == "q1":
                                pe.wait_ge(S["q_weights_in"], 64 * (x.body(b) + 2))
                                at = in_nodes(x.pick(b, node_col(c - 1), node_col(c) - NBLK * BLK) + (b + 1) * BLK)
                                project(w_q[:, 0, :], nodes[:, bass.ds(at, BLK)], job)
                            if name == "q2":
                                at = next_block(x, b)
                                project(w_q[:, 1, :], nodes[:, bass.ds(at, BLK)], job)
                            if name == "k1":
                                pe.wait_ge(S["node_weights_in"], 64 + 80 * (c + 1))
                                project(w_k[:, 0, :], nodes[:, bass.ds(node_col(NODE[c + 1]["k"]) + b * BLK, BLK)], job)
                            if name == "k2":
                                project(w_k[:, 1, :], t_tmp[:, :], job)
                            if name == "v1":
                                project(w_v[:, 0, :], nodes[:, bass.ds(node_col(NODE[c + 1]["v"]) + b * BLK, BLK)], job)
                            if name == "v2":
                                project_tiles(t_tmp[:, :], w_v[:, 1, :], job)
                        if s % 2 == 1:
                            if s == 1:
                                if h:
                                    pv_quad(u - 1, h - 1, 3)
                            else:
                                pv_quad(u, h, s // 2 - 1)
                pv_quad(u0 + heads - 1, heads - 1, 3)

            each_block(pe, x, emit)

        turn_normed(3)
        pe.wait_ge(S["turn_copied"], NBLK * 4)
        pe.wait_ge(S["mlp_in"], 16 * 9)
        for k in range(2):
            for t in range(8):
                j = 8 * k + t
                last = pe.matmul(ps[:, k, t * GA:(t + 1) * GA], xT[:, j * P:(j + 1) * P], gate_a, start=True, stop=True)
            last.then_inc(S["gates_ready"], 1)
        pe.wait_ge(S["gates_copied"], 2)
        for b in range(NBLK):
            for t in range(QT):
                last = pe.transpose(ps[0:EXPERTS * RANK, 2 + b, t * P:(t + 1) * P], low[:, QT * b + t, :], ident[:, :])
            last.then_inc(S["low_turned"], 1)

        def mlp_out(b):
            pe.wait_ge(S["hid_free"], FC * (b + 1))
            need(pe, S["mlp_free"], b - 1)
            for t in range(QT):
                for c in range(FC):
                    last = pe.matmul(ps[:, 6 + b % 2, t * P:(t + 1) * P], hid[:, b % 2, c, t * P:(t + 1) * P], wo[:, c, :],
                                     start=(c == 0), stop=(c == FC - 1))
            last.then_inc(S["mlp_full"], 1)

        for b in range(NBLK):
            pe.wait_ge(S["low_copied"], b + 1)
            for c in range(FC):
                i = FC * b + c
                need(pe, S["hid_free"], i - 1)
                pe.matmul(ps[:, i % 2, :], wi[:, c * P:(c + 1) * P], xT[:, b * BLK:(b + 1) * BLK], start=True, stop=False)
                pe.matmul(ps[:, i % 2, :], lora_b[:, c * P:(c + 1) * P], low_T[:, b * BLK:(b + 1) * BLK],
                          start=False, stop=True).then_inc(S["hid_full"], 1)
            if b:
                mlp_out(b - 1)
        mlp_out(NBLK - 1)

    @block.vector
    def _(dve):
        steps = [0]

        def link(ins):
            steps[0] += 1
            ins.then_inc(S["dve_step"], 1)
            dve.wait_ge(S["dve_step"], steps[0])

        norms = [0]

        def statistics(src, eps):
            for t in range(TILES):
                last = dve.bn_stats(stats[:, t, :], src[:, t, :])
            link(last)
            for t in range(TILES):
                last = dve.bn_aggr(mean_var[:, t, :], stats[:, t, :])
            link(last)
            dve.tensor_scalar(rstd[:, 0, :], mean_var[:, :, 1], eps, None, ALU.add).then_inc(S["var_ready"], 1)
            norms[0] += 1
            dve.wait_ge(S["std_ready"], norms[0])
            link(dve.reciprocal(rstd[:, 2, :], rstd[:, 1, :]))
            link(dve.tensor_tensor(rstd[:, 1, :], rstd[:, 2, :], rstd[:, 2, :], ALU.mult))
            link(dve.tensor_tensor(rstd[:, 1, :], rstd[:, 1, :], rstd[:, 0, :], ALU.mult))
            link(dve.tensor_scalar(rstd[:, 1, :], rstd[:, 1, :], -0.5, 1.5, ALU.mult, ALU.add))
            link(dve.tensor_tensor(rstd[:, 2, :], rstd[:, 2, :], rstd[:, 1, :], ALU.mult))

        def center(dst, src, t):
            return dve.tensor_scalar(dst[:, t, :], src[:, t, :], mean_var[:, t, 0:1], rstd[:, 2, t:t + 1],
                                     ALU.subtract, ALU.mult)

        def norm_for_turn():
            statistics(x_res, 1e-5)
            for b in range(NBLK):
                for t in range(QT * b, QT * (b + 1)):
                    last = center(normed_x, x_res, t)
                last.then_inc(S["normed"], 1)

        def norm_in_place(y, eps):
            statistics(y, eps)
            for t in range(TILES):
                last = center(y, y, t)
            link(last)

        def add_to_stream(y):
            link(dve.tensor_tensor(x_res[:, :, :], x_res[:, :, :], y[:, :, :], ALU.add))

        def spread(row, n):
            return row.unsqueeze(1).to_broadcast([P, n, row.shape[1]])

        link(dve.memset(vst[:, :], 0.0))
        link(dve.memset(v_cols[:, :, L0_DIM:L0_DIM + 1], 1.0))
        dve.wait_ge(S["const_in"], 16)
        dve.tensor_copy(ident_b[:, :], ident[:, :]).then_inc(S["consts_made"], 1)
        dve.wait_ge(S["small_in"], 16)
        dve.tensor_copy(pick_b[:, :], t_tmp[:, 0:P]).then_inc(S["consts_made"], 1)
        dve.wait_ge(S["x_in"], 16)
        norm_for_turn()

        dve.wait_ge(S["w0_in"], 16 * 6)
        dve.wait_ge(S["masks_in"], 16)
        for dst in (mask_rows[0], mask_rows[1], mask_only):
            dve.tensor_copy(dst, t_tmp[:, :]).then_inc(S["masks_made"], 1)
        dve.wait_ge(S["masks_made"], 3)
        dve.wait_ge(S["turned"], NBLK)
        for n in range(2 * NBLK):
            dve.wait_ge(S["l_full"], n + 1)
            need(dve, l_parts_sent[n % 2], 16 * (n // 2))
            need(dve, S["l_parts_ready"], n)
            i = n % 2
            bias = col[:, LB + 1:LB + 2] if n < NBLK else col[:, LB:LB + 1]
            dve.tensor_scalar(rest[:, :], ps[:, n % 4, :], bias, None, ALU.add).then_inc(S["l_free"], 1)
            dve.wait_ge(S["l_free"], n + 1)
            link(dve.tensor_copy(parts2[:, i, 0, :], rest[:, :]))
            link(dve.tensor_tensor(rest[:, :], rest[:, :], parts2[:, i, 0, :], ALU.subtract))
            link(dve.tensor_copy(parts2[:, i, 1, :], rest[:, :]))
            dve.tensor_tensor(parts2[:, i, 2, :], rest[:, :], parts2[:, i, 1, :], ALU.subtract) \
                .then_inc(S["l_parts_ready"], 1)
        for b in range(NBLK):
            n = 2 * NBLK + b
            dve.wait_ge(S["l_full"], n + 1)
            dve.tensor_tensor(v_16[:, QT * b:QT * (b + 1), :, 0:L0_DIM],
                              ps[:, n % 4, :].rearrange("p (t h d) -> p t h d", t=QT, d=L0_DIM),
                              w_o[:, 0, :].rearrange("p (h d) -> p h d", d=L0_DIM).unsqueeze(1)
                              .to_broadcast([P, QT, L0_HEADS, L0_DIM]), ALU.add).then_inc(S["l_free"], 1)
        dve.wait_ge(S["l_free"], 3 * NBLK)
        for sent in l_parts_sent:
            dve.wait_ge(sent, 16 * NBLK)
        dve.wait_ge(S["l_parts_ready"], 2 * NBLK)

        def local_max(n, i):
            dve.wait_ge(S["l_scores"], n + 1)
            need(dve, S["l_maxparts"], n - 1)
            dve.tensor_reduce(neg_max[:, i, :], ps[:, MAXES + i, :].rearrange("p (h k) -> p h k", h=4), AX.X, ALU.max,
                              negate=True).then_inc(S["l_neg"], 1)

        def local_vnow(n, t, grp, i):
            need(dve, S["l_pv"], n - 1)
            if isinstance(t, int):
                src = v_16[:, t, 4 * grp:4 * grp + 4, :].rearrange("p h w -> p (h w)")
            else:
                src = vst[:, bass.ds(t * (16 * VW) + 4 * grp * VW, 4 * VW)]
            dve.tensor_scalar((w_q, w_k)[i][:, 0, :], src, 1.0, None, ALU.mult).then_inc(S["l_vnow"], 1)

        def local_acc(n, t, i):
            dve.wait_ge(S["l_pv"], n + 1)
            dve.tensor_scalar(ob[:, bass.ds(t * P, P)], ps[:, ACC + i, 0:P], 1.0, None, ALU.mult) \
                .then_inc(S["l_acc"], 1)

        for grp in range(L0_HEADS // 4):
            n0 = grp * TILES
            local_max(n0, 0)
            local_vnow(n0, 0, grp, 0)
            local_max(n0 + 1, 1)
            local_vnow(n0 + 1, 1, grp, 1)
            with dve.Fori(1, TILES // 2) as pair:
                t = 2 * pair
                for i in range(2):
                    local_max(n0 + i + t, i)
                    local_acc(n0 + i - 2 + t, t + (i - 2), i)
                    local_vnow(n0 + i + t, t + i, grp, i)
            local_acc(n0 + TILES - 2, TILES - 2, 0)
            local_acc(n0 + TILES - 1, TILES - 1, 1)
            for k in range(4):
                dve.wait_ge(S["l_turned"], 4 * grp + k + 1)
                view = ps[:, k, :].rearrange("p (j h w) -> p j h w", j=4, w=VW)
                r = recip[:, :].rearrange("p (j h) -> p j h", j=4)
                link(dve.reciprocal(r, view[:, :, :, L0_DIM]))
                dst = att[:, 4 * grp:4 * grp + 4, 4 * k * L0_DIM:4 * (k + 1) * L0_DIM] \
                    .rearrange("p h (j d) -> p j h d", d=L0_DIM)
                dve.tensor_tensor(dst, view[:, :, :, 0:L0_DIM], r.unsqueeze(3).to_broadcast([P, 4, 4, L0_DIM]),
                                  ALU.mult).then_inc(S["l_normed"], 1)
                dve.wait_ge(S["l_normed"], 4 * grp + k + 1)

        norm_in_place(att, 1e-5)
        add_to_stream(att)
        norm_for_turn()
        link(dve.memset(v_cols[:, :, NAS_DIM:NAS_DIM + 1], 1.0))
        dve.wait_ge(S["nas_cols_in"], 48)
        dve.wait_ge(S["q_weights_in"], 64)

        def max_tile(u, i, par):
            dve.wait_ge(S["tile_ready"], 16 * u + i + 1)
            dve.tensor_reduce(row_max[:, par, i:i + 1], ps[:, MAXES + i % 2, :], AX.X, ALU.max) \
                .then_inc(S["tile_done"], 1)
            if i == 15:
                dve.wait_ge(S["tile_done"], 16 * u + 16)
                need(dve, S["maxparts_ready"], u - 1)
                dve.tensor_reduce(neg_max[:, par, :], row_max[:, par, :].rearrange("p (t k) -> p t k", k=4), AX.X,
                                  ALU.max, negate=True).then_inc(S["neg_ready"], 1)

        def fold(kind, u, h, job):
            d = dims[kind]
            dve.wait_ge(S["misc_full"], job + 1)
            need(dve, S["heads_normed"], u)
            dve.tensor_reduce(sums[:, :, 0:d + 1], misc.rearrange("p (t g w) -> p t w g", t=QT, w=VW)[:, :, 0:d + 1, :],
                              AX.X, ALU.add).then_inc(S["misc_free"], 1)
            dve.wait_ge(S["misc_free"], job + 1)
            dve.reciprocal(recip[:, 0:QT], sums[:, :, d]).then_inc(S["heads_recip"], 1)
            dve.wait_ge(S["heads_recip"], u + 1)
            dve.tensor_tensor(o_tok[:, :, h * d:(h + 1) * d], sums[:, :, 0:d],
                              recip[:, 0:QT].unsqueeze(2).to_broadcast([P, QT, d]), ALU.mult) \
                .then_inc(S["heads_normed"], 1)

        def out_job(kind, node, at, b, job):
            dve.wait_ge(S["misc_full"], job + 1)
            if kind == "nas":
                dst = nodes[:, bass.ds(at, BLK)]
                dve.scalar_tensor_tensor(dst, misc, col[:, AW + node:AW + node + 1], dst, ALU.mult, ALU.add) \
                    .then_inc(S["misc_free"], 1)
            else:
                dst = big[:, bass.ds(N + b * BLK, BLK)].rearrange("p (t d) -> p t d", d=D)
                dve.tensor_tensor(dst, misc.rearrange("p (t d) -> p t d", d=D), spread(rows[:, 1, :], QT), ALU.add) \
                    .then_inc(S["misc_free"], 1)

        def edge(dst, be, ew, job):
            dve.wait_ge(S["misc_full"], job + 1)
            dve.tensor_scalar(dst, misc, be, ew, ALU.add, ALU.mult).then_inc(S["misc_free"], 1)

        def lower_parts(job, split):
            dve.wait_ge(S["high_ready"], split + 1)
            dve.tensor_tensor(rest[:, :], misc, parts[:, 0, :], ALU.subtract).then_inc(S["misc_free"], 1)
            dve.wait_ge(S["misc_free"], job + 1)
            dve.tensor_copy(parts[:, 1, :], rest[:, :]).then_inc(S["mid_ready"], 1)
            dve.wait_ge(S["mid_ready"], split + 1)
            dve.tensor_tensor(parts[:, 2, :], rest[:, :], parts[:, 1, :], ALU.subtract).then_inc(S["parts_ready"], 1)

        def rotate_a(blk, bias, job):
            dve.wait_ge(S["misc_full"], job + 1)
            dve.scalar_tensor_tensor(rot_a, misc, bias, cos[:, bass.ds(blk * BLK, BLK)], ALU.add, ALU.mult) \
                .then_inc(S["misc_free"], 1)

        def rotate_b(blk, bias, job, split):
            k = split - rot_split0
            dve.wait_ge(S["misc_full"], job + 1)
            dve.scalar_tensor_tensor(rot_b, misc, bias, sin[:, bass.ds(blk * BLK, BLK)], ALU.add, ALU.mult) \
                .then_inc(S["misc_free"], 1)
            dve.wait_ge(S["misc_free"], job + 1)
            dve.tensor_tensor(rot_sum, rot_a, rot_b, ALU.add).then_inc(S["rot_sum_done"], 1)
            dve.wait_ge(S["rot_sum_done"], k + 1)
            need(dve, S["parts_sent"], 16 * split)
            dve.tensor_copy(parts[:, 0, :], rot_sum).then_inc(S["rot_high_ready"], 1)
            dve.wait_ge(S["rot_high_ready"], k + 1)
            dve.tensor_tensor(rest[:, :], rot_sum, parts[:, 0, :], ALU.subtract).then_inc(S["rest_ready"], 1)
            dve.wait_ge(S["rest_ready"], k + 1)
            dve.tensor_copy(parts[:, 1, :], rest[:, :]).then_inc(S["mid_ready"], 1)
            dve.wait_ge(S["mid_ready"], split + 1)
            dve.tensor_tensor(parts[:, 2, :], rest[:, :], parts[:, 1, :], ALU.subtract).then_inc(S["parts_ready"], 1)

        def cell_values(par, b, job):
            dve.wait_ge(S["misc_full"], job + 1)
            size = NAS_HEADS * VW
            dst = vst[:, bass.ds(par * TILES * size + b * (QT * size), QT * size)] \
                .rearrange("p (t h w) -> p t h w", t=QT, w=VW)[:, :, :, 0:NAS_DIM]
            dve.tensor_scalar(dst, misc.rearrange("p (t h d) -> p t h d", t=QT, d=NAS_DIM), 1.0, None, ALU.mult) \
                .then_inc(S["misc_free"], 1)

        for x in PLAN:
            kind = x.kind
            if isinstance(x, Serial):
                if kind == "rot" and x.jobs[0][0] == "q1":
                    dve.wait_ge(S["rot_in"], 16 * 8)
                    dve.wait_ge(S["rot_rows_in"], 32)
                    for w in (w_q, w_k):
                        a = w[:, 0, :].rearrange("p (h a r) -> p h a r", a=2, r=ROT_DIM // 2)
                        z = w[:, 1, :].rearrange("p (h a r) -> p h a r", a=2, r=ROT_DIM // 2)
                        for i in range(2):
                            last = dve.tensor_copy(z[:, :, i, :], a[:, :, 1 - i, :])
                        last.then_inc(S["rot_swapped"], 1)
                    dve.memset(qst[64:M_ROW, :].bitcast(F32), 0.0).then_inc(S["pads_ready"], 1)
                    link(dve.memset(v_cols[:, :, ROT_DIM:NAS_DIM + 1], 0.0))
                    link(dve.memset(v_cols[:, :, ROT_DIM:ROT_DIM + 1], 1.0))
                job, split, u0 = x.before["job"], x.before["split"], x.before["unit"]
                for name, b in x.jobs:
                    c = x.node
                    if name == "fold":
                        fold(kind, u0 - 1, heads_of[kind] - 1, job)
                    if name == "out":
                        out_job(kind, c, node_col(c, b), b, job)
                    if kind == "nas":
                        plan = NODE[c]
                        if name == "q1":
                            at = node_col(0)
                            edge(nodes[:, at:at + BLK], col[:, QBE:QBE + 1], col[:, QEW:QEW + 1], job)
                        if name == "k1":
                            edge(t_tmp[:, :], col[:, BE + plan["ek"]:BE + plan["ek"] + 1],
                                 col[:, EW + 3 * c + 1:EW + 3 * c + 2], job)
                        if name == "v1":
                            edge(t_tmp[:, :], col[:, BE + plan["ev"]:BE + plan["ev"] + 1],
                                 col[:, EW + 3 * c + 2:EW + 3 * c + 3], job)
                        if name in ("q2", "k2"):
                            lower_parts(job, split)
                        if name == "v2":
                            cell_values(c % 2, b, job)
                    else:
                        r = RB if name in ("q1", "q2") else RB + 2
                        if name in ("q1", "k1"):
                            rotate_a(b, col[:, r:r + 1], job)
                        if name in ("q2", "k2"):
                            rotate_b(b, col[:, r + 1:r + 2], job, split)
                        if name == "v2":
                            dve.wait_ge(S["misc_full"], job + 1)
                            dve.tensor_tensor(v_16[:, QT * b:QT * (b + 1), :, 0:ROT_DIM],
                                              misc.rearrange("p (t h d) -> p t h d", t=QT, d=ROT_DIM),
                                              rows[:, 0, :].rearrange("p (h d) -> p h d", d=ROT_DIM).unsqueeze(1)
                                              .to_broadcast([P, QT, ROT_HEADS, ROT_DIM]), ALU.add) \
                                .then_inc(S["misc_free"], 1)
                    if name == "prime":
                        for i in range(16):
                            max_tile(u0, i, 0)
                        for i in range(8):
                            max_tile(u0 + 1, i, 1)
                    split += name in ("q2", "k2")
                    job += 1
                if kind == "nas" and x.jobs[0][0] == "fold" and c == NODES - 1:
                    dve.wait_ge(S["cell_copied"], NBLK)
                    dve.wait_ge(S["norm_rows_in"], 32)
                    norm_in_place(tok, 1e-6)
                    link(dve.tensor_tensor(tok, tok, spread(t_tmp[:, 0:D], TILES), ALU.mult))
                    link(dve.tensor_tensor(tok, tok, spread(t_tmp[:, D:2 * D], TILES), ALU.add))
                    norm_in_place(tok, 1e-5)
                    add_to_stream(tok)
                    norm_for_turn()
                continue

            def emit(b, x=x, kind=kind):
                c, heads, u0 = x.node, x.heads, x.unit(b)
                for h in range(heads):
                    u = u0 + h
                    for s in range(8):
                        ahead, first = (1, 8 + 2 * s) if s < 4 else (2, 2 * s - 8)
                        if not (x.last and h + ahead >= heads):
                            for k in range(2):
                                max_tile(u + ahead, first + k, (h + ahead) % 2)
                        name = x.jobs.get((h, s))
                        if not name:
                            continue
                        job = x.job(b, h, s)
                        if name == "fold":
                            fold(kind, u - 1, (h - 1) % heads, job)
                        if name == "out":
                            node, blk = x.out_of(b)
                            out_job(kind, node, node_col(node) + blk * BLK, blk, job)
                        if name == "q1" and kind == "rot":
                            rotate_a(b + 1, col[:, RB:RB + 1], job)
                        if name == "q2" and kind == "rot":
                            rotate_b(b + 1, col[:, RB + 1:RB + 2], job, x.split(b))
                        if kind == "nas":
                            n = c + 1
                            if name == "q1":
                                edge(nodes[:, bass.ds(next_block(x, b), BLK)], col[:, QBE:QBE + 1],
                                     col[:, QEW:QEW + 1], job)
                            if name == "q2":
                                lower_parts(job, x.split(b))
                            if name == "k1":
                                e = BE + NODE[n]["ek"]
                                edge(t_tmp[:, :], col[:, e:e + 1], col[:, EW + 3 * n + 1:EW + 3 * n + 2], job)
                            if name == "k2":
                                lower_parts(job, x.split(b) + 1)
                            if name == "v1":
                                e = BE + NODE[n]["ev"]
                                edge(t_tmp[:, :], col[:, e:e + 1], col[:, EW + 3 * n + 2:EW + 3 * n + 3], job)
                            if name == "v2":
                                cell_values(n % 2, b, job)

            each_block(dve, x, emit)

        dve.wait_ge(S["misc_free"], job)
        norm_in_place(tok, 1e-5)
        add_to_stream(tok)
        norm_for_turn()

        dve.wait_ge(S["mlp_in"], 16 * 9)
        for k in range(2):
            dve.wait_ge(S["gates_ready"], k + 1)
            view = ps[:, k, 0:8 * GA].rearrange("p (t e) -> p t e", e=GA)
            link(dve.tensor_tensor(logits[:, 8 * k:8 * k + 8, :], view[:, :, 0:EXPERTS], spread(gate_bias, 8), ALU.add))

        def wide(v):
            return v.unsqueeze(2).to_broadcast([P, TILES, EXPERTS])

        link(dve.tensor_reduce(top, logits, AX.X, ALU.max))
        link(dve.tensor_tensor(chosen, logits, wide(top), ALU.is_equal))
        link(dve.tensor_tensor(chosen, chosen, spread(rank_row, TILES), ALU.mult))
        link(dve.tensor_reduce(top, chosen, AX.X, ALU.max))
        link(dve.tensor_tensor(chosen, chosen, wide(top), ALU.is_equal))
        for k in range(2):
            view = ps[:, k, 0:8 * GA].rearrange("p (t e) -> p t e", e=GA)[:, :, EXPERTS:GA] \
                .rearrange("p t (e r) -> p t e r", r=RANK)
            dve.tensor_tensor(low[:, 8 * k:8 * k + 8, :].rearrange("p t (e r) -> p t e r", r=RANK), view,
                              chosen[:, 8 * k:8 * k + 8, :].unsqueeze(3).to_broadcast([P, 8, EXPERTS, RANK]),
                              ALU.mult).then_inc(S["gates_copied"], 1)
        for b in range(NBLK):
            dve.wait_ge(S["mlp_full"], b + 1)
            dve.tensor_tensor(tok[:, QT * b:QT * (b + 1), :], ps[:, 6 + b % 2, :].rearrange("p (t d) -> p t d", d=D),
                              spread(wo_bias, QT), ALU.add).then_inc(S["mlp_free"], 1)
        dve.wait_ge(S["mlp_free"], NBLK)
        norm_in_place(tok, 1e-5)
        for b in range(NBLK):
            at = slice(QT * b, QT * (b + 1))
            dve.tensor_tensor(x_res[:, at, :], x_res[:, at, :], tok[:, at, :], ALU.add).then_inc(S["out_ready"], 1)


def kernel(**inputs):
    import concourse.bacc as bacc
    from concourse.bass_utils import run_bass_kernel_spmd as run

    def get(name):
        return np.asarray(inputs[name])

    def heads_swapped(bias):
        return bias.reshape(ROT_HEADS, 2, ROT_DIM // 2)[:, ::-1, :].reshape(-1)

    pos = np.arange(P)
    pick = np.zeros((P, P), np.float32)
    pick[:P // L0_SPAN] = pos // L0_SPAN == np.arange(P // L0_SPAN)[:, None]
    mask = np.zeros((P, BLK), np.float32)
    mask[:P // L0_SPAN] = np.tile((pick[:P // L0_SPAN] - 1) * np.float32(1e30), (1, 4))
    pick[M_ROW:K_ROWS] = 1.0
    half = ROT_DIM // 2
    inv = (np.float32(1.0) / np.float32(10000.0) ** (np.arange(half, dtype=np.float32) / np.float32(half))) \
        .astype(np.float32)
    angle = (inv[:, None] * np.arange(N, dtype=np.float32)[None, :]).astype(np.float32)
    cos = np.tile(np.cos(angle), (2 * ROT_HEADS, 1)).astype(np.float32)
    sin = np.tile(np.concatenate([-np.sin(angle), np.sin(angle)]), (ROT_HEADS, 1)).astype(np.float32)

    arrays = {
        "x": get("L0_attn_hidden_states"),
        "w_qkvT": get("L0_attn_w_qkv").T, "b_qkv": get("L0_attn_b_qkv"),
        "ew": get("L0_ffn_ew"), "act_w": get("L0_ffn_act_w"), "We": get("L0_ffn_We"), "be": get("L0_ffn_be"),
        "Wq": get("L0_ffn_Wq"), "Wk": get("L0_ffn_Wk"), "Wv": get("L0_ffn_Wv"), "Wo": get("L0_ffn_Wo"),
        "ln_g": get("L0_ffn_ln_g"), "ln_b": get("L0_ffn_ln_b"),
        "wq_w": get("L1_attn_wq_w"), "wk_w": get("L1_attn_wk_w"), "wv_w": get("L1_attn_wv_w"),
        "wo_w": get("L1_attn_wo_w"), "wq_b": get("L1_attn_wq_b"), "wk_b": get("L1_attn_wk_b"),
        "wq_b_swapped": heads_swapped(get("L1_attn_wq_b")), "wk_b_swapped": heads_swapped(get("L1_attn_wk_b")),
        "wv_b": get("L1_attn_wv_b"), "wo_b": get("L1_attn_wo_b"),
        "gate_T": get("L1_ffn_gate_W").T, "gate_b": get("L1_ffn_gate_b"),
        "wi_T": get("L1_ffn_wi_W").T, "wi_b": get("L1_ffn_wi_b"),
        "wo_T": get("L1_ffn_wo_W").T, "ffn_wo_b": get("L1_ffn_wo_b"),
        "lora_AT": get("L1_ffn_lora_A").reshape(EXPERTS * RANK, D).T,
        "lora_BT": get("L1_ffn_lora_B").transpose(0, 2, 1).reshape(EXPERTS * RANK, FF),
        "c_ident": np.eye(P, dtype=np.float32), "c_pick": pick, "c_mask": mask,
        "c_cos": cos, "c_sin": sin,
        "c_rank": np.arange(EXPERTS, 0, -1, dtype=np.float32)[None, :],
    }
    nc = bacc.Bacc("TRN2", target_bir_lowering=False, num_devices=1)
    given, A = {}, {}
    for name, a in arrays.items():
        a = np.ascontiguousarray(a)
        given[f"in_{name}"] = a
        A[name] = nc.dram_tensor(f"in_{name}", a.shape, mybir.dt.from_np(a.dtype), kind="ExternalInput").ap()
    out = nc.dram_tensor("out", (1, N, D), F32, kind="ExternalOutput").ap()
    build(nc, A, out)
    r = run(nc, [given], core_ids=[0])
    return r.results[0]["out"]
```

```python
from contextlib import ExitStack

import numpy as np

import concourse.bass as bass
from concourse import mybir

F32 = mybir.dt.float32
BF16 = mybir.dt.bfloat16
U32 = mybir.dt.uint32
ALU = mybir.AluOpType
ACT = mybir.ActivationFunctionType
AX = mybir.AxisListType

P = 128
N = 2048
D = 128
TILES = N // P
BLK = 512
NBLK = N // BLK
QT = BLK // P
M_ROW = 96
K_ROWS = M_ROW + 3
VW = 32
NODES = 6
MAX_PREV = 5
L0_HEADS, L0_DIM, L0_SPAN = 16, 8, 16
NAS_HEADS, NAS_DIM = 8, 16
ROT_HEADS, ROT_DIM = 16, 8
EXPERTS, RANK, FF = 8, 4, 512
FC = FF // P

TERMS = {
    16: ((0, 0, 1, 0, 1, 2), (0, 1, 0, 2, 1, 0)),
    8: ((0, 0, 0, 1, 1, 1, 2, 2, 2), (0, 1, 2, 0, 1, 2, 0, 1, 2)),
}


FOLD_STEP, ROWS_STEP = 3, 5


def node_plan():
    plan, first = [], 0
    for c in range(NODES):
        n = min(c + 1, MAX_PREV)
        src = c - n
        plan.append(dict(eq=first + n - 1, ek=first, ev=first + n // 2, q=c - 1, k=src, v=src + n // 2))
        first += n
    return plan


NODE = node_plan()


def slot_of(node):
    return 0 if node == NODES - 1 else node + 1


def node_col(node, blk=0):
    return slot_of(node) * N + blk * BLK


BANK = [i % 3 for i in range(15)] + [1]
TAKEN = [next(d for d in range(1, 17) if BANK[(i - d) % 16] == BANK[i]) for i in range(16)]


def maxima_of(s):
    return (1, 8 + 2 * s) if s < 4 else (2, 2 * s - 8)


class Body:

    def __init__(self, kind, node, b0, b1, before, *, with_out, next_q, next_k, next_v, last):
        self.kind, self.node, self.b0, self.b1 = kind, node, b0, b1
        self.heads = NAS_HEADS if kind == "nas" else ROT_HEADS
        self.before = dict(before)
        self.with_out, self.next_q, self.next_k, self.next_v, self.last = with_out, next_q, next_k, next_v, last
        self.jobs = {}
        for h in range(self.heads):
            if h or with_out:
                self.jobs[h, FOLD_STEP] = "fold"
            if not (last and h == self.heads - 1):
                self.jobs[h, ROWS_STEP] = "rows"
        places = {"turn": (0, 7), "k1": (1, 1), "k2": (1, 7), "q1": (2, 7), "q2": (3, 1), "out": (3, 7),
                  "v1": (4, 7), "v2": (5, 7)}
        for names, wanted in (("turn out", with_out), ("q1 q2", next_q), ("k1 k2", next_k), ("v1 v2", next_v)):
            if wanted:
                self.jobs.update({places[name]: name for name in names.split()})
        self.goes_on = False
        self.late_before = 0
        self.order = {hs: n for n, hs in enumerate(sorted(self.jobs))}
        self.n_jobs = len(self.jobs)
        self.n_splits = int(next_q) + int(next_k)

    def late(self):
        return sum(k > (self.heads - 1, ROWS_STEP) for k in self.jobs)

    def unit(self, b):
        return self.before["unit"] + self.heads * (b - self.b0)

    def job(self, b, h, s):
        return self.before["job"] + self.n_jobs * (b - self.b0) + self.order[h, s]

    def job_before(self, h, s, k, ago):
        half = 16 * h + 2 * s + k - ago
        at = (half // 16, half % 16 // 2)
        return (self.jobs.get(at) if half % 2 and half >= 0 else None, *at)

    def k_split(self, b):
        return self.before["split"] + self.n_splits * (b - self.b0)

    def q_split(self, b):
        return self.k_split(b) + int(self.next_k)

    def body(self, b):
        return self.before["body"] + (b - self.b0)

    def jobs_so_far(self, b, h, s):
        return self.before["job"] + self.n_jobs * (b - self.b0) + sum(k < (h, s) for k in self.jobs)

    def out_of(self, b):
        return (self.node, b - 1) if self.b0 or self.kind == "rot" else (self.node - 1, NBLK - 1)

    def turns_over(self):
        return self.kind == "nas" and self.b1 == NBLK and not self.last

    def pick(self, b, here, there):
        if not self.turns_over():
            return here
        if self.b1 - self.b0 == 1:
            return there
        return here + (b // (NBLK - 1)) * (there - here)


class Serial:

    def __init__(self, kind, node, before, jobs):
        self.kind, self.node, self.before, self.jobs = kind, node, dict(before), jobs


def make_plan():
    plan = []
    count = dict(unit=0, job=0, split=0, body=0)

    def body(kind, node, b0, b1, **kw):
        x = Body(kind, node, b0, b1, count, **kw)
        if isinstance(plan[-1], Body):
            plan[-1].goes_on = True
            x.late_before = plan[-1].late()
        plan.append(x)
        n = b1 - b0
        count["unit"] += x.heads * n
        count["job"] += x.n_jobs * n
        count["split"] += x.n_splits * n
        count["body"] += n

    def serial(kind, node, jobs):
        plan.append(Serial(kind, node, count, jobs))
        count["job"] += len(jobs)
        count["split"] += sum(name in ("q2", "k2") for name, _ in jobs)

    keys = [(j, b) for b in range(NBLK) for j in ("k1", "k2")]
    queries = [("q1", 0), ("q2", 0)]
    values = [(j, b) for b in range(NBLK) for j in ("v1", "v2")]
    finish = [("fold", NBLK - 1), ("turn", NBLK - 1), ("out", NBLK - 1)]
    serial("nas", 0, queries + keys + values + [("prime", 0)])
    for c in range(NODES):
        end = c == NODES - 1
        kw = dict(next_q=True, next_k=not end, next_v=not end and c > 0, last=False)
        body("nas", c, 0, 1, with_out=c > 1, **kw)
        body("nas", c, 1, NBLK - end, with_out=True, **kw)
        if end:
            body("nas", c, NBLK - 1, NBLK, with_out=True, next_q=False, next_k=False, next_v=False, last=True)
        if c == 0:
            serial("nas", 0, finish)
            serial("nas", 1, values)
    serial("nas", NODES - 1, finish)
    count["body"] = 0
    serial("rot", 0, queries + keys + [("v2", b) for b in range(NBLK)] + [("prime", 0)])
    kw = dict(next_k=False, next_v=False)
    body("rot", 0, 0, 1, with_out=False, next_q=True, last=False, **kw)
    body("rot", 0, 1, NBLK - 1, with_out=True, next_q=True, last=False, **kw)
    body("rot", 0, NBLK - 1, NBLK, with_out=True, next_q=False, last=True, **kw)
    serial("rot", 0, finish)
    return plan


PLAN = make_plan()


def need(eng, semaphore, value):
    if not (isinstance(value, int) and value <= 0):
        eng.wait_ge(semaphore, value)


def each_block(eng, body, emit):
    if body.b1 - body.b0 == 1:
        emit(body.b0)
    else:
        with eng.Fori(body.b0, body.b1) as b:
            emit(b)


def build(nc, A, out):
    with ExitStack() as ctx:
        build_program(nc, ctx, A, out)


def build_program(nc, ctx, A, out):
    def sb(name, shape, dt):
        return ctx.enter_context(nc.sbuf_tensor(name, shape, dt))

    def sem(name):
        return ctx.enter_context(nc.semaphore(name))

    big = sb("big", [P, 6 * N + 4096 + 4096], F32)
    nodes = big[:, 0:6 * N]
    xT = big[:, 0:N]
    tok = big[:, N:2 * N].rearrange("p (t d) -> p t d", d=D)
    att = big[:, 0:N].rearrange("p (t d) -> p t d", d=D)
    qst = big[:, 6 * N:6 * N + 4096].bitcast(BF16)
    probs = big[:, 6 * N + 4096:6 * N + 8192].rearrange("p (i n) -> p i n", i=8)
    q_loc = big[:, N:N + 16 * N // 2].bitcast(BF16)
    kst = sb("kst", [P, 16 * N], BF16)
    vst = sb("vst", [P, 256 * VW], F32)
    v_cols = vst[:, :].rearrange("p (x w) -> p x w", w=VW)
    v_nas = vst[:, :].rearrange("p (a t h w) -> p a t h w", a=2, t=TILES, h=NAS_HEADS)
    v_16 = vst[:, :].rearrange("p (t h w) -> p t h w", t=TILES, h=16)
    x_res = sb("x_res", [P, TILES, D], F32)
    ob = sb("ob", [P, N], F32)
    normed_x = ob[:, :].rearrange("p (t d) -> p t d", d=D)
    o_part = ob[:, 0:1024].rearrange("p (i n) -> p i n", i=2)
    o_tok = ob[:, 1024:1536].rearrange("p (t d) -> p t d", d=D)
    o_chan = ob[:, 1536:2048]
    parts2 = ob[:, 0:1536].bitcast(BF16).rearrange("p (i t n) -> p i t n", i=2, t=3)
    parts = sb("parts", [P, 3, BLK], BF16)
    rest = sb("rest", [P, BLK], F32)
    t_tmp = sb("t_tmp", [P, BLK], F32)
    l_probs = (rest, t_tmp)
    w_q, w_k, w_v, w_o = (sb(f"w_{x}", [P, 2, D], F32) for x in "qkvo")
    ident = sb("ident", [P, P], F32)
    ident_b = sb("ident_b", [P, P], BF16)
    pick_b = sb("pick_b", [P, P], BF16)
    col = sb("col", [P, 72], F32)
    BE, EW, AW, QBE, QEW, RB, LB, FB, EB = 0, 20, 38, 44, 45, 46, 50, 52, 56
    stats = sb("stats", [P, TILES, 6], F32)
    mean_var = sb("mean_var", [P, TILES, 2], F32)
    rstd = sb("rstd", [P, 3, TILES], F32)
    row_max = sb("row_max", [P, 2, 16], F32)
    neg_max = sb("neg_max", [P, 2, 4], F32)
    neg_rest = sb("neg_rest", [P, 2, 4], F32)
    zeros = sb("zeros", [P, 4], F32)
    max_parts = sb("max_parts", [P, 2, 4, 3], BF16)
    sums = sb("sums", [P, QT, NAS_DIM + 1], F32)
    recip = sb("recip", [P, 16], F32)
    v_now = [w[:, 0, :].rearrange("p (h w) -> p h w", w=VW) for w in (w_q, w_k)]
    mask_rows = [parts[:, 0, :], parts[:, 1, :]]
    mask_only = parts[:, 2, :]
    cos, sin = big[:, 2 * N:3 * N], big[:, 3 * N:4 * N]
    rot_a, rot_b, rot_sum = (big[:, 4 * N + i * BLK:4 * N + (i + 1) * BLK] for i in range(3))
    rows = big[:, 4 * N + 3 * BLK:4 * N + 3 * BLK + 384].rearrange("p (i d) -> p i d", d=D)
    M0 = 5 * N
    wi = big[:, M0:M0 + FF]
    wo = big[:, M0 + FF:M0 + 2 * FF].rearrange("p (c d) -> p c d", d=D)
    lora_b = big[0:EXPERTS * RANK, M0 + 2 * FF:M0 + 3 * FF]
    GA = EXPERTS + EXPERTS * RANK
    gate_a = big[:, M0 + 3 * FF:M0 + 3 * FF + GA]
    gate_bias = big[:, M0 + 3 * FF + 64:M0 + 3 * FF + 64 + EXPERTS]
    rank_row = big[:, M0 + 3 * FF + 80:M0 + 3 * FF + 80 + EXPERTS]
    wo_bias = big[:, M0 + 3 * FF + 128:M0 + 3 * FF + 256]
    hid = vst[:, 0:2 * FC * BLK].rearrange("p (i c n) -> p i c n", i=2, c=FC)
    low_T = big[0:EXPERTS * RANK, 3 * N:4 * N]
    G0 = 4 * N
    logits = big[:, G0:G0 + 128].rearrange("p (t e) -> p t e", e=EXPERTS)
    chosen = big[:, G0 + 128:G0 + 256].rearrange("p (t e) -> p t e", e=EXPERTS)
    top = big[:, G0 + 256:G0 + 272]
    low = big[:, G0 + 512:G0 + 1024].rearrange("p (t r) -> p t r", r=EXPERTS * RANK)

    ps = ctx.enter_context(nc.psum_tensor("ps", [P, 8, BLK], F32))
    MAXES, ACC, MISC = 3, 6, 7
    L_MAXES = 4
    misc = ps[:, MISC, :]
    acc = ps[:, ACC, :]

    scratch = {x: nc.dram_tensor(f"parts_{x}", [3, P, N], BF16, kind="Internal").ap() for x in "qk"}

    def stacked(x, term, dim, heads, c0, c1):
        return scratch[x][term, :, c0:c1].rearrange("(h r) n -> r h n", r=dim)[:, heads, :]

    S = {name: sem(name) for name in """
        x_in const_in small_in w0_in w0_row_in masks_in nas_cols_in norm_rows_in rot_in rot_rows_in mlp_in
        consts_made rows_ready zeros_ready masks_made
        var_ready std_ready normed turned turn_copied
        dve_step
        l_full l_free l_parts_ready l_parts_sent_even l_parts_sent_odd l_q_in l_k_in l_values
        l_scores l_neg l_pool l_maxparts l_rows l_rows_in l_st l_exp l_vnow l_pv l_acc l_turned l_normed
        tile_ready tile_done neg_ready pool_step maxparts_ready st_ready exp_done pv_done acc_copied
        misc_full misc_free high_ready mid_ready rest_ready parts_ready parts_sent
        heads_summed heads_recip heads_normed rot_a_done rot_b_done rot_sum_done
        q_weights_in node_weights_in nas_k_in nas_qa_in nas_qb_in rot_k_in rot_qa_in rot_qb_in
        cell_turned cell_copied edges_ready gates_ready gates_copied low_ready low_turned low_copied hid_full hid_free
        mlp_full mlp_free pads_ready out_ready rot_swapped rot_high_ready out_in""".split()}

    l_parts_sent = (S["l_parts_sent_even"], S["l_parts_sent_odd"])
    block = ctx.enter_context(nc.Block())
    n_terms = {kind: len(TERMS[dim][0]) for kind, dim in (("nas", NAS_DIM), ("rot", ROT_DIM))}
    dims = {"nas": NAS_DIM, "rot": ROT_DIM}
    heads_of = {"nas": NAS_HEADS, "rot": ROT_HEADS}
    rot_split0 = next(x for x in PLAN if x.kind == "rot").before["split"]

    def node_weights_count(node):
        return 64 + 80 * (node + 1) - 64 * (node == NODES - 1)

    def in_nodes(at):
        if isinstance(at, int):
            return at
        return nc.s_assert_within(at, 0, 6 * N - BLK, skip_runtime_bounds_check_because="blocks 0..3 of slots 0..5")

    def next_block(x, b):
        return in_nodes(x.pick(b, node_col(x.node), node_col(min(x.node + 1, NODES - 1)) - N) + (b + 1) * BLK)


    @block.sync
    def _(sp):
        def load(dst, src, semaphore, **kw):
            sp.dma_start(dst, src, **kw).then_inc(S[semaphore], 16)

        load(x_res[:, :, :], A["x"][0].rearrange("(t p) d -> p t d", p=P), "x_in")
        load(ident[:, :], A["c_ident"], "const_in")
        for w, i in ((w_q, 0), (w_k, 1), (w_v, 2)):
            load(w[:, 0, :], A["w_qkvT"][:, i * D:(i + 1) * D], "w0_in")
        for i in range(2):
            load(col[:, LB + i:LB + i + 1], A["b_qkv"][i * D:(i + 1) * D].rearrange("(p a) -> p a", a=1), "w0_in")
        load(w_o[:, 0, :], A["b_qkv"][2 * D:3 * D].rearrange("(a d) -> a d", a=1).partition_broadcast(P), "w0_in")
        load(t_tmp[:, 0:P], A["c_pick"], "small_in")
        sp.wait_ge(S["consts_made"], 2)
        load(t_tmp[:, :], A["c_mask"], "masks_in")

        terms_q, terms_k = TERMS[L0_DIM]
        for n in range(2 * NBLK):
            x, b = ("k", n) if n < NBLK else ("q", n - NBLK)
            sp.wait_ge(S["l_parts_ready"], n + 1)
            sp.dma_start(scratch[x][:, :, b * BLK:(b + 1) * BLK].rearrange("t p n -> p t n"),
                         parts2[:, n % 2, :, :]).then_inc(l_parts_sent[n % 2], 16)
            if n == NBLK - 1 or n == 2 * NBLK - 1:
                sp.wait_ge(S["rows_ready"], 2)
                for sent in l_parts_sent:
                    sp.wait_ge(sent, 16 * (n + 1) // 2)
                if n == NBLK - 1:
                    for j, term in enumerate(terms_k):
                        load(kst[8 * j:8 * j + 8, :].rearrange("p (h n) -> p h n", n=N),
                             stacked("k", term, L0_DIM, slice(0, 16), 0, N), "l_k_in")
                else:
                    for j, term in enumerate(terms_q):
                        load(q_loc[8 * j:8 * j + 8, :].rearrange("p (h n) -> p h n", n=N),
                             stacked("q", term, L0_DIM, slice(0, 16), 0, N), "l_q_in")

        sp.wait_ge(S["l_normed"], 16)
        load(col[:, BE:BE + 20], A["be"].rearrange("e d -> d e"), "nas_cols_in", allow_slow_non_contiguous=True)
        load(col[:, EW:EW + 18], A["ew"].rearrange("c g -> (c g)").rearrange("(a n) -> a n", a=1)
             .partition_broadcast(P), "nas_cols_in")
        load(col[:, AW:AW + NODES], A["act_w"].rearrange("(a n) -> a n", a=1).partition_broadcast(P), "nas_cols_in")

        def node_q_weights(b, x, node_here, node_there):
            e, c = NODE[node_here]["eq"], node_here
            if x:
                e, c = x.pick(b, e, NODE[node_there]["eq"]), x.pick(b, c, node_there)
            load(w_q[:, 0, :], A["We"][bass.ds(e, 1)].rearrange("a k n -> (a k) n"), "q_weights_in")
            load(w_q[:, 1, :], A["Wq"][bass.ds(c, 1)].rearrange("a k n -> (a k) n"), "q_weights_in")
            load(col[:, QBE:QBE + 1], A["be"][bass.ds(e, 1), :].rearrange("a d -> d a"), "q_weights_in",
                 allow_slow_non_contiguous=True)
            load(col[:, QEW:QEW + 1], A["ew"][bass.ds(c, 1), 0:1].partition_broadcast(P)
                 .rearrange("p a b -> p (a b)"), "q_weights_in")

        def kv_weights(c):
            load(w_k[:, 0, :], A["We"][NODE[c]["ek"]], "node_weights_in")
            load(w_k[:, 1, :], A["Wk"][c], "node_weights_in")
            load(w_v[:, 0, :], A["We"][NODE[c]["ev"]], "node_weights_in")
            load(w_v[:, 1, :], A["Wv"][c], "node_weights_in")

        node_q_weights(0, None, 0, 0)
        kv_weights(0)

        def send_parts(x, split, ready=None):
            sp.wait_ge(S["parts_ready"], split + 1 if ready is None else ready)
            sp.dma_start(scratch[x][:, :, 0:BLK].rearrange("t p n -> p t n"),
                         parts[:, :, :]).then_inc(S["parts_sent"], 16)
            sp.wait_ge(S["parts_sent"], 16 * (split + 1))

        def stage_queries(kind, half, semaphore):
            d, h2 = dims[kind], heads_of[kind] // 2
            for j, term in enumerate(TERMS[d][0]):
                load(qst[d * j:d * j + d, half * h2 * BLK:(half + 1) * h2 * BLK].rearrange("p (h n) -> p h n", n=BLK),
                     stacked("q", term, d, slice(half * h2, (half + 1) * h2), 0, BLK), semaphore)

        def stage_keys(kind, node, b):
            d, heads = dims[kind], heads_of[kind]
            slots = kst[:, :] if kind == "rot" else kst[:, (node % 2) * 8 * N:(node % 2) * 8 * N + 8 * N]
            for j, term in enumerate(TERMS[d][1]):
                load(slots[d * j:d * j + d, :].rearrange("p (h n) -> p h n", n=N)[:, :, bass.ds(b * BLK, BLK)],
                     stacked("k", term, d, slice(0, heads), 0, BLK), f"{kind}_k_in")

        splits_k = {"nas": 0, "rot": 0}
        for x in PLAN:
            kind = x.kind
            if isinstance(x, Serial):
                if kind == "rot" and x.jobs[0][0] == "q1":
                    sp.wait_ge(S["cell_turned"], 4)
                    load(w_q[:, 0, :], A["wq_w"], "rot_in")
                    load(w_k[:, 0, :], A["wk_w"], "rot_in")
                    load(w_v[:, 0, :], A["wv_w"], "rot_in")
                    load(w_o[:, 0, :], A["wo_w"], "rot_in")
                    for i, name in enumerate(("wq_b", "wk_b")):
                        load(col[:, RB + 2 * i:RB + 2 * i + 1], A[name].rearrange("(p a) -> p a", a=1), "rot_in")
                        load(col[:, RB + 2 * i + 1:RB + 2 * i + 2], A[name + "_swapped"].rearrange("(p a) -> p a", a=1),
                             "rot_in")
                    load(cos, A["c_cos"], "rot_in")
                    load(sin, A["c_sin"], "rot_in")
                    load(rows[:, 0, :], A["wv_b"].rearrange("(a d) -> a d", a=1).partition_broadcast(P), "rot_rows_in")
                    load(rows[:, 1, :], A["wo_b"].rearrange("(a d) -> a d", a=1).partition_broadcast(P), "rot_rows_in")
                    load(wi, A["wi_T"], "mlp_in")
                    load(wo, A["wo_T"].rearrange("(c p) d -> p c d", p=P), "mlp_in")
                    load(lora_b, A["lora_BT"], "mlp_in")
                    load(gate_a[:, 0:EXPERTS], A["gate_T"], "mlp_in")
                    load(gate_a[:, EXPERTS:GA], A["lora_AT"], "mlp_in")
                    load(gate_bias, A["gate_b"].rearrange("(a d) -> a d", a=1).partition_broadcast(P), "mlp_in")
                    load(rank_row, A["c_rank"].partition_broadcast(P), "mlp_in")
                    load(wo_bias, A["ffn_wo_b"].rearrange("(a d) -> a d", a=1).partition_broadcast(P), "mlp_in")
                    load(col[:, FB:FB + FC], A["wi_b"].rearrange("(c p) -> p c", p=P), "mlp_in",
                         allow_slow_non_contiguous=True)
                    sp.wait_ge(S["pads_ready"], 1)
                split = x.before["split"]
                for name, b in x.jobs:
                    if name == "q2":
                        send_parts("q", split)
                        stage_queries(kind, 0, f"{kind}_qa_in")
                        split += 1
                    if name == "k2":
                        if splits_k[kind] == 0:
                            sp.wait_ge(S[f"{kind}_qa_in"], 16 * n_terms[kind])
                        else:
                            sp.wait_ge(S[f"{kind}_k_in"], 16 * n_terms[kind] * splits_k[kind])
                        send_parts("k", split)
                        stage_keys(kind, 0, b)
                        split += 1
                        splits_k[kind] += 1
                continue

            def emit(b, x=x, kind=kind):
                c, g = x.node, x.body(b)
                nt = 16 * n_terms[kind]
                ready = {n: None if isinstance(b, int) else sp.to_reg(v + 1)
                         for n, v in (("k", x.k_split(b)), ("q", x.q_split(b)))}
                need(sp, S["misc_full"], x.before["job"] + x.n_jobs * (b - x.b0))
                need(sp, S["st_ready"], 16 * x.unit(b))
                if kind == "nas":
                    if x.b0 == 0:
                        if x.next_k:
                            kv_weights(c + 1)
                        load(w_o[:, c % 2, :], A["Wo"][c], "node_weights_in")
                    if x.next_q:
                        node_q_weights(b, x, c, min(c + 1, NODES - 1))
                stage_queries(kind, 1, f"{kind}_qb_in")
                if x.next_k:
                    sp.wait_ge(S["nas_k_in"], nt * (NBLK * (c + 1) + b))
                    send_parts("k", x.k_split(b), ready["k"])
                    stage_keys(kind, c + 1, b)
                if x.next_q:
                    sp.wait_ge(S[f"{kind}_qb_in"], nt * (g + 1))
                    send_parts("q", x.q_split(b), ready["q"])
                    sp.wait_ge(S["st_ready"], 16 * (x.unit(b) + x.heads // 2))
                    stage_queries(kind, 0, f"{kind}_qa_in")

            each_block(sp, x, emit)
            if kind == "nas" and x.last:
                load(t_tmp[:, 0:D], A["ln_g"].rearrange("(a d) -> a d", a=1).partition_broadcast(P), "norm_rows_in")
                load(t_tmp[:, D:2 * D], A["ln_b"].rearrange("(a d) -> a d", a=1).partition_broadcast(P), "norm_rows_in")

        for b in range(NBLK):
            sp.wait_ge(S["out_ready"], b + 1)
            load(out[0].rearrange("(t p) d -> p t d", p=P)[:, QT * b:QT * (b + 1), :],
                 x_res[:, QT * b:QT * (b + 1), :], "out_in")
        sp.wait_ge(S["out_in"], 16 * NBLK)

    @block.gpsimd
    def _(pool):
        pool.memset(zeros[:, :], 0.0).then_inc(S["zeros_ready"], 1)
        pool.wait_ge(S["zeros_ready"], 1)
        pool.memset(kst[64:P, :].bitcast(F32), float(np.array([0x3F803F80], np.uint32).view(np.float32)[0])) \
            .then_inc(S["rows_ready"], 1)
        pool.wait_ge(S["rows_ready"], 1)
        pool.memset(q_loc[64:M_ROW, :].bitcast(F32), 0.0).then_inc(S["rows_ready"], 1)
        pool.wait_ge(S["rows_ready"], 2)

        def split_max(neg, out3, step_sem, done_sem, n, i):
            pool.tensor_tensor(out3[:, i, :, 0], neg[:, i, :], zeros[:, :], ALU.add).then_inc(S[step_sem], 1)
            pool.wait_ge(S[step_sem], 3 * n + 1)
            pool.tensor_tensor(neg_rest[:, i, :], neg[:, i, :], out3[:, i, :, 0], ALU.subtract).then_inc(S[step_sem], 1)
            pool.wait_ge(S[step_sem], 3 * n + 2)
            pool.tensor_tensor(out3[:, i, :, 1], neg_rest[:, i, :], zeros[:, :], ALU.add) \
                .then_inc(S[step_sem], 1)
            pool.wait_ge(S[step_sem], 3 * n + 3)
            pool.tensor_tensor(out3[:, i, :, 2], neg_rest[:, i, :], out3[:, i, :, 1], ALU.subtract) \
                .then_inc(S[done_sem], 1)

        def local_step(n, i):
            pool.wait_ge(S["l_neg"], n + 1)
            need(pool, S["l_rows"], n - 1)
            split_max(neg_max, max_parts, "l_pool", "l_maxparts", n, i)

        for grp in range(L0_HEADS // 4):
            with pool.Fori(0, TILES // 2) as pair:
                t = 2 * pair
                for i in range(2):
                    if grp == 0:
                        pool.wait_ge(S["l_neg"], t + (i + 1))
                        split_max(neg_max, max_parts, "l_pool", "l_maxparts", t + i, i)
                    else:
                        local_step(grp * TILES + i + t, i)

        def attention_step(u, i):
            pool.wait_ge(S["neg_ready"], u + 1)
            split_max(neg_max, max_parts, "pool_step", "maxparts_ready", u, i)

        for x in PLAN:
            if isinstance(x, Serial):
                if x.jobs[-1][0] == "prime":
                    attention_step(x.before["unit"], 0)
                continue

            def emit(b, x=x):
                for h in range(x.heads):
                    if not (x.last and h == x.heads - 1):
                        attention_step(x.unit(b) + h + 1, (h + 1) % 2)

            each_block(pool, x, emit)

    @block.scalar
    def _(act):
        norms = [0]

        def root():
            act.wait_ge(S["var_ready"], norms[0] + 1)
            act.activation(rstd[:, 1, :], rstd[:, 0, :], ACT.Sqrt).then_inc(S["std_ready"], 1)
            norms[0] += 1

        def copy_turned(layer):
            for b in range(NBLK):
                act.wait_ge(S["turned"], NBLK * layer + b + 1)
                act.activation(xT[:, b * BLK:(b + 1) * BLK], ps[:, b, :], ACT.Copy).then_inc(S["turn_copied"], 1)

        root()
        copy_turned(0)

        act.wait_ge(S["masks_made"], 3)

        def local_step(n, i):
            act.wait_ge(S["l_rows"], n + 1)
            need(act, S["l_st"], n - 1)
            act.activation(mask_rows[i][M_ROW:K_ROWS, :], ps[M_ROW:K_ROWS, 2 + i, :], ACT.Copy) \
                .then_inc(S["l_rows_in"], 1)
            act.wait_ge(S["l_st"], n + 1)
            need(act, S["l_pv"], n - 1)
            act.activation(l_probs[i][:, :], ps[:, i, :], ACT.Exp, scale=float(L0_DIM) ** -0.5) \
                .then_inc(S["l_exp"], 1)

        for grp in range(L0_HEADS // 4):
            n0 = grp * TILES
            local_step(n0, 0)
            local_step(n0 + 1, 1)
            with act.Fori(1, TILES // 2) as pair:
                t = 2 * pair
                local_step(n0 + t, 0)
                local_step(n0 + 1 + t, 1)

        root()
        root()
        copy_turned(1)

        def rows_copy(job, slot):
            act.wait_ge(S["misc_full"], job + 1)
            act.activation(qst[M_ROW:K_ROWS, slot * BLK:(slot + 1) * BLK], misc[M_ROW:K_ROWS, :], ACT.Copy) \
                .then_inc(S["misc_free"], 1)

        def turn_copy(job):
            act.wait_ge(S["misc_full"], job + 1)
            act.activation(o_chan, misc, ACT.Copy).then_inc(S["misc_free"], 1)

        def high_part(job, split):
            act.wait_ge(S["misc_full"], job + 1)
            need(act, S["parts_sent"], 16 * split)
            act.activation(parts[:, 0, :], misc, ACT.Copy).then_inc(S["high_ready"], 1)

        def edge(e, job):
            act.wait_ge(S["misc_full"], job + 1)
            act.activation(t_tmp[:, :], misc, ACT.Identity, bias=col[:, EB + e:EB + e + 1],
                           scale=col[:, EW + 3 * (e // 2) + 1 + e % 2:EW + 3 * (e // 2) + 2 + e % 2]) \
                .then_inc(S["misc_free"], 1)

        def cell_values(par, b, job):
            act.wait_ge(S["misc_full"], job + 1)
            size = NAS_HEADS * VW
            dst = vst[:, bass.ds(par * TILES * size + b * (QT * size), QT * size)] \
                .rearrange("p (t h w) -> p t h w", t=QT, w=VW)[:, :, :, 0:NAS_DIM]
            act.activation(dst, misc.rearrange("p (t h d) -> p t h d", t=QT, d=NAS_DIM), ACT.Copy) \
                .then_inc(S["misc_free"], 1)

        def acc_copy(u, i):
            act.wait_ge(S["pv_done"], 4 * u + 4)
            act.activation(o_part[:, i, :], acc, ACT.Copy).then_inc(S["acc_copied"], 1)

        for x in PLAN:
            kind = x.kind
            if isinstance(x, Serial):
                job, split = x.before["job"], x.before["split"]
                for name, b in x.jobs:
                    if name == "prime":
                        rows_copy(job, 0)
                    if name == "turn":
                        turn_copy(job)
                    if name in ("q2", "k2"):
                        if kind == "nas":
                            high_part(job, split)
                        split += 1
                    if kind == "nas" and name in ("k1", "v1"):
                        if x.node == 0 and (name, b) == ("k1", 0):
                            act.wait_ge(S["edges_ready"], 2 * NODES)
                        edge(2 * x.node + (name == "v1"), job)
                    if kind == "nas" and name == "v2":
                        cell_values(x.node % 2, b, job)
                    job += 1
                if kind == "nas" and x.jobs[0][0] == "fold" and x.node == NODES - 1:
                    for b in range(NBLK):
                        act.wait_ge(S["cell_turned"], b + 1)
                        act.activation(tok[:, QT * b:QT * (b + 1), :].rearrange("p t d -> p (t d)"), ps[:, b, :],
                                       ACT.Copy).then_inc(S["cell_copied"], 1)
                    for _ in range(3):
                        root()
                    copy_turned(2)
                continue

            def emit(b, x=x, kind=kind):
                for h in range(x.heads):
                    u = x.unit(b) + h
                    for s in range(8):
                        for i in (2 * s, 2 * s + 1):
                            act.wait_ge(S["st_ready"], 16 * u + i + 1)
                            if i % 4 == 0:
                                need(act, S["pv_done"], 4 * u + i // 4 - 1)
                            act.activation(probs[:, i % 8, :], ps[:, BANK[i], :], ACT.Exp,
                                           scale=float(dims[kind]) ** -0.5).then_inc(S["exp_done"], 1)
                        if s == 1 and (h > 0 or x.with_out):
                            acc_copy(u - 1, (h - 1) % 2)
                        name = x.jobs.get((h, s))
                        if name == "rows":
                            rows_copy(x.job(b, h, s), (h + 1) % x.heads)
                        if name == "turn":
                            turn_copy(x.job(b, h, s))
                        if name == "q2" and kind == "nas":
                            high_part(x.job(b, h, s), x.q_split(b))
                        if name == "k2":
                            high_part(x.job(b, h, s), x.k_split(b))
                        if name in ("k1", "v1"):
                            edge(2 * (x.node + 1) + (name == "v1"), x.job(b, h, s))
                        if name == "v2":
                            cell_values((x.node + 1) % 2, b, x.job(b, h, s))

            each_block(act, x, emit)
            if not x.goes_on:
                acc_copy(x.unit(x.b1) - 1, (x.heads - 1) % 2)

        root()
        root()
        copy_turned(3)

        for b in range(NBLK):
            act.wait_ge(S["low_turned"], b + 1)
            act.activation(low_T[:, b * BLK:(b + 1) * BLK], ps[0:EXPERTS * RANK, 2 + b, :], ACT.Copy) \
                .then_inc(S["low_copied"], 1)
        act.wait_ge(S["mlp_in"], 16 * 9)
        for b in range(NBLK):
            for c in range(FC):
                i = FC * b + c
                act.wait_ge(S["hid_full"], i + 1)
                need(act, S["mlp_full"], b - 1)
                act.activation(hid[:, b % 2, c, :], ps[:, i % 2, :], ACT.Relu, bias=col[:, FB + c:FB + c + 1]) \
                    .then_inc(S["hid_free"], 1)
        root()

    @block.tensor
    def _(pe):
        def turn_normed(layer):
            for b in range(NBLK):
                pe.wait_ge(S["normed"], NBLK * layer + b + 1)
                for t in range(QT):
                    last = pe.transpose(ps[:, b, t * P:(t + 1) * P], normed_x[:, QT * b + t, :], ident[:, :])
                last.then_inc(S["turned"], 1)

        pe.wait_ge(S["const_in"], 16)
        turn_normed(0)

        pe.wait_ge(S["w0_in"], 16 * 6)
        for n in range(3 * NBLK):
            bank = ps[:, n % 4, :]
            pe.wait_ge(S["turn_copied"], NBLK if n < 4 else NBLK)
            need(pe, S["l_free"], n - 3)
            if n < 2 * NBLK:
                w, b = (w_k, n) if n < NBLK else (w_q, n - NBLK)
                pe.matmul(bank, w[:, 0, :], xT[:, b * BLK:(b + 1) * BLK], start=True, stop=True) \
                    .then_inc(S["l_full"], 1)
            else:
                for t in range(QT):
                    j = QT * (n - 2 * NBLK) + t
                    last = pe.matmul(bank[:, t * P:(t + 1) * P], xT[:, j * P:(j + 1) * P], w_v[:, 0, :],
                                     start=True, stop=True)
                last.then_inc(S["l_full"], 1)

        pe.wait_ge(S["consts_made"], 2)
        pe.wait_ge(S["masks_made"], 3)
        pe.wait_ge(S["l_free"], 3 * NBLK)
        pe.wait_ge(S["l_k_in"], 16 * len(TERMS[L0_DIM][0]))
        pe.wait_ge(S["l_q_in"], 16 * len(TERMS[L0_DIM][0]))
        pe.wait_ge(S["rows_ready"], 2)
        L_ROWS = M_ROW

        def local_maxes(n, t, grp, i):
            need(pe, S["l_neg"], n - 1)
            pe.matmul(ps[:, L_MAXES + i, :], pick_b[:, :], mask_only, start=True, stop=False, skip_group_check=True)
            for h in range(4):
                at = bass.ds((4 * grp + h) * N + t * P, P)
                last = pe.matmul(ps[:, L_MAXES + i, h * P:(h + 1) * P], q_loc[0:L_ROWS, at], kst[0:L_ROWS, at],
                                 start=False, stop=(h == 3), skip_group_check=True)
            last.then_inc(S["l_scores"], 1)

        def local_rows(n, i):
            pe.wait_ge(S["l_maxparts"], n + 1)
            need(pe, S["l_rows_in"], n - 1)
            for h in range(4):
                last = pe.matmul(ps[M_ROW:K_ROWS, 2 + i, h * P:(h + 1) * P], max_parts[:, i, h, :], ident_b[:, :],
                                 start=True, stop=True)
            last.then_inc(S["l_rows"], 1)

        def local_scores(n, t, grp, i):
            pe.wait_ge(S["l_rows_in"], n + 1)
            need(pe, S["l_exp"], n - 1)
            pe.matmul(ps[:, i, :], pick_b[:, :], mask_rows[i], start=True, stop=False, skip_group_check=True)
            for h in range(4):
                at = bass.ds((4 * grp + h) * N + t * P, P)
                last = pe.matmul(ps[:, i, h * P:(h + 1) * P], kst[0:L_ROWS, at], q_loc[0:L_ROWS, at],
                                 start=False, stop=(h == 3), skip_group_check=True)
            last.then_inc(S["l_st"], 1)

        def local_values(n, i):
            pe.wait_ge(S["l_exp"], n + 1)
            pe.wait_ge(S["l_vnow"], n + 1)
            need(pe, S["l_acc"], n - 1)
            for h in range(4):
                last = pe.matmul(ps[VW * h:VW * (h + 1), ACC + i, 0:P], v_now[i][:, h, :],
                                 l_probs[i][:, h * P:(h + 1) * P], start=True, stop=True)
            last.then_inc(S["l_pv"], 1)

        for grp in range(L0_HEADS // 4):
            n0 = grp * TILES

            def step(t, i, grp=grp, n0=n0, first=False, last=False):
                if not first or t >= 2:
                    local_rows(n0 + t - 2, i)
                if not last:
                    local_maxes(n0 + t, t, grp, i)
                if not first or t >= 3:
                    local_values(n0 + t - 3, 1 - i)
                if not (first and t < 2):
                    local_scores(n0 + t - 2, t - 2, grp, i)

            peeled = 6 if grp == 0 else 4
            for t in range(peeled):
                step(t, t % 2, first=True)
            with pe.Fori(peeled // 2, TILES // 2) as pair:
                for i in range(2):
                    step(2 * pair + i, i)
            for t in (TILES, TILES + 1):
                step(t, t % 2, last=True)
            local_values(n0 + TILES - 1, 1)
            pe.wait_ge(S["l_acc"], n0 + TILES)
            strided = ob[:, :].rearrange("p (b j) -> p j b", j=L0_SPAN)
            for j in range(L0_SPAN):
                if j % 4 == 0:
                    need(pe, S["l_normed"], 4 * (grp - 1) + j // 4 + 1)
                last = pe.transpose(ps[:, j // 4, (j % 4) * P:(j % 4 + 1) * P], strided[:, j, :], ident[:, :])
                if j % 4 == 3:
                    last.then_inc(S["l_turned"], 1)
            pe.wait_ge(S["l_normed"], 4 * (grp + 1))

        turn_normed(1)

        def start_job(job):
            need(pe, S["misc_free"], job)

        def fold(u, i, job):
            pe.wait_ge(S["acc_copied"], u + 1)
            start_job(job)
            for t in range(QT):
                last = pe.transpose(misc[:, t * P:(t + 1) * P], o_part[:, i, t * P:(t + 1) * P], ident[:, :])
            last.then_inc(S["misc_full"], 1)

        def turn(units, job):
            pe.wait_ge(S["heads_normed"], units)
            start_job(job)
            for t in range(QT):
                last = pe.transpose(misc[:, t * P:(t + 1) * P], o_tok[:, t, :], ident[:, :])
            last.then_inc(S["misc_full"], 1)

        def project(w, rhs, job):
            start_job(job)
            pe.matmul(misc, w, rhs, start=True, stop=True).then_inc(S["misc_full"], 1)

        def project_tiles(lhs_tiles, w, job):
            start_job(job)
            for t in range(QT):
                last = pe.matmul(misc[:, t * P:(t + 1) * P], lhs_tiles[:, t * P:(t + 1) * P], w, start=True, stop=True)
            last.then_inc(S["misc_full"], 1)

        def out_job(kind, node, job):
            if kind == "nas":
                pe.wait_ge(S["node_weights_in"], node_weights_count(node))
                project(w_o[:, node % 2, :], o_chan, job)
            else:
                project_tiles(o_chan, w_o[:, 0, :], job)

        def rows_job(u, i, job):
            pe.wait_ge(S["maxparts_ready"], u + 1)
            start_job(job)
            for t in range(QT):
                last = pe.matmul(misc[M_ROW:K_ROWS, t * P:(t + 1) * P], max_parts[:, i, t, :], ident_b[:, :],
                                 start=True, stop=True)
            last.then_inc(S["misc_full"], 1)

        def max_tile(u, i, slot, k_base):
            need(pe, S["tile_done"], 16 * u + i - TAKEN[i] + 1)
            q0 = slot * BLK + (i // 4) * P
            at = k_base + (i % 4) * BLK
            keys = kst[0:M_ROW, at:at + BLK] if isinstance(at, int) else kst[0:M_ROW, bass.ds(at, BLK)]
            pe.matmul(ps[:, MAXES + BANK[i], :], qst[0:M_ROW, q0:q0 + P], keys, start=True, stop=True) \
                .then_inc(S["tile_ready"], 1)

        for x in PLAN:
            kind = x.kind
            if isinstance(x, Serial):
                if kind == "rot" and x.jobs[0][0] == "q1":
                    turn_normed(2)
                    pe.wait_ge(S["turn_copied"], NBLK * 3)
                    pe.wait_ge(S["rot_in"], 16 * 8)
                    pe.wait_ge(S["rot_swapped"], 2)
                if kind == "nas" and x.jobs[0][0] == "q1":
                    pe.wait_ge(S["turn_copied"], NBLK * 2)
                    pe.wait_ge(S["q_weights_in"], 64)
                    pe.wait_ge(S["node_weights_in"], 64)
                job = x.before["job"]
                u0 = x.before["unit"]
                for name, b in x.jobs:
                    if name == "fold":
                        fold(u0 - 1, 1, job)
                    if name == "turn":
                        turn(u0, job)
                    if name == "out":
                        out_job(kind, x.node, job)
                    if name in ("q1", "k1") and kind == "rot":
                        project((w_q if name == "q1" else w_k)[:, 0, :], xT[:, b * BLK:(b + 1) * BLK], job)
                    if name in ("q2", "k2") and kind == "rot":
                        project((w_q if name == "q2" else w_k)[:, 1, :], xT[:, b * BLK:(b + 1) * BLK], job)
                    if name == "v2" and kind == "rot":
                        project_tiles(xT[:, b * BLK:(b + 1) * BLK], w_v[:, 0, :], job)
                    if kind == "nas":
                        plan = NODE[x.node]
                        if name == "q1":
                            project(w_q[:, 0, :], xT[:, 0:BLK], job)
                        if name == "q2":
                            at = node_col(0)
                            project(w_q[:, 1, :], nodes[:, at:at + BLK], job)
                        if name == "k1":
                            at = node_col(plan["k"], b)
                            project(w_k[:, 0, :], nodes[:, at:at + BLK], job)
                        if name == "k2":
                            project(w_k[:, 1, :], t_tmp[:, :], job)
                        if name == "v1":
                            at = node_col(plan["v"], b)
                            project(w_v[:, 0, :], nodes[:, at:at + BLK], job)
                        if name == "v2":
                            project_tiles(t_tmp[:, :], w_v[:, 1, :], job)
                    if name == "prime":
                        pe.wait_ge(S["rows_ready"], 1)
                        pe.wait_ge(S[f"{kind}_qa_in"], 16 * n_terms[kind])
                        pe.wait_ge(S[f"{kind}_k_in"], 16 * n_terms[kind] * NBLK)
                        for i in range(16):
                            max_tile(u0, i, 0, 0)
                        for i in range(8):
                            max_tile(u0 + 1, i, 1, N)
                        rows_job(u0, 0, job)
                    job += 1
                if kind == "nas" and x.jobs[0][0] == "fold" and x.node == NODES - 1:
                    pe.wait_ge(S["misc_free"], job)
                    for b in range(NBLK):
                        for t in range(QT):
                            last = pe.transpose(ps[:, b, t * P:(t + 1) * P], xT[:, (QT * b + t) * P:(QT * b + t + 1) * P],
                                                ident[:, :])
                        last.then_inc(S["cell_turned"], 1)
                continue

            def pv_quad(u, h, quad, c=x.node, kind=kind):
                pe.wait_ge(S["exp_done"], 16 * u + 4 * quad + 4)
                if quad == 0:
                    need(pe, S["acc_copied"], u)
                for k in range(4):
                    t = 4 * quad + k
                    value = v_nas[:, c % 2, t, h, :] if kind == "nas" else v_16[:, t, h, :]
                    last = pe.matmul(acc[VW * k:VW * (k + 1), :], value, probs[:, t % 8, :],
                                     start=(quad == 0), stop=(quad == 3), skip_group_check=True)
                last.then_inc(S["pv_done"], 1)

            def emit(b, x=x, kind=kind):
                c, heads, u0 = x.node, x.heads, x.unit(b)
                nt = 16 * n_terms[kind]
                par = (c % 2) * 8 if kind == "nas" else 0
                def score_tile(u, h, slot, i):
                    need(pe, S["exp_done"], 16 * u + i - TAKEN[i] + 1)
                    key0 = slot * N + i * P
                    pe.matmul(ps[:, BANK[i], :], kst[0:K_ROWS, key0:key0 + P],
                              qst[0:K_ROWS, h * BLK:(h + 1) * BLK], start=True, stop=True).then_inc(S["st_ready"], 1)

                for h in range(heads):
                    u = u0 + h
                    slot = par + h
                    for s in range(8):
                        if s == 0:
                            pe.wait_ge(S["misc_free"], x.job(b, h - 1, ROWS_STEP) + 1 if h
                                       else x.jobs_so_far(b, 0, 0) - x.late_before)
                        if s == 3 and h == 0:
                            pe.wait_ge(S["misc_free"], x.jobs_so_far(b, 0, 0))
                        if s == 1 and h:
                            pv_quad(u - 1, h - 1, 3)
                        if s == 1 and h == 0 and x.with_out:
                            pv_quad(u - 1, heads - 1, 3, c=c if x.b0 else c - 1)
                        if s % 2 == 1 and s > 1:
                            pv_quad(u, h, s // 2 - 1)
                        score_tile(u, h, slot, 2 * s)
                        ahead, first = maxima_of(s)
                        v, hv = u + ahead, h + ahead
                        needed = not (x.last and hv >= heads)
                        if needed:
                            wraps = hv >= heads
                            hv %= heads
                            if first == 0 and hv == 0 and wraps:
                                pe.wait_ge(S[f"{kind}_qa_in"], nt * (x.body(b) + 2))
                                if x.turns_over():
                                    pe.wait_ge(S["nas_k_in"], nt * (NBLK * (c + 1) + b + 1))
                            if first == 0 and hv == heads // 2 and not wraps:
                                pe.wait_ge(S[f"{kind}_qb_in"], nt * (x.body(b) + 1))
                            base = (x.pick(b, par, 8 - par) if wraps else par) + hv
                            max_tile(v, first, hv, base * N)
                        score_tile(u, h, slot, 2 * s + 1)
                        if needed:
                            max_tile(v, first + 1, hv, base * N)
                        name = x.jobs.get((h, s))
                        if name:
                            job = x.job(b, h, s)
                        if name == "fold":
                            if h:
                                fold(u - 1, (h - 1) % 2, job)
                            else:
                                fold(u - 1, 1, job)
                        if name == "turn":
                            turn(u0, job)
                        if name == "out":
                            out_job(kind, x.out_of(b)[0], job)
                        if name == "rows":
                            rows_job(u + 1, (h + 1) % 2, job)
                        if name in ("q1", "q2") and kind == "rot":
                            project(w_q[:, 0 if name == "q1" else 1, :], xT[:, bass.ds((b + 1) * BLK, BLK)], job)
                        if kind == "nas":
                            if name == "q1":
                                pe.wait_ge(S["q_weights_in"], 64 * (x.body(b) + 2))
                                at = in_nodes(x.pick(b, node_col(c - 1), node_col(c) - NBLK * BLK) + (b + 1) * BLK)
                                project(w_q[:, 0, :], nodes[:, bass.ds(at, BLK)], job)
                            if name == "q2":
                                at = next_block(x, b)
                                project(w_q[:, 1, :], nodes[:, bass.ds(at, BLK)], job)
                            if name == "k1":
                                pe.wait_ge(S["node_weights_in"], 64 + 80 * (c + 1))
                                project(w_k[:, 0, :], nodes[:, bass.ds(node_col(NODE[c + 1]["k"]) + b * BLK, BLK)], job)
                            if name == "k2":
                                project(w_k[:, 1, :], t_tmp[:, :], job)
                            if name == "v1":
                                project(w_v[:, 0, :], nodes[:, bass.ds(node_col(NODE[c + 1]["v"]) + b * BLK, BLK)], job)
                            if name == "v2":
                                project_tiles(t_tmp[:, :], w_v[:, 1, :], job)

            each_block(pe, x, emit)
            if not x.goes_on:
                pv_quad(x.unit(x.b1) - 1, x.heads - 1, 3)

        turn_normed(3)
        pe.wait_ge(S["turn_copied"], NBLK * 4)
        pe.wait_ge(S["mlp_in"], 16 * 9)
        for k in range(2):
            for t in range(8):
                j = 8 * k + t
                last = pe.matmul(ps[:, k, t * GA:(t + 1) * GA], xT[:, j * P:(j + 1) * P], gate_a, start=True, stop=True)
            last.then_inc(S["gates_ready"], 1)
        pe.wait_ge(S["gates_copied"], 2)
        for b in range(NBLK):
            for t in range(QT):
                last = pe.transpose(ps[0:EXPERTS * RANK, 2 + b, t * P:(t + 1) * P], low[:, QT * b + t, :], ident[:, :])
            last.then_inc(S["low_turned"], 1)

        def mlp_out(b):
            pe.wait_ge(S["hid_free"], FC * (b + 1))
            need(pe, S["mlp_free"], b - 1)
            for t in range(QT):
                for c in range(FC):
                    last = pe.matmul(ps[:, 6 + b % 2, t * P:(t + 1) * P], hid[:, b % 2, c, t * P:(t + 1) * P], wo[:, c, :],
                                     start=(c == 0), stop=(c == FC - 1))
            last.then_inc(S["mlp_full"], 1)

        for b in range(NBLK):
            pe.wait_ge(S["low_copied"], b + 1)
            for c in range(FC):
                i = FC * b + c
                need(pe, S["hid_free"], i - 1)
                pe.matmul(ps[:, i % 2, :], wi[:, c * P:(c + 1) * P], xT[:, b * BLK:(b + 1) * BLK], start=True, stop=False)
                pe.matmul(ps[:, i % 2, :], lora_b[:, c * P:(c + 1) * P], low_T[:, b * BLK:(b + 1) * BLK],
                          start=False, stop=True).then_inc(S["hid_full"], 1)
            if b:
                mlp_out(b - 1)
        mlp_out(NBLK - 1)

    @block.vector
    def _(dve):
        steps = [0]

        def link(ins):
            steps[0] += 1
            ins.then_inc(S["dve_step"], 1)
            dve.wait_ge(S["dve_step"], steps[0])

        norms = [0]

        def statistics(src, eps):
            for t in range(TILES):
                last = dve.bn_stats(stats[:, t, :], src[:, t, :])
            link(last)
            for t in range(TILES):
                last = dve.bn_aggr(mean_var[:, t, :], stats[:, t, :])
            link(last)
            dve.tensor_scalar(rstd[:, 0, :], mean_var[:, :, 1], eps, None, ALU.add).then_inc(S["var_ready"], 1)
            norms[0] += 1
            dve.wait_ge(S["std_ready"], norms[0])
            link(dve.reciprocal(rstd[:, 2, :], rstd[:, 1, :]))
            link(dve.tensor_tensor(rstd[:, 1, :], rstd[:, 2, :], rstd[:, 2, :], ALU.mult))
            link(dve.tensor_tensor(rstd[:, 1, :], rstd[:, 1, :], rstd[:, 0, :], ALU.mult))
            link(dve.tensor_scalar(rstd[:, 1, :], rstd[:, 1, :], -0.5, 1.5, ALU.mult, ALU.add))
            link(dve.tensor_tensor(rstd[:, 2, :], rstd[:, 2, :], rstd[:, 1, :], ALU.mult))

        def center(dst, src, t):
            return dve.tensor_scalar(dst[:, t, :], src[:, t, :], mean_var[:, t, 0:1], rstd[:, 2, t:t + 1],
                                     ALU.subtract, ALU.mult)

        def norm_for_turn():
            statistics(x_res, 1e-5)
            for b in range(NBLK):
                for t in range(QT * b, QT * (b + 1)):
                    last = center(normed_x, x_res, t)
                last.then_inc(S["normed"], 1)

        def norm_in_place(y, eps):
            statistics(y, eps)
            for t in range(TILES):
                last = center(y, y, t)
            link(last)

        def add_to_stream(y):
            link(dve.tensor_tensor(x_res[:, :, :], x_res[:, :, :], y[:, :, :], ALU.add))

        def spread(row, n):
            return row.unsqueeze(1).to_broadcast([P, n, row.shape[1]])

        link(dve.memset(vst[:, :], 0.0))
        link(dve.memset(v_cols[:, :, L0_DIM:L0_DIM + 1], 1.0))
        dve.wait_ge(S["const_in"], 16)
        dve.tensor_copy(ident_b[:, :], ident[:, :]).then_inc(S["consts_made"], 1)
        dve.wait_ge(S["small_in"], 16)
        dve.tensor_copy(pick_b[:, :], t_tmp[:, 0:P]).then_inc(S["consts_made"], 1)
        dve.wait_ge(S["x_in"], 16)
        norm_for_turn()

        dve.wait_ge(S["w0_in"], 16 * 6)
        dve.wait_ge(S["masks_in"], 16)
        for dst in (mask_rows[0], mask_rows[1], mask_only):
            dve.tensor_copy(dst, t_tmp[:, :]).then_inc(S["masks_made"], 1)
        dve.wait_ge(S["masks_made"], 3)
        dve.wait_ge(S["turned"], NBLK)
        for n in range(2 * NBLK):
            dve.wait_ge(S["l_full"], n + 1)
            need(dve, l_parts_sent[n % 2], 16 * (n // 2))
            need(dve, S["l_parts_ready"], n)
            i = n % 2
            bias = col[:, LB + 1:LB + 2] if n < NBLK else col[:, LB:LB + 1]
            dve.tensor_scalar(rest[:, :], ps[:, n % 4, :], bias, None, ALU.add).then_inc(S["l_free"], 1)
            dve.wait_ge(S["l_free"], n + 1)
            link(dve.tensor_copy(parts2[:, i, 0, :], rest[:, :]))
            link(dve.tensor_tensor(rest[:, :], rest[:, :], parts2[:, i, 0, :], ALU.subtract))
            link(dve.tensor_copy(parts2[:, i, 1, :], rest[:, :]))
            dve.tensor_tensor(parts2[:, i, 2, :], rest[:, :], parts2[:, i, 1, :], ALU.subtract) \
                .then_inc(S["l_parts_ready"], 1)
        for b in range(NBLK):
            n = 2 * NBLK + b
            dve.wait_ge(S["l_full"], n + 1)
            dve.tensor_tensor(v_16[:, QT * b:QT * (b + 1), :, 0:L0_DIM],
                              ps[:, n % 4, :].rearrange("p (t h d) -> p t h d", t=QT, d=L0_DIM),
                              w_o[:, 0, :].rearrange("p (h d) -> p h d", d=L0_DIM).unsqueeze(1)
                              .to_broadcast([P, QT, L0_HEADS, L0_DIM]), ALU.add).then_inc(S["l_free"], 1)
        dve.wait_ge(S["l_free"], 3 * NBLK)
        for sent in l_parts_sent:
            dve.wait_ge(sent, 16 * NBLK)
        dve.wait_ge(S["l_parts_ready"], 2 * NBLK)

        def local_max(n, i):
            dve.wait_ge(S["l_scores"], n + 1)
            need(dve, S["l_maxparts"], n - 1)
            dve.tensor_reduce(neg_max[:, i, :], ps[:, L_MAXES + i, :].rearrange("p (h k) -> p h k", h=4), AX.X, ALU.max,
                              negate=True).then_inc(S["l_neg"], 1)

        def local_vnow(n, t, grp, i):
            need(dve, S["l_pv"], n - 1)
            if isinstance(t, int):
                src = v_16[:, t, 4 * grp:4 * grp + 4, :].rearrange("p h w -> p (h w)")
            else:
                src = vst[:, bass.ds(t * (16 * VW) + 4 * grp * VW, 4 * VW)]
            dve.tensor_scalar((w_q, w_k)[i][:, 0, :], src, 1.0, None, ALU.mult).then_inc(S["l_vnow"], 1)

        def local_acc(n, t, i):
            dve.wait_ge(S["l_pv"], n + 1)
            dve.tensor_scalar(ob[:, bass.ds(t * P, P)], ps[:, ACC + i, 0:P], 1.0, None, ALU.mult) \
                .then_inc(S["l_acc"], 1)

        for grp in range(L0_HEADS // 4):
            n0 = grp * TILES
            local_max(n0, 0)
            local_max(n0 + 1, 1)
            local_max(n0 + 2, 0)
            local_vnow(n0, 0, grp, 0)
            local_max(n0 + 3, 1)
            local_acc(n0, 0, 0)
            local_vnow(n0 + 1, 1, grp, 1)
            with dve.Fori(2, TILES // 2) as pair:
                t = 2 * pair
                for i in range(2):
                    local_max(n0 + i + t, i)
                    local_acc(n0 + i - 3 + t, t + (i - 3), 1 - i)
                    local_vnow(n0 + i - 2 + t, t + (i - 2), grp, i)
            local_acc(n0 + TILES - 3, TILES - 3, 1)
            local_vnow(n0 + TILES - 2, TILES - 2, grp, 0)
            local_acc(n0 + TILES - 2, TILES - 2, 0)
            local_vnow(n0 + TILES - 1, TILES - 1, grp, 1)
            local_acc(n0 + TILES - 1, TILES - 1, 1)
            for k in range(4):
                dve.wait_ge(S["l_turned"], 4 * grp + k + 1)
                view = ps[:, k, :].rearrange("p (j h w) -> p j h w", j=4, w=VW)
                r = recip[:, :].rearrange("p (j h) -> p j h", j=4)
                link(dve.reciprocal(r, view[:, :, :, L0_DIM]))
                dst = att[:, 4 * grp:4 * grp + 4, 4 * k * L0_DIM:4 * (k + 1) * L0_DIM] \
                    .rearrange("p h (j d) -> p j h d", d=L0_DIM)
                dve.tensor_tensor(dst, view[:, :, :, 0:L0_DIM], r.unsqueeze(3).to_broadcast([P, 4, 4, L0_DIM]),
                                  ALU.mult).then_inc(S["l_normed"], 1)
                dve.wait_ge(S["l_normed"], 4 * grp + k + 1)

        norm_in_place(att, 1e-5)
        add_to_stream(att)
        norm_for_turn()
        link(dve.memset(v_cols[:, :, NAS_DIM:NAS_DIM + 1], 1.0))
        dve.wait_ge(S["nas_cols_in"], 48)
        dve.wait_ge(S["q_weights_in"], 64)
        for c in range(NODES):
            for i, e in enumerate(("ek", "ev")):
                at = EB + 2 * c + i
                dve.tensor_tensor(col[:, at:at + 1], col[:, BE + NODE[c][e]:BE + NODE[c][e] + 1],
                                  col[:, EW + 3 * c + 1 + i:EW + 3 * c + 2 + i], ALU.mult) \
                    .then_inc(S["edges_ready"], 1)

        def max_tile(u, i, par):
            dve.wait_ge(S["tile_ready"], 16 * u + i + 1)
            dve.tensor_reduce(row_max[:, par, i:i + 1], ps[:, MAXES + BANK[i], :], AX.X, ALU.max) \
                .then_inc(S["tile_done"], 1)
            if i == 15:
                dve.wait_ge(S["tile_done"], 16 * u + 16)
                need(dve, S["maxparts_ready"], u - 1)
                dve.tensor_reduce(neg_max[:, par, :], row_max[:, par, :].rearrange("p (t k) -> p t k", k=4), AX.X,
                                  ALU.max, negate=True).then_inc(S["neg_ready"], 1)

        def fold_sum(kind, u, job):
            d = dims[kind]
            dve.wait_ge(S["misc_full"], job + 1)
            need(dve, S["heads_normed"], u)
            dve.tensor_reduce(sums[:, :, 0:d + 1], misc.rearrange("p (t g w) -> p t w g", t=QT, w=VW)[:, :, 0:d + 1, :],
                              AX.X, ALU.add).then_inc(S["misc_free"], 1)

        def fold_recip(kind, u, job):
            dve.wait_ge(S["misc_free"], job + 1)
            dve.reciprocal(recip[:, 0:QT], sums[:, :, dims[kind]]).then_inc(S["heads_recip"], 1)

        def fold_scale(kind, u, h):
            d = dims[kind]
            dve.wait_ge(S["heads_recip"], u + 1)
            dve.tensor_tensor(o_tok[:, :, h * d:(h + 1) * d], sums[:, :, 0:d],
                              recip[:, 0:QT].unsqueeze(2).to_broadcast([P, QT, d]), ALU.mult) \
                .then_inc(S["heads_normed"], 1)

        def out_job(kind, node, at, b, job):
            dve.wait_ge(S["misc_full"], job + 1)
            if kind == "nas":
                dst = nodes[:, bass.ds(at, BLK)]
                dve.scalar_tensor_tensor(dst, misc, col[:, AW + node:AW + node + 1], dst, ALU.mult, ALU.add) \
                    .then_inc(S["misc_free"], 1)
            else:
                dst = big[:, bass.ds(N + b * BLK, BLK)].rearrange("p (t d) -> p t d", d=D)
                dve.tensor_tensor(dst, misc.rearrange("p (t d) -> p t d", d=D), spread(rows[:, 1, :], QT), ALU.add) \
                    .then_inc(S["misc_free"], 1)

        def edge(dst, be, ew, job):
            dve.wait_ge(S["misc_full"], job + 1)
            dve.tensor_scalar(dst, misc, be, ew, ALU.add, ALU.mult).then_inc(S["misc_free"], 1)

        def rest_part(job, split):
            dve.wait_ge(S["high_ready"], split + 1)
            dve.tensor_tensor(rest[:, :], misc, parts[:, 0, :], ALU.subtract).then_inc(S["misc_free"], 1)

        def middle_part(job, split):
            dve.wait_ge(S["misc_free"], job + 1)
            dve.tensor_copy(parts[:, 1, :], rest[:, :]).then_inc(S["mid_ready"], 1)

        def low_part(split):
            dve.wait_ge(S["mid_ready"], split + 1)
            dve.tensor_tensor(parts[:, 2, :], rest[:, :], parts[:, 1, :], ALU.subtract).then_inc(S["parts_ready"], 1)

        def rotate_a(blk, bias, job):
            dve.wait_ge(S["misc_full"], job + 1)
            dve.scalar_tensor_tensor(rot_a, misc, bias, cos[:, bass.ds(blk * BLK, BLK)], ALU.add, ALU.mult) \
                .then_inc(S["misc_free"], 1)

        def rotate_b(blk, bias, job, split):
            k = split - rot_split0
            dve.wait_ge(S["misc_full"], job + 1)
            dve.scalar_tensor_tensor(rot_b, misc, bias, sin[:, bass.ds(blk * BLK, BLK)], ALU.add, ALU.mult) \
                .then_inc(S["misc_free"], 1)
            dve.wait_ge(S["misc_free"], job + 1)
            dve.tensor_tensor(rot_sum, rot_a, rot_b, ALU.add).then_inc(S["rot_sum_done"], 1)
            dve.wait_ge(S["rot_sum_done"], k + 1)
            need(dve, S["parts_sent"], 16 * split)
            dve.tensor_copy(parts[:, 0, :], rot_sum).then_inc(S["rot_high_ready"], 1)
            dve.wait_ge(S["rot_high_ready"], k + 1)
            dve.tensor_tensor(rest[:, :], rot_sum, parts[:, 0, :], ALU.subtract).then_inc(S["rest_ready"], 1)
            dve.wait_ge(S["rest_ready"], k + 1)
            dve.tensor_copy(parts[:, 1, :], rest[:, :]).then_inc(S["mid_ready"], 1)
            dve.wait_ge(S["mid_ready"], split + 1)
            dve.tensor_tensor(parts[:, 2, :], rest[:, :], parts[:, 1, :], ALU.subtract).then_inc(S["parts_ready"], 1)

        for x in PLAN:
            kind = x.kind
            if isinstance(x, Serial):
                if kind == "rot" and x.jobs[0][0] == "q1":
                    dve.wait_ge(S["rot_in"], 16 * 8)
                    dve.wait_ge(S["rot_rows_in"], 32)
                    for w in (w_q, w_k):
                        a = w[:, 0, :].rearrange("p (h a r) -> p h a r", a=2, r=ROT_DIM // 2)
                        z = w[:, 1, :].rearrange("p (h a r) -> p h a r", a=2, r=ROT_DIM // 2)
                        for i in range(2):
                            last = dve.tensor_copy(z[:, :, i, :], a[:, :, 1 - i, :])
                        last.then_inc(S["rot_swapped"], 1)
                    dve.memset(qst[64:M_ROW, :].bitcast(F32), 0.0).then_inc(S["pads_ready"], 1)
                    link(dve.memset(v_cols[:, :, ROT_DIM:NAS_DIM + 1], 0.0))
                    link(dve.memset(v_cols[:, :, ROT_DIM:ROT_DIM + 1], 1.0))
                job, split, u0 = x.before["job"], x.before["split"], x.before["unit"]
                for name, b in x.jobs:
                    c = x.node
                    if name == "fold":
                        fold_sum(kind, u0 - 1, job)
                        fold_recip(kind, u0 - 1, job)
                        fold_scale(kind, u0 - 1, heads_of[kind] - 1)
                    if name == "out":
                        out_job(kind, c, node_col(c, b), b, job)
                    if kind == "nas":
                        if name == "q1":
                            at = node_col(0)
                            edge(nodes[:, at:at + BLK], col[:, QBE:QBE + 1], col[:, QEW:QEW + 1], job)
                        if name in ("q2", "k2"):
                            rest_part(job, split)
                            middle_part(job, split)
                            low_part(split)
                    else:
                        r = RB if name in ("q1", "q2") else RB + 2
                        if name in ("q1", "k1"):
                            rotate_a(b, col[:, r:r + 1], job)
                        if name in ("q2", "k2"):
                            rotate_b(b, col[:, r + 1:r + 2], job, split)
                        if name == "v2":
                            dve.wait_ge(S["misc_full"], job + 1)
                            dve.tensor_tensor(v_16[:, QT * b:QT * (b + 1), :, 0:ROT_DIM],
                                              misc.rearrange("p (t h d) -> p t h d", t=QT, d=ROT_DIM),
                                              rows[:, 0, :].rearrange("p (h d) -> p h d", d=ROT_DIM).unsqueeze(1)
                                              .to_broadcast([P, QT, ROT_HEADS, ROT_DIM]), ALU.add) \
                                .then_inc(S["misc_free"], 1)
                    if name == "prime":
                        for i in range(16):
                            max_tile(u0, i, 0)
                        for i in range(8):
                            max_tile(u0 + 1, i, 1)
                    split += name in ("q2", "k2")
                    job += 1
                if kind == "nas" and x.jobs[0][0] == "fold" and c == NODES - 1:
                    dve.wait_ge(S["cell_copied"], NBLK)
                    dve.wait_ge(S["norm_rows_in"], 32)
                    norm_in_place(tok, 1e-6)
                    link(dve.tensor_tensor(tok, tok, spread(t_tmp[:, 0:D], TILES), ALU.mult))
                    link(dve.tensor_tensor(tok, tok, spread(t_tmp[:, D:2 * D], TILES), ALU.add))
                    norm_in_place(tok, 1e-5)
                    add_to_stream(tok)
                    norm_for_turn()
                continue

            def emit(b, x=x, kind=kind):
                c, heads, u0 = x.node, x.heads, x.unit(b)
                for h in range(heads):
                    u = u0 + h
                    for s in range(8):
                        ahead, first = maxima_of(s)
                        for k in range(2):
                            if not (x.last and h + ahead >= heads):
                                max_tile(u + ahead, first + k, (h + ahead) % 2)
                            name, hj, sj = x.job_before(h, s, k, 0)
                            if name:
                                job = x.job(b, hj, sj)
                            if name == "fold":
                                fold_sum(kind, u0 + hj - 1, job)
                            if name == "out":
                                node, blk = x.out_of(b)
                                out_job(kind, node, node_col(node) + blk * BLK, blk, job)
                            if name == "q1" and kind == "rot":
                                rotate_a(b + 1, col[:, RB:RB + 1], job)
                            if name == "q2" and kind == "rot":
                                rotate_b(b + 1, col[:, RB + 1:RB + 2], job, x.q_split(b))
                            if name == "q1" and kind == "nas":
                                edge(nodes[:, bass.ds(next_block(x, b), BLK)], col[:, QBE:QBE + 1],
                                     col[:, QEW:QEW + 1], job)
                            if name == "q2" and kind == "nas":
                                rest_part(job, x.q_split(b))
                            if name == "k2":
                                rest_part(job, x.k_split(b))
                            name, hj, sj = x.job_before(h, s, k, 1)
                            if name == "fold":
                                fold_recip(kind, u0 + hj - 1, x.job(b, hj, sj))
                            if name == "q2" and kind == "nas":
                                middle_part(x.job(b, hj, sj), x.q_split(b))
                            if name == "k2":
                                middle_part(x.job(b, hj, sj), x.k_split(b))
                            name, hj, sj = x.job_before(h, s, k, 2)
                            if name == "fold":
                                fold_scale(kind, u0 + hj - 1, (hj - 1) % heads)
                            if name == "q2" and kind == "nas":
                                low_part(x.q_split(b))
                            if name == "k2":
                                low_part(x.k_split(b))

            each_block(dve, x, emit)

        dve.wait_ge(S["misc_free"], job)
        norm_in_place(tok, 1e-5)
        add_to_stream(tok)
        norm_for_turn()

        dve.wait_ge(S["mlp_in"], 16 * 9)
        for k in range(2):
            dve.wait_ge(S["gates_ready"], k + 1)
            view = ps[:, k, 0:8 * GA].rearrange("p (t e) -> p t e", e=GA)
            link(dve.tensor_tensor(logits[:, 8 * k:8 * k + 8, :], view[:, :, 0:EXPERTS], spread(gate_bias, 8), ALU.add))

        def wide(v):
            return v.unsqueeze(2).to_broadcast([P, TILES, EXPERTS])

        link(dve.tensor_reduce(top, logits, AX.X, ALU.max))
        link(dve.tensor_tensor(chosen, logits, wide(top), ALU.is_equal))
        link(dve.tensor_tensor(chosen, chosen, spread(rank_row, TILES), ALU.mult))
        link(dve.tensor_reduce(top, chosen, AX.X, ALU.max))
        link(dve.tensor_tensor(chosen, chosen, wide(top), ALU.is_equal))
        for k in range(2):
            view = ps[:, k, 0:8 * GA].rearrange("p (t e) -> p t e", e=GA)[:, :, EXPERTS:GA] \
                .rearrange("p t (e r) -> p t e r", r=RANK)
            dve.tensor_tensor(low[:, 8 * k:8 * k + 8, :].rearrange("p t (e r) -> p t e r", r=RANK), view,
                              chosen[:, 8 * k:8 * k + 8, :].unsqueeze(3).to_broadcast([P, 8, EXPERTS, RANK]),
                              ALU.mult).then_inc(S["gates_copied"], 1)
        for b in range(NBLK):
            dve.wait_ge(S["mlp_full"], b + 1)
            dve.tensor_tensor(tok[:, QT * b:QT * (b + 1), :], ps[:, 6 + b % 2, :].rearrange("p (t d) -> p t d", d=D),
                              spread(wo_bias, QT), ALU.add).then_inc(S["mlp_free"], 1)
        dve.wait_ge(S["mlp_free"], NBLK)
        norm_in_place(tok, 1e-5)
        for b in range(NBLK):
            at = slice(QT * b, QT * (b + 1))
            dve.tensor_tensor(x_res[:, at, :], x_res[:, at, :], tok[:, at, :], ALU.add).then_inc(S["out_ready"], 1)


def kernel(**inputs):
    import concourse.bacc as bacc
    from concourse.bass_utils import run_bass_kernel_spmd as run

    def get(name):
        return np.asarray(inputs[name])

    def heads_swapped(bias):
        return bias.reshape(ROT_HEADS, 2, ROT_DIM // 2)[:, ::-1, :].reshape(-1)

    pos = np.arange(P)
    pick = np.zeros((P, P), np.float32)
    pick[:P // L0_SPAN] = pos // L0_SPAN == np.arange(P // L0_SPAN)[:, None]
    mask = np.zeros((P, BLK), np.float32)
    mask[:P // L0_SPAN] = np.tile((pick[:P // L0_SPAN] - 1) * np.float32(1e30), (1, 4))
    pick[M_ROW:K_ROWS] = 1.0
    half = ROT_DIM // 2
    inv = (np.float32(1.0) / np.float32(10000.0) ** (np.arange(half, dtype=np.float32) / np.float32(half))) \
        .astype(np.float32)
    angle = (inv[:, None] * np.arange(N, dtype=np.float32)[None, :]).astype(np.float32)
    cos = np.tile(np.cos(angle), (2 * ROT_HEADS, 1)).astype(np.float32)
    sin = np.tile(np.concatenate([-np.sin(angle), np.sin(angle)]), (ROT_HEADS, 1)).astype(np.float32)

    arrays = {
        "x": get("L0_attn_hidden_states"),
        "w_qkvT": get("L0_attn_w_qkv").T, "b_qkv": get("L0_attn_b_qkv"),
        "ew": get("L0_ffn_ew"), "act_w": get("L0_ffn_act_w"), "We": get("L0_ffn_We"), "be": get("L0_ffn_be"),
        "Wq": get("L0_ffn_Wq"), "Wk": get("L0_ffn_Wk"), "Wv": get("L0_ffn_Wv"), "Wo": get("L0_ffn_Wo"),
        "ln_g": get("L0_ffn_ln_g"), "ln_b": get("L0_ffn_ln_b"),
        "wq_w": get("L1_attn_wq_w"), "wk_w": get("L1_attn_wk_w"), "wv_w": get("L1_attn_wv_w"),
        "wo_w": get("L1_attn_wo_w"), "wq_b": get("L1_attn_wq_b"), "wk_b": get("L1_attn_wk_b"),
        "wq_b_swapped": heads_swapped(get("L1_attn_wq_b")), "wk_b_swapped": heads_swapped(get("L1_attn_wk_b")),
        "wv_b": get("L1_attn_wv_b"), "wo_b": get("L1_attn_wo_b"),
        "gate_T": get("L1_ffn_gate_W").T, "gate_b": get("L1_ffn_gate_b"),
        "wi_T": get("L1_ffn_wi_W").T, "wi_b": get("L1_ffn_wi_b"),
        "wo_T": get("L1_ffn_wo_W").T, "ffn_wo_b": get("L1_ffn_wo_b"),
        "lora_AT": get("L1_ffn_lora_A").reshape(EXPERTS * RANK, D).T,
        "lora_BT": get("L1_ffn_lora_B").transpose(0, 2, 1).reshape(EXPERTS * RANK, FF),
        "c_ident": np.eye(P, dtype=np.float32), "c_pick": pick, "c_mask": mask,
        "c_cos": cos, "c_sin": sin,
        "c_rank": np.arange(EXPERTS, 0, -1, dtype=np.float32)[None, :],
    }
    nc = bacc.Bacc("TRN2", target_bir_lowering=False, num_devices=1)
    given, A = {}, {}
    for name, a in arrays.items():
        a = np.ascontiguousarray(a)
        given[f"in_{name}"] = a
        A[name] = nc.dram_tensor(f"in_{name}", a.shape, mybir.dt.from_np(a.dtype), kind="ExternalInput").ap()
    out = nc.dram_tensor("out", (1, N, D), F32, kind="ExternalOutput").ap()
    build(nc, A, out)
    r = run(nc, [given], core_ids=[0])
    return r.results[0]["out"]
```

```python
from contextlib import ExitStack

import numpy as np

import concourse.bass as bass
from concourse import mybir

F32 = mybir.dt.float32
BF16 = mybir.dt.bfloat16
U32 = mybir.dt.uint32
ALU = mybir.AluOpType
ACT = mybir.ActivationFunctionType
AX = mybir.AxisListType

P = 128
N = 2048
D = 128
TILES = N // P
BLK = 512
NBLK = N // BLK
QT = BLK // P
M_ROW = 96
K_ROWS = M_ROW + 3
VW = 32
NODES = 6
MAX_PREV = 5
L0_HEADS, L0_DIM, L0_SPAN = 16, 8, 16
NAS_HEADS, NAS_DIM = 8, 16
ROT_HEADS, ROT_DIM = 16, 8
MASK_ROW = 48
EXPERTS, RANK, FF = 8, 4, 512
FC = FF // P

TERMS = ((0, 0, 1, 0, 1, 2), (0, 1, 0, 2, 1, 0))


FOLD_STEP, ROWS_STEP = 3, 5


def node_plan():
    plan, first = [], 0
    for c in range(NODES):
        n = min(c + 1, MAX_PREV)
        src = c - n
        plan.append(dict(eq=first + n - 1, ek=first, ev=first + n // 2, q=c - 1, k=src, v=src + n // 2))
        first += n
    return plan


NODE = node_plan()


def slot_of(node):
    return 0 if node == NODES - 1 else node + 1


def node_col(node, blk=0):
    return slot_of(node) * N + blk * BLK


BANK = [0, 1, 2, 1, 0, 2, 1, 0, 2, 1, 0, 1, 2, 0, 1, 2]
TAKEN = [next(d for d in range(1, 17) if BANK[(i - d) % 16] == BANK[i]) for i in range(16)]


MAX_TILE = [(i % 8 // 2, 2 * (i // 8) + i % 2) for i in range(16)]


def maxima_of(s):
    return (1, 8 + 2 * s) if s < 4 else (2, 2 * s - 8)


class Body:

    def __init__(self, kind, node, b0, b1, before, *, with_out, next_q, next_k, next_v, last):
        self.kind, self.node, self.b0, self.b1 = kind, node, b0, b1
        self.heads = NAS_HEADS if kind == "nas" else ROT_HEADS
        self.before = dict(before)
        self.with_out, self.next_q, self.next_k, self.next_v, self.last = with_out, next_q, next_k, next_v, last
        self.jobs = {}
        for h in range(self.heads):
            if h or with_out:
                self.jobs[h, FOLD_STEP] = "fold"
            if not (last and h == self.heads - 1):
                self.jobs[h, ROWS_STEP] = "rows"
        places = {"turn": (0, 7), "k1": (1, 1), "k2": (1, 7), "q1": (2, 1), "q2": (2, 7), "out": (3, 7),
                  "v1": (4, 7), "v2": (5, 7)}
        for names, wanted in (("turn out", with_out), ("q1 q2", next_q), ("k1 k2", next_k), ("v1 v2", next_v)):
            if wanted:
                self.jobs.update({places[name]: name for name in names.split()})
        self.goes_on = False
        self.late_before = 0
        self.order = {hs: n for n, hs in enumerate(sorted(self.jobs))}
        self.n_jobs = len(self.jobs)
        self.n_splits = int(next_q) + int(next_k)

    def late(self):
        return sum(k > (self.heads - 1, ROWS_STEP) for k in self.jobs)

    def unit(self, b):
        return self.before["unit"] + self.heads * (b - self.b0)

    def job(self, b, h, s):
        return self.before["job"] + self.n_jobs * (b - self.b0) + self.order[h, s]

    def job_before(self, h, s, k, ago):
        half = 16 * h + 2 * s + k - ago
        at = (half // 16, half % 16 // 2)
        return (self.jobs.get(at) if half % 2 and half >= 0 else None, *at)

    def k_split(self, b):
        return self.before["split"] + self.n_splits * (b - self.b0)

    def q_split(self, b):
        return self.k_split(b) + int(self.next_k)

    def body(self, b):
        return self.before["body"] + (b - self.b0)

    def jobs_so_far(self, b, h, s):
        return self.before["job"] + self.n_jobs * (b - self.b0) + sum(k < (h, s) for k in self.jobs)

    def out_of(self, b):
        return (self.node, b - 1) if self.b0 or self.kind == "rot" else (self.node - 1, NBLK - 1)

    def turns_over(self):
        return self.kind == "nas" and self.b1 == NBLK and not self.last

    def pick(self, b, here, there):
        if not self.turns_over():
            return here
        if self.b1 - self.b0 == 1:
            return there
        return here + (b // (NBLK - 1)) * (there - here)


class Serial:

    def __init__(self, kind, node, before, jobs):
        self.kind, self.node, self.before, self.jobs = kind, node, dict(before), jobs


class Prep:

    def __init__(self, kind, node, before, jobs):
        self.kind, self.node, self.before, self.jobs = kind, node, dict(before), jobs
        self.at = {job: before["prep"] + i for i, job in enumerate(jobs)}
        self.has_keys = ("k2", 0) in self.at

    def numbered(self):
        return [(name, b, n) for (name, b), n in self.at.items()]


def make_plan():
    plan = []
    count = dict(unit=0, job=0, split=0, body=0, prep=0)

    def body(kind, node, b0, b1, **kw):
        x = Body(kind, node, b0, b1, count, **kw)
        if isinstance(plan[-1], Body):
            plan[-1].goes_on = True
            x.late_before = plan[-1].late()
        plan.append(x)
        n = b1 - b0
        count["unit"] += x.heads * n
        count["job"] += x.n_jobs * n
        count["split"] += x.n_splits * n
        count["body"] += n

    def serial(kind, node, jobs):
        plan.append(Serial(kind, node, count, jobs))
        count["job"] += len(jobs)

    def prep(kind, node, jobs):
        plan.append(Prep(kind, node, count, jobs))
        count["prep"] += len(jobs)

    def over_blocks(name):
        return [(name, b) for b in range(NBLK)]

    values = over_blocks("v1") + over_blocks("v2")
    finish = [("fold", NBLK - 1), ("turn", NBLK - 1), ("out", NBLK - 1)]
    prep("nas", 0, [("q1", 0)] + over_blocks("k1") + [("q2", 0)] + over_blocks("k2") + values)
    serial("nas", 0, [("prime", 0)])
    for c in range(NODES):
        end = c == NODES - 1
        kw = dict(next_q=True, next_k=not end, next_v=not end and c > 0, last=False)
        body("nas", c, 0, 1, with_out=c > 1, **kw)
        body("nas", c, 1, NBLK - end, with_out=True, **kw)
        if end:
            body("nas", c, NBLK - 1, NBLK, with_out=True, next_q=False, next_k=False, next_v=False, last=True)
        if c == 0:
            serial("nas", 0, finish)
            prep("nas", 1, values)
    serial("nas", NODES - 1, finish)
    count["body"] = 0
    prep("rot", 0, [("q1", 0), ("q2", 0)] + [(name, b) for b in range(NBLK) for name in ("k1", "k2")]
         + over_blocks("v2"))
    serial("rot", 0, [("prime", 0)])
    kw = dict(next_k=False, next_v=False)
    body("rot", 0, 0, 1, with_out=False, next_q=True, last=False, **kw)
    body("rot", 0, 1, NBLK - 1, with_out=True, next_q=True, last=False, **kw)
    body("rot", 0, NBLK - 1, NBLK, with_out=True, next_q=False, last=True, **kw)
    serial("rot", 0, finish)
    return plan


PLAN = make_plan()


def need(eng, semaphore, value):
    if not (isinstance(value, int) and value <= 0):
        eng.wait_ge(semaphore, value)


def each_block(eng, body, emit):
    if body.b1 - body.b0 == 1:
        emit(body.b0)
    else:
        with eng.Fori(body.b0, body.b1) as b:
            emit(b)


def build(nc, A, out):
    with ExitStack() as ctx:
        build_program(nc, ctx, A, out)


def build_program(nc, ctx, A, out):
    def sb(name, shape, dt):
        return ctx.enter_context(nc.sbuf_tensor(name, shape, dt))

    def sem(name):
        return ctx.enter_context(nc.semaphore(name))

    big = sb("big", [P, 6 * N + 4096 + 4096], F32)
    nodes = big[:, 0:6 * N]
    xT = big[:, 0:N]
    tok = big[:, N:2 * N].rearrange("p (t d) -> p t d", d=D)
    att = big[:, 0:N].rearrange("p (t d) -> p t d", d=D)
    qst = big[:, 6 * N:6 * N + 4096].bitcast(BF16)
    probs = big[:, 6 * N + 4096:6 * N + 8192].rearrange("p (i n) -> p i n", i=8)
    prep_parts = [big[:, 6 * N + 4096 + i * 768:6 * N + 4096 + (i + 1) * 768].bitcast(BF16)
                  .rearrange("p (t n) -> p t n", t=3) for i in range(1 + NBLK)]
    q_loc = big[:, N:N + 16 * N // 2].bitcast(BF16)
    q_loc_heads = q_loc.rearrange("p (h n) -> p h n", n=N)
    kst = sb("kst", [P, 16 * N], BF16)
    vst = sb("vst", [P, 256 * VW], F32)
    v_cols = vst[:, :].rearrange("p (x w) -> p x w", w=VW)
    v_nas = vst[:, :].rearrange("p (a t h w) -> p a t h w", a=2, t=TILES, h=NAS_HEADS)
    v_16 = vst[:, :].rearrange("p (t h w) -> p t h w", t=TILES, h=16)
    x_res = sb("x_res", [P, TILES, D], F32)
    ob = sb("ob", [P, N], F32)
    normed_x = ob[:, :].rearrange("p (t d) -> p t d", d=D)
    o_part = ob[:, 0:1024].rearrange("p (i n) -> p i n", i=2)
    o_tok = ob[:, 1024:1536].rearrange("p (t d) -> p t d", d=D)
    o_chan = ob[:, 1536:2048]
    prep_edges = [ob[:, b * BLK:(b + 1) * BLK] for b in range(NBLK)]
    local_parts = [ob[:, i * 768:(i + 1) * 768].bitcast(BF16).rearrange("p (t n) -> p t n", t=3) for i in range(2)]
    local_parts += prep_parts[3:5]
    parts = sb("parts", [P, 3, BLK], BF16)
    rest = sb("rest", [P, BLK], F32)
    t_tmp = sb("t_tmp", [P, BLK], F32)
    l_probs = (rest, t_tmp)
    w_q, w_k, w_v, w_o = (sb(f"w_{x}", [P, 2, D], F32) for x in "qkvo")
    ident = sb("ident", [P, P], F32)
    ident_b = sb("ident_b", [P, P], BF16)
    blocks_b = sb("blocks_b", [P // L0_SPAN, 2, P], BF16)
    col = sb("col", [P, 72], F32)
    BE, EW, AW, QBE, QEW, RB, LB, FB, EB = 0, 20, 38, 44, 45, 46, 50, 52, 56
    stats = sb("stats", [P, TILES, 6], F32)
    mean_var = sb("mean_var", [P, TILES, 2], F32)
    rstd = sb("rstd", [P, 3, TILES], F32)
    row_max = sb("row_max", [P, 2, 16], F32)
    neg_max = sb("neg_max", [P, 2, 4], F32)
    neg_rest = sb("neg_rest", [P, 2, 4], F32)
    zeros = sb("zeros", [P, 4], F32)
    max_parts = sb("max_parts", [P, 2, 4, 3], BF16)
    sums = sb("sums", [P, QT, NAS_DIM + 1], F32)
    recip = sb("recip", [P, 16], F32)
    v_now = [w[:, 0, :].rearrange("p (h w) -> p h w", w=VW) for w in (w_q, w_k)]
    cos, sin = big[:, 2 * N:3 * N], big[:, 3 * N:4 * N]
    rot_a, rot_b, rot_sum = (big[:, 4 * N + i * BLK:4 * N + (i + 1) * BLK] for i in range(3))
    rot_sums = [rot_sum, t_tmp[:, :]]
    rows = big[:, 4 * N + 3 * BLK:4 * N + 3 * BLK + 384].rearrange("p (i d) -> p i d", d=D)
    M0 = 5 * N
    wi = big[:, M0:M0 + FF]
    wo = big[:, M0 + FF:M0 + 2 * FF].rearrange("p (c d) -> p c d", d=D)
    lora_b = big[:, M0 + 2 * FF:M0 + 3 * FF]
    GA = EXPERTS + EXPERTS * RANK
    gate_a = big[:, M0 + 3 * FF:M0 + 3 * FF + GA]
    gate_bias = big[:, M0 + 3 * FF + 64:M0 + 3 * FF + 64 + EXPERTS]
    rank_row = big[:, M0 + 3 * FF + 80:M0 + 3 * FF + 80 + EXPERTS]
    wo_bias = big[:, M0 + 3 * FF + 128:M0 + 3 * FF + 256]
    hid = vst[:, 0:2 * FC * BLK].rearrange("p (i c n) -> p i c n", i=2, c=FC)
    low_T = big[:, 6 * N:7 * N]
    G0 = 4 * N
    logits = big[:, G0:G0 + 128].rearrange("p (t e) -> p t e", e=EXPERTS)
    chosen = big[:, G0 + 128:G0 + 256].rearrange("p (t e) -> p t e", e=EXPERTS)
    top = big[:, G0 + 256:G0 + 272]
    low = big[:, G0 + 512:G0 + 1024].rearrange("p (t r) -> p t r", r=EXPERTS * RANK)

    ps = ctx.enter_context(nc.psum_tensor("ps", [P, 8, BLK], F32))
    MAXES, ACC, MISC = 3, 6, 7
    L_MAXES = 4
    misc = ps[:, MISC, :]
    acc = ps[:, ACC, :]

    scratch = {x: nc.dram_tensor(f"parts_{x}", [3, P, N], BF16, kind="Internal").ap() for x in "qk"}

    def stacked(x, term, dim, heads, c0, c1):
        return scratch[x][term, :, c0:c1].rearrange("(h r) n -> r h n", r=dim)[:, heads, :]

    S = {name: sem(name) for name in """
        x_in const_in small_in w0_in late_keys_in nas_cols_in norm_rows_in rot_in rot_rows_in mlp_in
        consts_made rows_ready q_rows_ready zeros_ready
        var_ready std_ready normed turned turn_copied
        dve_step
        l_full l_free l_parts_ready l_parts_sent_0 l_parts_sent_1 l_parts_sent_2 l_parts_sent_3 l_q_in l_k_in
        l_scores l_neg l_pool l_maxparts l_rows l_rows_in l_st l_exp l_vnow l_pv l_acc l_turned l_normed
        tile_ready tile_done neg_ready pool_step maxparts_ready st_ready exp_done pv_done acc_copied
        prep_full prep_free_0 prep_free_1 prep_free_2 prep_free_3 prep_parts_ready prep_sent
        prep_high_ready prep_sum_ready
        misc_full misc_free high_ready mid_ready rest_ready parts_ready parts_sent
        heads_recip heads_normed rot_sum_done
        q_weights_in node_weights_in nas_k_in nas_qa_in nas_qb_in rot_k_in rot_qa_in rot_qb_in
        low_cleared cell_turned cell_copied edges_ready gates_ready gates_copied low_turned low_copied hid_full hid_free
        mlp_full mlp_free pads_ready out_ready rot_swapped rot_high_ready out_in""".split()}

    l_parts_sent = [S[f"l_parts_sent_{i}"] for i in range(4)]
    block = ctx.enter_context(nc.Block())
    n_terms = len(TERMS[0])
    dims = {"nas": NAS_DIM, "rot": ROT_DIM}
    heads_of = {"nas": NAS_HEADS, "rot": ROT_HEADS}
    rot_split0 = next(x for x in PLAN if x.kind == "rot").before["split"]
    prep_free = [S[f"prep_free_{i}"] for i in range(4)]

    ROT_PADS = 6

    def node_weights_count(node):
        return 64 + 80 * (node + 1) - 64 * (node == NODES - 1)

    def in_nodes(at):
        if isinstance(at, int):
            return at
        return nc.s_assert_within(at, 0, 6 * N - BLK, skip_runtime_bounds_check_because="blocks 0..3 of slots 0..5")

    def next_block(x, b):
        return in_nodes(x.pick(b, node_col(x.node), node_col(min(x.node + 1, NODES - 1)) - N) + (b + 1) * BLK)


    @block.sync
    def _(sp):
        def load(dst, src, semaphore, **kw):
            sp.dma_start(dst, src, **kw).then_inc(S[semaphore], 16)

        load(x_res[:, :, :], A["x"][0].rearrange("(t p) d -> p t d", p=P), "x_in")
        load(ident[:, :], A["c_ident"], "const_in")
        for w, i in ((w_q, 0), (w_k, 1), (w_v, 2)):
            load(w[:, 0, :], A["w_qkvT"][:, i * D:(i + 1) * D], "w0_in")
        for i in range(2):
            load(col[:, LB + i:LB + i + 1], A["b_qkv"][i * D:(i + 1) * D].rearrange("(p a) -> p a", a=1), "w0_in")
        load(w_o[:, 0, :], A["b_qkv"][2 * D:3 * D].rearrange("(a d) -> a d", a=1).partition_broadcast(P), "w0_in")
        load(t_tmp[0:P // L0_SPAN, 0:2 * P], A["c_blocks"], "small_in")

        terms_q, terms_k = TERMS

        def load_blocks(stack, i, semaphore):
            load(stack[MASK_ROW:MASK_ROW + P // L0_SPAN, :].rearrange("p (a n) -> p a n", n=P),
                 blocks_b[:, i, :].unsqueeze(1).to_broadcast([P // L0_SPAN, L0_HEADS * TILES, P]), semaphore)

        for n in range(2 * NBLK):
            x, b = ("k", n) if n < NBLK else ("q", n - NBLK)
            sp.wait_ge(S["l_parts_ready"], n + 1)
            sp.dma_start(scratch[x][:, :, b * BLK:(b + 1) * BLK].rearrange("t p n -> p t n"),
                         local_parts[n % 4]).then_inc(l_parts_sent[n % 4], 16)
            if n == NBLK - 1 or n == 2 * NBLK - 1:
                sp.wait_ge(S["rows_ready"], 1)
                need(sp, S["q_rows_ready"], 0 if n < NBLK else 2)
                for sent in l_parts_sent:
                    sp.wait_ge(sent, 16 * (n + 1) // 4)
                if n == NBLK - 1:
                    sp.wait_ge(S["consts_made"], 2)
                    load_blocks(kst, 1, "l_k_in")
                    for j, term in enumerate(terms_k):
                        load(kst[8 * j:8 * j + 8, :].rearrange("p (h n) -> p h n", n=N),
                             stacked("k", term, L0_DIM, slice(0, 16), 0, N), "l_k_in")
                else:
                    load_blocks(q_loc, 0, "l_q_in")
                    for j, term in enumerate(terms_q):
                        load(q_loc[8 * j:8 * j + 8, :].rearrange("p (h n) -> p h n", n=N),
                             stacked("q", term, L0_DIM, slice(0, 16), 0, N), "l_q_in")

        sp.wait_ge(S["l_normed"], 16)
        load(col[:, BE:BE + 20], A["be"].rearrange("e d -> d e"), "nas_cols_in", allow_slow_non_contiguous=True)
        load(col[:, EW:EW + 18], A["ew"].rearrange("c g -> (c g)").rearrange("(a n) -> a n", a=1)
             .partition_broadcast(P), "nas_cols_in")
        load(col[:, AW:AW + NODES], A["act_w"].rearrange("(a n) -> a n", a=1).partition_broadcast(P), "nas_cols_in")

        def node_q_weights(b, x, node_here, node_there):
            e, c = NODE[node_here]["eq"], node_here
            if x:
                e, c = x.pick(b, e, NODE[node_there]["eq"]), x.pick(b, c, node_there)
            load(w_q[:, 0, :], A["We"][bass.ds(e, 1)].rearrange("a k n -> (a k) n"), "q_weights_in")
            load(w_q[:, 1, :], A["Wq"][bass.ds(c, 1)].rearrange("a k n -> (a k) n"), "q_weights_in")
            load(col[:, QBE:QBE + 1], A["be"][bass.ds(e, 1), :].rearrange("a d -> d a"), "q_weights_in",
                 allow_slow_non_contiguous=True)
            load(col[:, QEW:QEW + 1], A["ew"][bass.ds(c, 1), 0:1].partition_broadcast(P)
                 .rearrange("p a b -> p (a b)"), "q_weights_in")

        def kv_weights(c):
            load(w_k[:, 0, :], A["We"][NODE[c]["ek"]], "node_weights_in")
            load(w_k[:, 1, :], A["Wk"][c], "node_weights_in")
            load(w_v[:, 0, :], A["We"][NODE[c]["ev"]], "node_weights_in")
            load(w_v[:, 1, :], A["Wv"][c], "node_weights_in")

        node_q_weights(0, None, 0, 0)
        kv_weights(0)

        def send_parts(x, split, ready=None):
            sp.wait_ge(S["parts_ready"], split + 1 if ready is None else ready)
            sp.dma_start(scratch[x][:, :, 0:BLK].rearrange("t p n -> p t n"),
                         parts[:, :, :]).then_inc(S["parts_sent"], 16)
            sp.wait_ge(S["parts_sent"], 16 * (split + 1))

        def stage_queries(kind, half, semaphore):
            d, h2 = dims[kind], heads_of[kind] // 2
            for j, term in enumerate(TERMS[0]):
                load(qst[d * j:d * j + d, half * h2 * BLK:(half + 1) * h2 * BLK].rearrange("p (h n) -> p h n", n=BLK),
                     stacked("q", term, d, slice(half * h2, (half + 1) * h2), 0, BLK), semaphore)

        def stage_keys(kind, node, at, source, width, semaphore=None):
            d, heads = dims[kind], heads_of[kind]
            slots = kst[:, :] if kind == "rot" else kst[:, (node % 2) * 8 * N:(node % 2) * 8 * N + 8 * N]
            for j, term in enumerate(TERMS[1]):
                load(slots[d * j:d * j + d, :].rearrange("p (h n) -> p h n", n=N)[:, :, bass.ds(at, width)],
                     stacked("k", term, d, slice(0, heads), source, source + width), semaphore or f"{kind}_k_in")

        preps = 0
        for x in PLAN:
            kind = x.kind
            if isinstance(x, Serial):
                continue
            if isinstance(x, Prep):
                if kind == "rot":
                    sp.wait_ge(S["cell_turned"], 4)
                    load(w_q[:, 0, :], A["wq_w"], "rot_in")
                    load(w_k[:, 0, :], A["wk_w"], "rot_in")
                    load(w_v[:, 0, :], A["wv_w"], "rot_in")
                    load(w_o[:, 0, :], A["wo_w"], "rot_in")
                    for i, name in enumerate(("wq_b", "wk_b")):
                        load(col[:, RB + 2 * i:RB + 2 * i + 1], A[name].rearrange("(p a) -> p a", a=1), "rot_in")
                        load(col[:, RB + 2 * i + 1:RB + 2 * i + 2], A[name + "_swapped"].rearrange("(p a) -> p a", a=1),
                             "rot_in")
                    load(cos, A["c_cos"], "rot_in")
                    load(sin, A["c_sin"], "rot_in")
                    load(rows[:, 0, :], A["wv_b"].rearrange("(a d) -> a d", a=1).partition_broadcast(P), "rot_rows_in")
                    load(rows[:, 1, :], A["wo_b"].rearrange("(a d) -> a d", a=1).partition_broadcast(P), "rot_rows_in")
                    load(wi, A["wi_T"], "mlp_in")
                    load(wo, A["wo_T"].rearrange("(c p) d -> p c d", p=P), "mlp_in")
                    load(lora_b[0:EXPERTS * RANK, :], A["lora_BT"], "mlp_in")
                    load(gate_a[:, 0:EXPERTS], A["gate_T"], "mlp_in")
                    load(gate_a[:, EXPERTS:GA], A["lora_AT"], "mlp_in")
                    load(gate_bias, A["gate_b"].rearrange("(a d) -> a d", a=1).partition_broadcast(P), "mlp_in")
                    load(rank_row, A["c_rank"].partition_broadcast(P), "mlp_in")
                    load(wo_bias, A["ffn_wo_b"].rearrange("(a d) -> a d", a=1).partition_broadcast(P), "mlp_in")
                    load(col[:, FB:FB + FC], A["wi_b"].rearrange("(c p) -> p c", p=P), "mlp_in",
                         allow_slow_non_contiguous=True)
                    sp.wait_ge(S["pads_ready"], ROT_PADS)
                if not x.has_keys:
                    continue
                ready = (1 + NBLK) * preps
                for i in range(1 + NBLK):
                    ready += 1
                    sp.wait_ge(S["prep_parts_ready"], ready)
                    dst = scratch["q"][:, :, 0:BLK] if i == 0 else scratch["k"][:, :, (i - 1) * BLK:i * BLK]
                    sp.dma_start(dst.rearrange("t p n -> p t n"), prep_parts[i]).then_inc(S["prep_sent"], 16)
                    if i in (NBLK // 2, NBLK):
                        sp.wait_ge(S["prep_sent"], 16 * ready)
                    if i == NBLK // 2:
                        stage_queries(kind, 0, f"{kind}_qa_in")
                        stage_keys(kind, 0, 0, 0, N // 2)
                    if i == NBLK:
                        stage_keys(kind, 0, N // 2, N // 2, N // 2, "late_keys_in")
                preps += 1
                continue

            def emit(b, x=x, kind=kind):
                c, g = x.node, x.body(b)
                nt = 16 * n_terms
                ready = {n: None if isinstance(b, int) else sp.to_reg(v + 1)
                         for n, v in (("k", x.k_split(b)), ("q", x.q_split(b)))}
                need(sp, S["misc_full"], x.before["job"] + x.n_jobs * (b - x.b0))
                need(sp, S["st_ready"], 16 * x.unit(b))
                sp.wait_ge(S["prep_full"], x.before["prep"])
                if kind == "nas":
                    if x.b0 == 0:
                        if x.next_k:
                            kv_weights(c + 1)
                        load(w_o[:, c % 2, :], A["Wo"][c], "node_weights_in")
                    if x.next_q:
                        node_q_weights(b, x, c, min(c + 1, NODES - 1))
                stage_queries(kind, 1, f"{kind}_qb_in")
                if x.next_k:
                    sp.wait_ge(S["nas_k_in"], nt * (1 + NBLK * c + b))
                    send_parts("k", x.k_split(b), ready["k"])
                    stage_keys(kind, c + 1, b * BLK, 0, BLK)
                if x.next_q:
                    sp.wait_ge(S[f"{kind}_qb_in"], nt * (g + 1))
                    send_parts("q", x.q_split(b), ready["q"])
                    sp.wait_ge(S["st_ready"], 16 * (x.unit(b) + x.heads // 2))
                    stage_queries(kind, 0, f"{kind}_qa_in")

            each_block(sp, x, emit)
            if kind == "nas" and x.last:
                load(t_tmp[:, 0:D], A["ln_g"].rearrange("(a d) -> a d", a=1).partition_broadcast(P), "norm_rows_in")
                load(t_tmp[:, D:2 * D], A["ln_b"].rearrange("(a d) -> a d", a=1).partition_broadcast(P), "norm_rows_in")

        for b in range(NBLK):
            sp.wait_ge(S["out_ready"], b + 1)
            load(out[0].rearrange("(t p) d -> p t d", p=P)[:, QT * b:QT * (b + 1), :],
                 x_res[:, QT * b:QT * (b + 1), :], "out_in")
        sp.wait_ge(S["out_in"], 16 * NBLK)

    @block.gpsimd
    def _(pool):
        pool.memset(zeros[:, :], 0.0).then_inc(S["zeros_ready"], 1)
        pool.wait_ge(S["zeros_ready"], 1)
        two_ones = float(np.array([0x3F803F80], np.uint32).view(np.float32)[0])
        for i, at in enumerate((slice(32, 64), slice(64, P))):
            pool.memset(kst[at, :].bitcast(F32), two_ones).then_inc(S["rows_ready"], 1)
            pool.wait_ge(S["rows_ready"], i + 1)

        def split_max(neg, out3, step_sem, done_sem, n, i):
            pool.tensor_tensor(out3[:, i, :, 0], neg[:, i, :], zeros[:, :], ALU.add).then_inc(S[step_sem], 1)
            pool.wait_ge(S[step_sem], 3 * n + 1)
            pool.tensor_tensor(neg_rest[:, i, :], neg[:, i, :], out3[:, i, :, 0], ALU.subtract).then_inc(S[step_sem], 1)
            pool.wait_ge(S[step_sem], 3 * n + 2)
            pool.tensor_tensor(out3[:, i, :, 1], neg_rest[:, i, :], zeros[:, :], ALU.add) \
                .then_inc(S[step_sem], 1)
            pool.wait_ge(S[step_sem], 3 * n + 3)
            pool.tensor_tensor(out3[:, i, :, 2], neg_rest[:, i, :], out3[:, i, :, 1], ALU.subtract) \
                .then_inc(S[done_sem], 1)

        def local_step(n, i):
            pool.wait_ge(S["l_neg"], n + 1)
            need(pool, S["l_rows"], n - 1)
            split_max(neg_max, max_parts, "l_pool", "l_maxparts", n, i)

        for grp in range(L0_HEADS // 4):
            with pool.Fori(0, TILES // 2) as pair:
                t = 2 * pair
                for i in range(2):
                    if grp == 0:
                        pool.wait_ge(S["l_neg"], t + (i + 1))
                        split_max(neg_max, max_parts, "l_pool", "l_maxparts", t + i, i)
                    else:
                        local_step(grp * TILES + i + t, i)

        def low_part(split):
            pool.wait_ge(S["mid_ready"], split + 1)
            pool.tensor_tensor(parts[:, 2, :], rest[:, :], parts[:, 1, :], ALU.subtract).then_inc(S["parts_ready"], 1)

        def attention_step(u, i):
            pool.wait_ge(S["neg_ready"], u + 1)
            split_max(neg_max, max_parts, "pool_step", "maxparts_ready", u, i)

        for x in PLAN:
            if isinstance(x, Prep) and x.kind == "rot":
                pool.wait_ge(S["cell_turned"], NBLK)
                pads = 0
                for dst, value in ((qst[32:64, :].bitcast(F32), 0.0), (qst[64:M_ROW, :].bitcast(F32), 0.0),
                                   (v_cols[:, :, ROT_DIM:NAS_DIM + 1], 0.0), (v_cols[:, :, ROT_DIM:ROT_DIM + 1], 1.0),
                                   (lora_b[32:64, :], 0.0), (lora_b[64:P, :], 0.0)):
                    pool.memset(dst, value).then_inc(S["pads_ready"], 1)
                    pads += 1
                    pool.wait_ge(S["pads_ready"], pads)
            if not isinstance(x, Body):
                if x.jobs[-1][0] == "prime":
                    attention_step(x.before["unit"], 0)
                continue

            def emit(b, x=x):
                for h in range(x.heads):
                    if not (x.last and h == x.heads - 1):
                        attention_step(x.unit(b) + h + 1, (h + 1) % 2)
                    if x.kind == "nas" and x.jobs.get((h, 7)) == "k2":
                        low_part(x.k_split(b))
                    if x.kind == "nas" and x.jobs.get((h, 7)) == "q2":
                        low_part(x.q_split(b))

            each_block(pool, x, emit)

        units = PLAN[-1].before["unit"]
        pool.wait_ge(S["st_ready"], 16 * units)
        pool.wait_ge(S["tile_ready"], 16 * units)
        for i, dst in enumerate((low_T[32:64, :], low_T[64:P, :])):
            pool.memset(dst, 0.0).then_inc(S["low_cleared"], 1)
            pool.wait_ge(S["low_cleared"], i + 1)

    @block.scalar
    def _(act):
        norms = [0]

        def root(t0=0, t1=TILES):
            act.wait_ge(S["var_ready"], norms[0] + 1)
            act.activation(rstd[:, 1, t0:t1], rstd[:, 0, t0:t1], ACT.Sqrt).then_inc(S["std_ready"], 1)
            norms[0] += 1

        def copy_turned(layer):
            for b in range(NBLK):
                act.wait_ge(S["turned"], NBLK * layer + b + 1)
                act.activation(xT[:, b * BLK:(b + 1) * BLK], ps[:, b, :], ACT.Copy).then_inc(S["turn_copied"], 1)

        root()
        copy_turned(0)
        act.wait_ge(S["zeros_ready"], 1)
        for at in (slice(32, 64), slice(64, M_ROW)):
            act.activation(big[at, N:N + 16 * N // 2], zeros[at, 0:1].to_broadcast([32, 16 * N // 2]), ACT.Copy) \
                .then_inc(S["q_rows_ready"], 1)


        def local_rows(n, t, grp, i):
            act.wait_ge(S["l_rows"], n + 1)
            act.activation(q_loc_heads[M_ROW:K_ROWS, 4 * grp:4 * grp + 4, bass.ds(t * P, P)],
                           ps[M_ROW:K_ROWS, 2 + i, :].rearrange("p (h n) -> p h n", h=4), ACT.Copy) \
                .then_inc(S["l_rows_in"], 1)

        def local_exp(n, i):
            act.wait_ge(S["l_st"], n + 1)
            need(act, S["l_pv"], n - 1)
            act.activation(l_probs[i][:, :], ps[:, i, :], ACT.Exp, scale=float(L0_DIM) ** -0.5) \
                .then_inc(S["l_exp"], 1)

        for grp in range(L0_HEADS // 4):
            n0 = grp * TILES
            for t in range(4):
                local_rows(n0 + t, t, grp, t % 2)
                if t:
                    local_exp(n0 + t - 1, (t - 1) % 2)
            with act.Fori(1, TILES // 4) as quad:
                for i in range(4):
                    local_rows(n0 + i + 4 * quad, 4 * quad + i, grp, i % 2)
                    local_exp(n0 + i - 1 + 4 * quad, 1 - i % 2)
            local_exp(n0 + TILES - 1, 1)

        root()
        root()
        copy_turned(1)

        def rows_copy(job, slot):
            act.wait_ge(S["misc_full"], job + 1)
            act.activation(qst[M_ROW:K_ROWS, slot * BLK:(slot + 1) * BLK], misc[M_ROW:K_ROWS, :], ACT.Copy) \
                .then_inc(S["misc_free"], 1)

        def turn_copy(job):
            act.wait_ge(S["misc_full"], job + 1)
            act.activation(o_chan, misc, ACT.Copy).then_inc(S["misc_free"], 1)

        def high_part(job, split):
            act.wait_ge(S["misc_full"], job + 1)
            need(act, S["parts_sent"], 16 * split)
            act.activation(parts[:, 0, :], misc, ACT.Copy).then_inc(S["high_ready"], 1)

        def middle_part(job, split):
            act.wait_ge(S["misc_free"], job + 1)
            act.activation(parts[:, 1, :], rest[:, :], ACT.Copy).then_inc(S["mid_ready"], 1)

        def edge(e, job):
            act.wait_ge(S["misc_full"], job + 1)
            act.activation(t_tmp[:, :], misc, ACT.Identity, bias=col[:, EB + e:EB + e + 1],
                           scale=col[:, EW + 3 * (e // 2) + 1 + e % 2:EW + 3 * (e // 2) + 2 + e % 2]) \
                .then_inc(S["misc_free"], 1)

        def cell_values(par, b, job):
            act.wait_ge(S["misc_full"], job + 1)
            size = NAS_HEADS * VW
            dst = vst[:, bass.ds(par * TILES * size + b * (QT * size), QT * size)] \
                .rearrange("p (t h w) -> p t h w", t=QT, w=VW)[:, :, :, 0:NAS_DIM]
            act.activation(dst, misc.rearrange("p (t h d) -> p t h d", t=QT, d=NAS_DIM), ACT.Copy) \
                .then_inc(S["misc_free"], 1)

        def acc_copy(u, i):
            act.wait_ge(S["pv_done"], 4 * u + 4)
            act.activation(o_part[:, i, :], acc, ACT.Copy).then_inc(S["acc_copied"], 1)

        rot_sums_done = 0
        for x in PLAN:
            kind = x.kind
            if isinstance(x, Prep):
                need(act, S["misc_free"], x.before["job"])
                if kind == "nas" and x.node == 0:
                    act.wait_ge(S["edges_ready"], 2 * NODES)
                for name, b, n in x.numbered():
                    if kind == "nas":
                        act.wait_ge(S["prep_full"], n + 1)
                        bank = ps[:, n % 4, :]
                    if kind == "nas" and name in ("k1", "v1"):
                        if name == "v1" and x.has_keys:
                            act.wait_ge(S["prep_full"], x.at["k2", b] + 1)
                        e = 2 * x.node + (name == "v1")
                        gate = EW + 3 * x.node + 1 + (name == "v1")
                        act.activation(prep_edges[b], bank, ACT.Identity, bias=col[:, EB + e:EB + e + 1],
                                       scale=col[:, gate:gate + 1]).then_inc(prep_free[n % 4], 1)
                    if kind == "nas" and name in ("q2", "k2"):
                        act.activation(prep_parts[b + (name == "k2")][:, 0, :], bank, ACT.Copy) \
                            .then_inc(S["prep_high_ready"], 1)
                    if kind == "rot" and name in ("q2", "k2"):
                        act.wait_ge(S["prep_sum_ready"], rot_sums_done + 1)
                        act.activation(prep_parts[b + (name == "k2")][:, 0, :], rot_sums[rot_sums_done % 2], ACT.Copy) \
                            .then_inc(S["prep_high_ready"], 1)
                        rot_sums_done += 1
                    if kind == "nas" and name == "v2":
                        dst = v_nas[:, x.node % 2, QT * b:QT * (b + 1), :, 0:NAS_DIM]
                        act.activation(dst, bank.rearrange("p (t h d) -> p t h d", t=QT, d=NAS_DIM), ACT.Copy) \
                            .then_inc(prep_free[n % 4], 1)
                continue
            if isinstance(x, Serial):
                job = x.before["job"]
                for name, b in x.jobs:
                    if name == "prime":
                        rows_copy(job, 0)
                    if name == "turn":
                        turn_copy(job)
                    job += 1
                if kind == "nas" and x.jobs[0][0] == "fold" and x.node == NODES - 1:
                    for b in range(NBLK):
                        act.wait_ge(S["cell_turned"], b + 1)
                        act.activation(tok[:, QT * b:QT * (b + 1), :].rearrange("p t d -> p (t d)"), ps[:, b, :],
                                       ACT.Copy).then_inc(S["cell_copied"], 1)
                    for _ in range(3):
                        root()
                    copy_turned(2)
                continue

            def emit(b, x=x, kind=kind):
                for h in range(x.heads):
                    u = x.unit(b) + h
                    for s in range(8):
                        for i in (2 * s, 2 * s + 1):
                            act.wait_ge(S["st_ready"], 16 * u + i + 1)
                            if i % 4 == 0:
                                need(act, S["pv_done"], 4 * u + i // 4 - 1)
                            act.activation(probs[:, i % 8, :], ps[:, BANK[i], :], ACT.Exp,
                                           scale=float(dims[kind]) ** -0.5).then_inc(S["exp_done"], 1)
                        if s == 1 and (h > 0 or x.with_out):
                            acc_copy(u - 1, (h - 1) % 2)
                        name, hj, sj = x.job_before(h, s, 1, 2)
                        if name == "q2" and kind == "nas":
                            middle_part(x.job(b, hj, sj), x.q_split(b))
                        if name == "k2":
                            middle_part(x.job(b, hj, sj), x.k_split(b))
                        name = x.jobs.get((h, s))
                        if name == "rows":
                            rows_copy(x.job(b, h, s), (h + 1) % x.heads)
                        if name == "turn":
                            turn_copy(x.job(b, h, s))
                        if name == "q2" and kind == "nas":
                            high_part(x.job(b, h, s), x.q_split(b))
                        if name == "k2":
                            high_part(x.job(b, h, s), x.k_split(b))
                        if name in ("k1", "v1"):
                            edge(2 * (x.node + 1) + (name == "v1"), x.job(b, h, s))
                        if name == "v2":
                            cell_values((x.node + 1) % 2, b, x.job(b, h, s))

            each_block(act, x, emit)
            if not x.goes_on:
                acc_copy(x.unit(x.b1) - 1, (x.heads - 1) % 2)

        root()
        root()
        copy_turned(3)

        for b in range(NBLK):
            act.wait_ge(S["low_turned"], b + 1)
            act.activation(low_T[0:EXPERTS * RANK, b * BLK:(b + 1) * BLK], ps[0:EXPERTS * RANK, 2 + b, :], ACT.Copy) \
                .then_inc(S["low_copied"], 1)
        act.wait_ge(S["mlp_in"], 16 * 9)
        for b in range(NBLK):
            for c in range(FC):
                i = FC * b + c
                act.wait_ge(S["hid_full"], i + 1)
                need(act, S["mlp_full"], b - 1)
                act.activation(hid[:, b % 2, c, :], ps[:, i % 2, :], ACT.Relu, bias=col[:, FB + c:FB + c + 1]) \
                    .then_inc(S["hid_free"], 1)
            if b:
                root(QT * (b - 1), QT * b)
        root(QT * (NBLK - 1), TILES)

    @block.tensor
    def _(pe):
        def turn_normed(layer):
            for b in range(NBLK):
                pe.wait_ge(S["normed"], NBLK * layer + b + 1)
                for t in range(QT):
                    last = pe.transpose(ps[:, b, t * P:(t + 1) * P], normed_x[:, QT * b + t, :], ident[:, :])
                last.then_inc(S["turned"], 1)

        pe.wait_ge(S["const_in"], 16)
        turn_normed(0)

        pe.wait_ge(S["w0_in"], 16 * 6)
        for n in range(3 * NBLK):
            bank = ps[:, n % 4, :]
            pe.wait_ge(S["turn_copied"], NBLK)
            need(pe, S["l_free"], n - 3)
            if n < 2 * NBLK:
                w, b = (w_k, n) if n < NBLK else (w_q, n - NBLK)
                pe.matmul(bank, w[:, 0, :], xT[:, b * BLK:(b + 1) * BLK], start=True, stop=True) \
                    .then_inc(S["l_full"], 1)
            else:
                for t in range(QT):
                    j = QT * (n - 2 * NBLK) + t
                    last = pe.matmul(bank[:, t * P:(t + 1) * P], xT[:, j * P:(j + 1) * P], w_v[:, 0, :],
                                     start=True, stop=True)
                last.then_inc(S["l_full"], 1)

        pe.wait_ge(S["consts_made"], 2)
        pe.wait_ge(S["l_free"], 3 * NBLK)
        pe.wait_ge(S["l_k_in"], 16 * (1 + len(TERMS[0])))
        pe.wait_ge(S["l_q_in"], 16 * (1 + len(TERMS[0])))
        pe.wait_ge(S["rows_ready"], 2)
        pe.wait_ge(S["q_rows_ready"], 2)

        def local_maxes(n, t, grp, i):
            need(pe, S["l_neg"], n - 1)
            for h in range(4):
                at = bass.ds((4 * grp + h) * N + t * P, P)
                last = pe.matmul(ps[:, L_MAXES + i, h * P:(h + 1) * P], q_loc[0:M_ROW, at], kst[0:M_ROW, at],
                                 start=True, stop=True)
            last.then_inc(S["l_scores"], 1)

        def local_rows(n, i):
            pe.wait_ge(S["l_maxparts"], n + 1)
            need(pe, S["l_rows_in"], n - 1)
            for h in range(4):
                last = pe.matmul(ps[M_ROW:K_ROWS, 2 + i, h * P:(h + 1) * P], max_parts[:, i, h, :], ident_b[:, :],
                                 start=True, stop=True)
            last.then_inc(S["l_rows"], 1)

        def local_scores(n, t, grp, i):
            pe.wait_ge(S["l_rows_in"], n + 1)
            need(pe, S["l_exp"], n - 1)
            for h in range(4):
                at = bass.ds((4 * grp + h) * N + t * P, P)
                last = pe.matmul(ps[:, i, h * P:(h + 1) * P], kst[0:K_ROWS, at], q_loc[0:K_ROWS, at],
                                 start=True, stop=True)
            last.then_inc(S["l_st"], 1)

        def local_values(n, i):
            pe.wait_ge(S["l_exp"], n + 1)
            pe.wait_ge(S["l_vnow"], n + 1)
            need(pe, S["l_acc"], n - 1)
            for h in range(4):
                last = pe.matmul(ps[VW * h:VW * (h + 1), ACC + i, 0:P], v_now[i][:, h, :],
                                 l_probs[i][:, h * P:(h + 1) * P], start=True, stop=True)
            last.then_inc(S["l_pv"], 1)

        for grp in range(L0_HEADS // 4):
            n0 = grp * TILES

            def step(t, i, grp=grp, n0=n0, first=False, last=False):
                if not (first and t < 2) and not (last and t > TILES + 1):
                    local_rows(n0 + t - 2, i)
                if not last and not (first and t < 2 and grp):
                    local_maxes(n0 + t, t, grp, i)
                if last and t < TILES + 2 and grp < L0_HEADS // 4 - 1:
                    local_maxes(n0 + t, t - TILES, grp + 1, i)
                if not (first and t < 4):
                    local_values(n0 + t - 4, i)
                if not (first and t < 3) and not (last and t > TILES + 2):
                    local_scores(n0 + t - 3, t - 3, grp, 1 - i)

            peeled = 8 if grp == 0 else 4
            for t in range(peeled):
                step(t, t % 2, first=True)
            with pe.Fori(peeled // 4, TILES // 4) as quad:
                for i in range(4):
                    step(4 * quad + i, i % 2)
            for t in range(TILES, TILES + 4):
                step(t, t % 2, last=True)
            pe.wait_ge(S["l_acc"], n0 + TILES)
            strided = ob[:, :].rearrange("p (b j) -> p j b", j=L0_SPAN)
            for j in range(L0_SPAN):
                if j % 4 == 0:
                    need(pe, S["l_normed"], 4 * (grp - 1) + j // 4 + 1)
                last = pe.transpose(ps[:, j // 4, (j % 4) * P:(j % 4 + 1) * P], strided[:, j, :], ident[:, :])
                if j % 4 == 3:
                    last.then_inc(S["l_turned"], 1)
            pe.wait_ge(S["l_normed"], 4 * (grp + 1))

        turn_normed(1)

        def start_job(job):
            need(pe, S["misc_free"], job)

        def fold(u, i, job):
            pe.wait_ge(S["acc_copied"], u + 1)
            start_job(job)
            for t in range(QT):
                last = pe.transpose(misc[:, t * P:(t + 1) * P], o_part[:, i, t * P:(t + 1) * P], ident[:, :])
            last.then_inc(S["misc_full"], 1)

        def turn(units, job):
            pe.wait_ge(S["heads_normed"], units)
            start_job(job)
            for t in range(QT):
                last = pe.transpose(misc[:, t * P:(t + 1) * P], o_tok[:, t, :], ident[:, :])
            last.then_inc(S["misc_full"], 1)

        def project(w, rhs, job):
            start_job(job)
            pe.matmul(misc, w, rhs, start=True, stop=True).then_inc(S["misc_full"], 1)

        def project_tiles(lhs_tiles, w, job):
            start_job(job)
            for t in range(QT):
                last = pe.matmul(misc[:, t * P:(t + 1) * P], lhs_tiles[:, t * P:(t + 1) * P], w, start=True, stop=True)
            last.then_inc(S["misc_full"], 1)

        def out_job(kind, node, job):
            if kind == "nas":
                pe.wait_ge(S["node_weights_in"], node_weights_count(node))
                project(w_o[:, node % 2, :], o_chan, job)
            else:
                project_tiles(o_chan, w_o[:, 0, :], job)

        def rows_job(u, i, job):
            pe.wait_ge(S["maxparts_ready"], u + 1)
            start_job(job)
            for t in range(QT):
                last = pe.matmul(misc[M_ROW:K_ROWS, t * P:(t + 1) * P], max_parts[:, i, t, :], ident_b[:, :],
                                 start=True, stop=True)
            last.then_inc(S["misc_full"], 1)

        def max_tile(u, i, slot, k_base):
            q_tile, key_block = MAX_TILE[i]
            need(pe, S["tile_done"], 16 * u + i - TAKEN[i] + 1)
            q0 = slot * BLK + q_tile * P
            at = k_base + key_block * BLK
            keys = kst[0:M_ROW, at:at + BLK] if isinstance(at, int) else kst[0:M_ROW, bass.ds(at, BLK)]
            pe.matmul(ps[:, MAXES + BANK[i], :], qst[0:M_ROW, q0:q0 + P], keys, start=True, stop=True) \
                .then_inc(S["tile_ready"], 1)

        for x in PLAN:
            kind = x.kind
            if isinstance(x, Prep):
                if kind == "rot":
                    turn_normed(2)
                    pe.wait_ge(S["turn_copied"], NBLK * 3)
                    pe.wait_ge(S["rot_in"], 16 * 8)
                    pe.wait_ge(S["rot_swapped"], 2)
                if kind == "nas" and x.has_keys:
                    pe.wait_ge(S["turn_copied"], NBLK * 2)
                    pe.wait_ge(S["q_weights_in"], 64)
                    pe.wait_ge(S["node_weights_in"], 64)
                if not x.has_keys:
                    pe.wait_ge(S["misc_free"], x.before["job"])
                    pe.wait_ge(S["exp_done"], 16 * x.before["unit"])
                for name, b, n in x.numbered():
                    need(pe, prep_free[n % 4], n // 4)
                    if kind == "nas":
                        if name == "q2":
                            pe.wait_ge(prep_free[x.at["q1", 0] % 4], x.at["q1", 0] // 4 + 1)
                        if name in ("k2", "v2"):
                            first = x.at[name[0] + "1", b]
                            pe.wait_ge(prep_free[first % 4], first // 4 + 1)
                    bank = ps[:, n % 4, :]
                    w = {"q": w_q, "k": w_k, "v": w_v}[name[0]][:, int(name[1]) - 1, :]
                    if name == "v2":
                        src = prep_edges[b] if kind == "nas" else xT[:, b * BLK:(b + 1) * BLK]
                        w = w_v[:, 1, :] if kind == "nas" else w_v[:, 0, :]
                        for t in range(QT):
                            last = pe.matmul(bank[:, t * P:(t + 1) * P], src[:, t * P:(t + 1) * P], w,
                                             start=True, stop=True)
                    elif kind == "rot":
                        last = pe.matmul(bank, w, xT[:, b * BLK:(b + 1) * BLK], start=True, stop=True)
                    elif name[1] == "1":
                        source = -1 if name == "q1" else NODE[x.node][name[0]]
                        last = pe.matmul(bank, w, nodes[:, node_col(source, b):node_col(source, b) + BLK],
                                         start=True, stop=True)
                    else:
                        src = nodes[:, node_col(0):node_col(0) + BLK] if name == "q2" else prep_edges[b]
                        last = pe.matmul(bank, w, src, start=True, stop=True)
                    last.then_inc(S["prep_full"], 1)
                for k in range(4):
                    done = sum(n % 4 == k for n in range(x.before["prep"] + len(x.jobs)))
                    pe.wait_ge(prep_free[k], done)
                continue
            if isinstance(x, Serial):
                job = x.before["job"]
                u0 = x.before["unit"]
                for name, b in x.jobs:
                    if name == "fold":
                        fold(u0 - 1, 1, job)
                    if name == "turn":
                        turn(u0, job)
                    if name == "out":
                        out_job(kind, x.node, job)
                    if name == "prime":
                        pe.wait_ge(S["rows_ready"], 2)
                        pe.wait_ge(S[f"{kind}_qa_in"], 16 * n_terms)
                        pe.wait_ge(S[f"{kind}_k_in"], 16 * n_terms)
                        for i in range(16):
                            if i == 8:
                                pe.wait_ge(S["late_keys_in"], 16 * n_terms * (1 if kind == "nas" else 2))
                            max_tile(u0, i, 0, 0)
                        for i in range(8):
                            max_tile(u0 + 1, i, 1, N)
                        rows_job(u0, 0, job)
                    job += 1
                if kind == "nas" and x.jobs[0][0] == "fold" and x.node == NODES - 1:
                    pe.wait_ge(S["misc_free"], job)
                    for b in range(NBLK):
                        for t in range(QT):
                            at = (QT * b + t) * P
                            last = pe.transpose(ps[:, b, t * P:(t + 1) * P], xT[:, at:at + P], ident[:, :])
                        last.then_inc(S["cell_turned"], 1)
                continue

            def pv_quad(u, h, quad, c=x.node, kind=kind):
                pe.wait_ge(S["exp_done"], 16 * u + 4 * quad + 4)
                if quad == 0:
                    need(pe, S["acc_copied"], u)
                for k in range(4):
                    t = 4 * quad + k
                    value = v_nas[:, c % 2, t, h, :] if kind == "nas" else v_16[:, t, h, :]
                    last = pe.matmul(acc[VW * k:VW * (k + 1), :], value, probs[:, t % 8, :],
                                     start=(quad == 0), stop=(quad == 3), skip_group_check=True)
                last.then_inc(S["pv_done"], 1)

            def emit(b, x=x, kind=kind):
                c, heads, u0 = x.node, x.heads, x.unit(b)
                nt = 16 * n_terms
                par = (c % 2) * 8 if kind == "nas" else 0
                def score_tile(u, h, slot, i):
                    need(pe, S["exp_done"], 16 * u + i - TAKEN[i] + 1)
                    key0 = slot * N + i * P
                    pe.matmul(ps[:, BANK[i], :], kst[0:K_ROWS, key0:key0 + P],
                              qst[0:K_ROWS, h * BLK:(h + 1) * BLK], start=True, stop=True).then_inc(S["st_ready"], 1)

                for h in range(heads):
                    u = u0 + h
                    slot = par + h
                    for s in range(8):
                        if s == 0:
                            pe.wait_ge(S["misc_free"], x.job(b, h - 1, ROWS_STEP) + 1 if h
                                       else x.jobs_so_far(b, 0, 0) - x.late_before)
                        if s == 3 and h == 0:
                            pe.wait_ge(S["misc_free"], x.jobs_so_far(b, 0, 0))
                        score_tile(u, h, slot, 2 * s)
                        ahead, first = maxima_of(s)
                        v, hv = u + ahead, h + ahead
                        needed = not (x.last and hv >= heads)
                        if needed:
                            wraps = hv >= heads
                            hv %= heads
                            if first == 0 and hv == 0 and wraps:
                                pe.wait_ge(S[f"{kind}_qa_in"], nt * (x.body(b) + 2))
                                if x.turns_over():
                                    pe.wait_ge(S["nas_k_in"], nt * (1 + NBLK * c + b + 1))
                            if first == 0 and hv == heads // 2 and not wraps:
                                pe.wait_ge(S[f"{kind}_qb_in"], nt * (x.body(b) + 1))
                            base = (x.pick(b, par, 8 - par) if wraps else par) + hv
                            max_tile(v, first, hv, base * N)
                        if s == 1 and h:
                            pv_quad(u - 1, h - 1, 3)
                        if s == 1 and h == 0 and x.with_out:
                            pv_quad(u - 1, heads - 1, 3, c=c if x.b0 else c - 1)
                        if s % 2 == 1 and s > 1:
                            pv_quad(u, h, s // 2 - 1)
                        score_tile(u, h, slot, 2 * s + 1)
                        if needed:
                            max_tile(v, first + 1, hv, base * N)
                        name = x.jobs.get((h, s))
                        if name:
                            job = x.job(b, h, s)
                        if name == "fold":
                            if h:
                                fold(u - 1, (h - 1) % 2, job)
                            else:
                                fold(u - 1, 1, job)
                        if name == "turn":
                            turn(u0, job)
                        if name == "out":
                            out_job(kind, x.out_of(b)[0], job)
                        if name == "rows":
                            rows_job(u + 1, (h + 1) % 2, job)
                        if name in ("q1", "q2") and kind == "rot":
                            project(w_q[:, 0 if name == "q1" else 1, :], xT[:, bass.ds((b + 1) * BLK, BLK)], job)
                        if kind == "nas":
                            if name == "q1":
                                pe.wait_ge(S["q_weights_in"], 64 * (x.body(b) + 2))
                                at = in_nodes(x.pick(b, node_col(c - 1), node_col(c) - NBLK * BLK) + (b + 1) * BLK)
                                project(w_q[:, 0, :], nodes[:, bass.ds(at, BLK)], job)
                            if name == "q2":
                                at = next_block(x, b)
                                project(w_q[:, 1, :], nodes[:, bass.ds(at, BLK)], job)
                            if name == "k1":
                                pe.wait_ge(S["node_weights_in"], 64 + 80 * (c + 1))
                                project(w_k[:, 0, :], nodes[:, bass.ds(node_col(NODE[c + 1]["k"]) + b * BLK, BLK)], job)
                            if name == "k2":
                                project(w_k[:, 1, :], t_tmp[:, :], job)
                            if name == "v1":
                                project(w_v[:, 0, :], nodes[:, bass.ds(node_col(NODE[c + 1]["v"]) + b * BLK, BLK)], job)
                            if name == "v2":
                                project_tiles(t_tmp[:, :], w_v[:, 1, :], job)

            each_block(pe, x, emit)
            if not x.goes_on:
                pv_quad(x.unit(x.b1) - 1, x.heads - 1, 3)

        turn_normed(3)
        pe.wait_ge(S["turn_copied"], NBLK * 4)
        pe.wait_ge(S["mlp_in"], 16 * 9)
        for k in range(2):
            for t in range(8):
                j = 8 * k + t
                last = pe.matmul(ps[:, k, t * GA:(t + 1) * GA], xT[:, j * P:(j + 1) * P], gate_a, start=True, stop=True)
            last.then_inc(S["gates_ready"], 1)
        pe.wait_ge(S["gates_copied"], 2)
        for b in range(NBLK):
            for t in range(QT):
                last = pe.transpose(ps[0:EXPERTS * RANK, 2 + b, t * P:(t + 1) * P], low[:, QT * b + t, :], ident[:, :])
            last.then_inc(S["low_turned"], 1)

        def mlp_out(b):
            pe.wait_ge(S["hid_free"], FC * (b + 1))
            need(pe, S["mlp_free"], b - 1)
            for t in range(QT):
                for c in range(FC):
                    at = slice(t * P, (t + 1) * P)
                    last = pe.matmul(ps[:, 6 + b % 2, at], hid[:, b % 2, c, at], wo[:, c, :],
                                     start=(c == 0), stop=(c == FC - 1))
            last.then_inc(S["mlp_full"], 1)

        pe.wait_ge(S["low_cleared"], 2)
        for b in range(NBLK):
            pe.wait_ge(S["low_copied"], b + 1)
            for c in range(FC):
                i = FC * b + c
                need(pe, S["hid_free"], i - 1)
                pe.matmul(ps[:, i % 2, :], wi[:, c * P:(c + 1) * P], xT[:, b * BLK:(b + 1) * BLK],
                          start=True, stop=False)
                pe.matmul(ps[:, i % 2, :], lora_b[:, c * P:(c + 1) * P], low_T[:, b * BLK:(b + 1) * BLK],
                          start=False, stop=True).then_inc(S["hid_full"], 1)
            if b:
                mlp_out(b - 1)
        mlp_out(NBLK - 1)

    @block.vector
    def _(dve):
        steps = [0]

        def link(ins):
            steps[0] += 1
            ins.then_inc(S["dve_step"], 1)
            dve.wait_ge(S["dve_step"], steps[0])

        norms = [0]

        def measure(src, t0, t1):
            for t in range(t0, t1):
                last = dve.bn_stats(stats[:, t, :], src[:, t, :])
            link(last)
            for t in range(t0, t1):
                last = dve.bn_aggr(mean_var[:, t, :], stats[:, t, :])
            link(last)

        def inverse_root(eps, t0=0, t1=TILES):
            v, root, y = (rstd[:, i, t0:t1] for i in range(3))
            dve.tensor_scalar(v, mean_var[:, t0:t1, 1], eps, None, ALU.add).then_inc(S["var_ready"], 1)
            norms[0] += 1
            dve.wait_ge(S["std_ready"], norms[0])
            link(dve.reciprocal(y, root))
            link(dve.tensor_tensor(root, y, y, ALU.mult))
            link(dve.tensor_tensor(root, root, v, ALU.mult))
            link(dve.tensor_scalar(root, root, -0.5, 1.5, ALU.mult, ALU.add))
            link(dve.tensor_tensor(y, y, root, ALU.mult))

        def center(dst, src, t):
            return dve.tensor_scalar(dst[:, t, :], src[:, t, :], mean_var[:, t, 0:1], rstd[:, 2, t:t + 1],
                                     ALU.subtract, ALU.mult)

        def norm_for_turn():
            measure(x_res, 0, TILES)
            inverse_root(1e-5)
            for b in range(NBLK):
                for t in range(QT * b, QT * (b + 1)):
                    last = center(normed_x, x_res, t)
                last.then_inc(S["normed"], 1)

        def norm_in_place(y, eps, t0=0, t1=TILES, measured=0):
            measure(y, max(t0, measured), t1)
            inverse_root(eps, t0, t1)
            for t in range(t0, t1):
                last = center(y, y, t)
            link(last)

        def add_to_stream(y):
            link(dve.tensor_tensor(x_res[:, :, :], x_res[:, :, :], y[:, :, :], ALU.add))

        def spread(row, n):
            return row.unsqueeze(1).to_broadcast([P, n, row.shape[1]])

        link(dve.memset(vst[:, :], 0.0))
        link(dve.memset(v_cols[:, :, L0_DIM:L0_DIM + 1], 1.0))
        dve.wait_ge(S["const_in"], 16)
        dve.tensor_copy(ident_b[:, :], ident[:, :]).then_inc(S["consts_made"], 1)
        dve.wait_ge(S["small_in"], 16)
        dve.tensor_copy(blocks_b[:, :, :].rearrange("p a n -> p (a n)"), t_tmp[0:P // L0_SPAN, 0:2 * P]) \
            .then_inc(S["consts_made"], 1)
        dve.wait_ge(S["x_in"], 16)
        norm_for_turn()

        dve.wait_ge(S["w0_in"], 16 * 6)
        dve.wait_ge(S["turned"], NBLK)
        for n in range(2 * NBLK):
            dve.wait_ge(S["l_full"], n + 1)
            need(dve, l_parts_sent[n % 4], 16 * (n // 4))
            need(dve, S["l_parts_ready"], n)
            three = local_parts[n % 4]
            bias = col[:, LB + 1:LB + 2] if n < NBLK else col[:, LB:LB + 1]
            dve.tensor_scalar(rest[:, :], ps[:, n % 4, :], bias, None, ALU.add).then_inc(S["l_free"], 1)
            dve.wait_ge(S["l_free"], n + 1)
            link(dve.tensor_copy(three[:, 0, :], rest[:, :]))
            link(dve.tensor_tensor(rest[:, :], rest[:, :], three[:, 0, :], ALU.subtract))
            link(dve.tensor_copy(three[:, 1, :], rest[:, :]))
            dve.tensor_tensor(three[:, 2, :], rest[:, :], three[:, 1, :], ALU.subtract) \
                .then_inc(S["l_parts_ready"], 1)
        for b in range(NBLK):
            n = 2 * NBLK + b
            dve.wait_ge(S["l_full"], n + 1)
            dve.tensor_tensor(v_16[:, QT * b:QT * (b + 1), :, 0:L0_DIM],
                              ps[:, n % 4, :].rearrange("p (t h d) -> p t h d", t=QT, d=L0_DIM),
                              w_o[:, 0, :].rearrange("p (h d) -> p h d", d=L0_DIM).unsqueeze(1)
                              .to_broadcast([P, QT, L0_HEADS, L0_DIM]), ALU.add).then_inc(S["l_free"], 1)
        dve.wait_ge(S["l_free"], 3 * NBLK)
        for sent in l_parts_sent:
            dve.wait_ge(sent, 16 * 2)
        dve.wait_ge(S["l_parts_ready"], 2 * NBLK)

        def local_max(n, i):
            dve.wait_ge(S["l_scores"], n + 1)
            need(dve, S["l_maxparts"], n - 1)
            dve.tensor_reduce(neg_max[:, i, :], ps[:, L_MAXES + i, :].rearrange("p (h k) -> p h k", h=4), AX.X, ALU.max,
                              negate=True).then_inc(S["l_neg"], 1)

        def local_vnow(n, t, grp, i):
            need(dve, S["l_pv"], n - 1)
            if isinstance(t, int):
                src = v_16[:, t, 4 * grp:4 * grp + 4, :].rearrange("p h w -> p (h w)")
            else:
                src = vst[:, bass.ds(t * (16 * VW) + 4 * grp * VW, 4 * VW)]
            dve.tensor_scalar((w_q, w_k)[i][:, 0, :], src, 1.0, None, ALU.mult).then_inc(S["l_vnow"], 1)

        def local_acc(n, t, i):
            dve.wait_ge(S["l_pv"], n + 1)
            dve.tensor_scalar(ob[:, bass.ds(t * P, P)], ps[:, ACC + i, 0:P], 1.0, None, ALU.mult) \
                .then_inc(S["l_acc"], 1)

        for grp in range(L0_HEADS // 4):
            n0 = grp * TILES

            def step(t, i, grp=grp, n0=n0, first=False, last=False):
                if not (last or first and t < 2 and grp) or last and t < TILES + 2 and grp < L0_HEADS // 4 - 1:
                    local_max(n0 + t, i)
                if not (first and t < 4):
                    local_acc(n0 + t - 4, t - 4, i)
                if not (first and t < 3) and not (last and t > TILES + 2):
                    local_vnow(n0 + t - 3, t - 3, grp, 1 - i)

            for t in range(8):
                step(t, t % 2, first=True)
            with dve.Fori(2, TILES // 4) as quad:
                for i in range(4):
                    step(4 * quad + i, i % 2)
            for t in range(TILES, TILES + 4):
                step(t, t % 2, last=True)
            for k in range(4):
                dve.wait_ge(S["l_turned"], 4 * grp + k + 1)
                view = ps[:, k, :].rearrange("p (j h w) -> p j h w", j=4, w=VW)
                r = recip[:, :].rearrange("p (j h) -> p j h", j=4)
                link(dve.reciprocal(r, view[:, :, :, L0_DIM]))
                dst = att[:, 4 * grp:4 * grp + 4, 4 * k * L0_DIM:4 * (k + 1) * L0_DIM] \
                    .rearrange("p h (j d) -> p j h d", d=L0_DIM)
                dve.tensor_tensor(dst, view[:, :, :, 0:L0_DIM], r.unsqueeze(3).to_broadcast([P, 4, 4, L0_DIM]),
                                  ALU.mult).then_inc(S["l_normed"], 1)
                dve.wait_ge(S["l_normed"], 4 * grp + k + 1)

        norm_in_place(att, 1e-5)
        add_to_stream(att)
        norm_for_turn()
        link(dve.memset(v_cols[:, :, NAS_DIM:NAS_DIM + 1], 1.0))
        dve.wait_ge(S["nas_cols_in"], 48)
        dve.wait_ge(S["q_weights_in"], 64)
        for c in range(NODES):
            for i, e in enumerate(("ek", "ev")):
                at = EB + 2 * c + i
                dve.tensor_tensor(col[:, at:at + 1], col[:, BE + NODE[c][e]:BE + NODE[c][e] + 1],
                                  col[:, EW + 3 * c + 1 + i:EW + 3 * c + 2 + i], ALU.mult) \
                    .then_inc(S["edges_ready"], 1)

        def max_tile(u, i, par):
            dve.wait_ge(S["tile_ready"], 16 * u + i + 1)
            q_tile, key_block = MAX_TILE[i]
            at = 4 * q_tile + key_block
            dve.tensor_reduce(row_max[:, par, at:at + 1], ps[:, MAXES + BANK[i], :], AX.X, ALU.max) \
                .then_inc(S["tile_done"], 1)
            if i == 15:
                dve.wait_ge(S["tile_done"], 16 * u + 16)
                need(dve, S["maxparts_ready"], u - 1)
                dve.tensor_reduce(neg_max[:, par, :], row_max[:, par, :].rearrange("p (t k) -> p t k", k=4), AX.X,
                                  ALU.max, negate=True).then_inc(S["neg_ready"], 1)

        def fold_sum(kind, u, job):
            d = dims[kind]
            dve.wait_ge(S["misc_full"], job + 1)
            need(dve, S["heads_normed"], u)
            dve.tensor_reduce(sums[:, :, 0:d + 1], misc.rearrange("p (t g w) -> p t w g", t=QT, w=VW)[:, :, 0:d + 1, :],
                              AX.X, ALU.add).then_inc(S["misc_free"], 1)

        def fold_recip(kind, u, job):
            dve.wait_ge(S["misc_free"], job + 1)
            dve.reciprocal(recip[:, 0:QT], sums[:, :, dims[kind]]).then_inc(S["heads_recip"], 1)

        def fold_scale(kind, u, h):
            d = dims[kind]
            dve.wait_ge(S["heads_recip"], u + 1)
            dve.tensor_tensor(o_tok[:, :, h * d:(h + 1) * d], sums[:, :, 0:d],
                              recip[:, 0:QT].unsqueeze(2).to_broadcast([P, QT, d]), ALU.mult) \
                .then_inc(S["heads_normed"], 1)

        def out_job(kind, node, at, b, job):
            dve.wait_ge(S["misc_full"], job + 1)
            if kind == "nas":
                dst = nodes[:, bass.ds(at, BLK)]
                dve.scalar_tensor_tensor(dst, misc, col[:, AW + node:AW + node + 1], dst, ALU.mult, ALU.add) \
                    .then_inc(S["misc_free"], 1)
            else:
                dst = big[:, bass.ds(N + b * BLK, BLK)].rearrange("p (t d) -> p t d", d=D)
                dve.tensor_tensor(dst, misc.rearrange("p (t d) -> p t d", d=D), spread(rows[:, 1, :], QT), ALU.add) \
                    .then_inc(S["misc_free"], 1)

        def edge(dst, be, ew, job):
            dve.wait_ge(S["misc_full"], job + 1)
            dve.tensor_scalar(dst, misc, be, ew, ALU.add, ALU.mult).then_inc(S["misc_free"], 1)

        def rest_part(job, split):
            dve.wait_ge(S["high_ready"], split + 1)
            dve.tensor_tensor(rest[:, :], misc, parts[:, 0, :], ALU.subtract).then_inc(S["misc_free"], 1)

        def rotate_a(blk, bias, job):
            dve.wait_ge(S["misc_full"], job + 1)
            dve.scalar_tensor_tensor(rot_a, misc, bias, cos[:, bass.ds(blk * BLK, BLK)], ALU.add, ALU.mult) \
                .then_inc(S["misc_free"], 1)

        def rotate_b(blk, bias, job, split):
            k = split - rot_split0
            dve.wait_ge(S["misc_full"], job + 1)
            dve.scalar_tensor_tensor(rot_b, misc, bias, sin[:, bass.ds(blk * BLK, BLK)], ALU.add, ALU.mult) \
                .then_inc(S["misc_free"], 1)
            dve.wait_ge(S["misc_free"], job + 1)
            dve.tensor_tensor(rot_sum, rot_a, rot_b, ALU.add).then_inc(S["rot_sum_done"], 1)
            dve.wait_ge(S["rot_sum_done"], k + 1)
            need(dve, S["parts_sent"], 16 * split)
            dve.tensor_copy(parts[:, 0, :], rot_sum).then_inc(S["rot_high_ready"], 1)
            dve.wait_ge(S["rot_high_ready"], k + 1)
            dve.tensor_tensor(rest[:, :], rot_sum, parts[:, 0, :], ALU.subtract).then_inc(S["rest_ready"], 1)
            dve.wait_ge(S["rest_ready"], k + 1)
            dve.tensor_copy(parts[:, 1, :], rest[:, :]).then_inc(S["mid_ready"], 1)
            dve.wait_ge(S["mid_ready"], split + 1)
            dve.tensor_tensor(parts[:, 2, :], rest[:, :], parts[:, 1, :], ALU.subtract).then_inc(S["parts_ready"], 1)

        preps_done = sums_done = 0
        for x in PLAN:
            kind = x.kind
            if isinstance(x, Prep):
                if kind == "rot":
                    dve.wait_ge(S["rot_in"], 16 * 8)
                    dve.wait_ge(S["rot_rows_in"], 32)
                    for w in (w_q, w_k):
                        a = w[:, 0, :].rearrange("p (h a r) -> p h a r", a=2, r=ROT_DIM // 2)
                        z = w[:, 1, :].rearrange("p (h a r) -> p h a r", a=2, r=ROT_DIM // 2)
                        for i in range(2):
                            last = dve.tensor_copy(z[:, :, i, :], a[:, :, 1 - i, :])
                        last.then_inc(S["rot_swapped"], 1)
                    dve.wait_ge(S["pads_ready"], ROT_PADS)
                splits = (1 + NBLK) * preps_done
                for name, b, n in x.numbered():
                    bank = ps[:, n % 4, :]
                    if kind == "rot" or name in ("q1", "q2", "k2"):
                        dve.wait_ge(S["prep_full"], n + 1)
                    if kind == "nas" and name == "q1":
                        at = node_col(0)
                        dve.tensor_scalar(nodes[:, at:at + BLK], bank, col[:, QBE:QBE + 1], col[:, QEW:QEW + 1],
                                          ALU.add, ALU.mult).then_inc(prep_free[n % 4], 1)
                    if kind == "rot" and name == "v2":
                        dve.tensor_tensor(v_16[:, QT * b:QT * (b + 1), :, 0:ROT_DIM],
                                          bank.rearrange("p (t h d) -> p t h d", t=QT, d=ROT_DIM),
                                          rows[:, 0, :].rearrange("p (h d) -> p h d", d=ROT_DIM).unsqueeze(1)
                                          .to_broadcast([P, QT, ROT_HEADS, ROT_DIM]), ALU.add) \
                            .then_inc(prep_free[n % 4], 1)
                    if kind == "rot" and name in ("q1", "k1"):
                        bias = RB if name == "q1" else RB + 2
                        dve.scalar_tensor_tensor(rot_a, bank, col[:, bias:bias + 1], cos[:, b * BLK:(b + 1) * BLK],
                                                 ALU.add, ALU.mult).then_inc(prep_free[n % 4], 1)
                    if name in ("q2", "k2"):
                        three = prep_parts[b + (name == "k2")]
                        if kind == "rot":
                            bias = RB + 1 if name == "q2" else RB + 3
                            dve.scalar_tensor_tensor(rot_b, bank, col[:, bias:bias + 1],
                                                     sin[:, b * BLK:(b + 1) * BLK], ALU.add, ALU.mult) \
                                .then_inc(prep_free[n % 4], 1)
                            dve.wait_ge(prep_free[n % 4], n // 4 + 1)
                            total = rot_sums[sums_done % 2]
                            dve.tensor_tensor(total, rot_a, rot_b, ALU.add).then_inc(S["prep_sum_ready"], 1)
                            sums_done += 1
                            dve.wait_ge(S["prep_sum_ready"], sums_done)
                        dve.wait_ge(S["prep_high_ready"], splits + 1)
                        if kind == "rot":
                            link(dve.tensor_tensor(rest[:, :], total, three[:, 0, :], ALU.subtract))
                        else:
                            dve.tensor_tensor(rest[:, :], bank, three[:, 0, :], ALU.subtract) \
                                .then_inc(prep_free[n % 4], 1)
                            dve.wait_ge(prep_free[n % 4], n // 4 + 1)
                        link(dve.tensor_copy(three[:, 1, :], rest[:, :]))
                        dve.tensor_tensor(three[:, 2, :], rest[:, :], three[:, 1, :], ALU.subtract) \
                            .then_inc(S["prep_parts_ready"], 1)
                        splits += 1
                        dve.wait_ge(S["prep_parts_ready"], splits)
                preps_done += x.has_keys
                continue
            if isinstance(x, Serial):
                job, u0 = x.before["job"], x.before["unit"]
                for name, b in x.jobs:
                    c = x.node
                    if name == "fold":
                        fold_sum(kind, u0 - 1, job)
                        fold_recip(kind, u0 - 1, job)
                        fold_scale(kind, u0 - 1, heads_of[kind] - 1)
                        if kind == "rot":
                            dve.wait_ge(S["misc_free"], x.before["job"])
                            measure(tok, 0, QT * (NBLK - 1))
                    if name == "out":
                        out_job(kind, c, node_col(c, b), b, job)
                    if name == "prime":
                        for i in range(16):
                            max_tile(u0, i, 0)
                        for i in range(8):
                            max_tile(u0 + 1, i, 1)
                    job += 1
                if kind == "nas" and x.jobs[0][0] == "fold" and c == NODES - 1:
                    dve.wait_ge(S["cell_copied"], NBLK)
                    dve.wait_ge(S["norm_rows_in"], 32)
                    norm_in_place(tok, 1e-6)
                    link(dve.tensor_tensor(tok, tok, spread(t_tmp[:, 0:D], TILES), ALU.mult))
                    link(dve.tensor_tensor(tok, tok, spread(t_tmp[:, D:2 * D], TILES), ALU.add))
                    norm_in_place(tok, 1e-5)
                    add_to_stream(tok)
                    norm_for_turn()
                continue

            def emit(b, x=x, kind=kind):
                c, heads, u0 = x.node, x.heads, x.unit(b)
                for h in range(heads):
                    u = u0 + h
                    for s in range(8):
                        ahead, first = maxima_of(s)
                        for k in range(2):
                            if not (x.last and h + ahead >= heads):
                                max_tile(u + ahead, first + k, (h + ahead) % 2)
                            name, hj, sj = x.job_before(h, s, k, 0)
                            if name:
                                job = x.job(b, hj, sj)
                            if name == "fold":
                                fold_sum(kind, u0 + hj - 1, job)
                            if name == "out":
                                node, blk = x.out_of(b)
                                out_job(kind, node, node_col(node) + blk * BLK, blk, job)
                            if name == "q1" and kind == "rot":
                                rotate_a(b + 1, col[:, RB:RB + 1], job)
                            if name == "q2" and kind == "rot":
                                rotate_b(b + 1, col[:, RB + 1:RB + 2], job, x.q_split(b))
                            if name == "q1" and kind == "nas":
                                edge(nodes[:, bass.ds(next_block(x, b), BLK)], col[:, QBE:QBE + 1],
                                     col[:, QEW:QEW + 1], job)
                            if name == "q2" and kind == "nas":
                                rest_part(job, x.q_split(b))
                            if name == "k2":
                                rest_part(job, x.k_split(b))
                            name, hj, sj = x.job_before(h, s, k, 1)
                            if name == "fold":
                                fold_recip(kind, u0 + hj - 1, x.job(b, hj, sj))
                            name, hj, sj = x.job_before(h, s, k, 2)
                            if name == "fold":
                                fold_scale(kind, u0 + hj - 1, (hj - 1) % heads)

            each_block(dve, x, emit)

        dve.wait_ge(S["misc_free"], job)
        norm_in_place(tok, 1e-5, measured=QT * (NBLK - 1))
        add_to_stream(tok)
        norm_for_turn()

        dve.wait_ge(S["mlp_in"], 16 * 9)
        for k in range(2):
            dve.wait_ge(S["gates_ready"], k + 1)
            view = ps[:, k, 0:8 * GA].rearrange("p (t e) -> p t e", e=GA)
            link(dve.tensor_tensor(logits[:, 8 * k:8 * k + 8, :], view[:, :, 0:EXPERTS], spread(gate_bias, 8), ALU.add))

        def wide(v):
            return v.unsqueeze(2).to_broadcast([P, TILES, EXPERTS])

        link(dve.tensor_reduce(top, logits, AX.X, ALU.max))
        link(dve.tensor_tensor(chosen, logits, wide(top), ALU.is_equal))
        link(dve.tensor_tensor(chosen, chosen, spread(rank_row, TILES), ALU.mult))
        link(dve.tensor_reduce(top, chosen, AX.X, ALU.max))
        link(dve.tensor_tensor(chosen, chosen, wide(top), ALU.is_equal))
        for k in range(2):
            view = ps[:, k, 0:8 * GA].rearrange("p (t e) -> p t e", e=GA)[:, :, EXPERTS:GA] \
                .rearrange("p t (e r) -> p t e r", r=RANK)
            dve.tensor_tensor(low[:, 8 * k:8 * k + 8, :].rearrange("p t (e r) -> p t e r", r=RANK), view,
                              chosen[:, 8 * k:8 * k + 8, :].unsqueeze(3).to_broadcast([P, 8, EXPERTS, RANK]),
                              ALU.mult).then_inc(S["gates_copied"], 1)
        for b in range(NBLK):
            at = slice(QT * b, QT * (b + 1))
            dve.wait_ge(S["mlp_full"], b + 1)
            dve.tensor_tensor(tok[:, at, :], ps[:, 6 + b % 2, :].rearrange("p (t d) -> p t d", d=D),
                              spread(wo_bias, QT), ALU.add).then_inc(S["mlp_free"], 1)
            dve.wait_ge(S["mlp_free"], b + 1)
            norm_in_place(tok, 1e-5, QT * b, QT * (b + 1))
            dve.tensor_tensor(x_res[:, at, :], x_res[:, at, :], tok[:, at, :], ALU.add).then_inc(S["out_ready"], 1)


def kernel(**inputs):
    import concourse.bacc as bacc
    from concourse.bass_utils import run_bass_kernel_spmd as run

    def get(name):
        return np.asarray(inputs[name])

    def heads_swapped(bias):
        return bias.reshape(ROT_HEADS, 2, ROT_DIM // 2)[:, ::-1, :].reshape(-1)

    in_block = np.equal.outer(np.arange(P // L0_SPAN), np.arange(P) // L0_SPAN).astype(np.float32)
    blocks = np.concatenate([in_block, (in_block - 1) * np.float32(1e30)], axis=1)
    half = ROT_DIM // 2
    inv = (np.float32(1.0) / np.float32(10000.0) ** (np.arange(half, dtype=np.float32) / np.float32(half))) \
        .astype(np.float32)
    angle = (inv[:, None] * np.arange(N, dtype=np.float32)[None, :]).astype(np.float32)
    cos = np.tile(np.cos(angle), (2 * ROT_HEADS, 1)).astype(np.float32)
    sin = np.tile(np.concatenate([-np.sin(angle), np.sin(angle)]), (ROT_HEADS, 1)).astype(np.float32)

    arrays = {
        "x": get("L0_attn_hidden_states"),
        "w_qkvT": get("L0_attn_w_qkv").T, "b_qkv": get("L0_attn_b_qkv"),
        "ew": get("L0_ffn_ew"), "act_w": get("L0_ffn_act_w"), "We": get("L0_ffn_We"), "be": get("L0_ffn_be"),
        "Wq": get("L0_ffn_Wq"), "Wk": get("L0_ffn_Wk"), "Wv": get("L0_ffn_Wv"), "Wo": get("L0_ffn_Wo"),
        "ln_g": get("L0_ffn_ln_g"), "ln_b": get("L0_ffn_ln_b"),
        "wq_w": get("L1_attn_wq_w"), "wk_w": get("L1_attn_wk_w"), "wv_w": get("L1_attn_wv_w"),
        "wo_w": get("L1_attn_wo_w"), "wq_b": get("L1_attn_wq_b"), "wk_b": get("L1_attn_wk_b"),
        "wq_b_swapped": heads_swapped(get("L1_attn_wq_b")), "wk_b_swapped": heads_swapped(get("L1_attn_wk_b")),
        "wv_b": get("L1_attn_wv_b"), "wo_b": get("L1_attn_wo_b"),
        "gate_T": get("L1_ffn_gate_W").T, "gate_b": get("L1_ffn_gate_b"),
        "wi_T": get("L1_ffn_wi_W").T, "wi_b": get("L1_ffn_wi_b"),
        "wo_T": get("L1_ffn_wo_W").T, "ffn_wo_b": get("L1_ffn_wo_b"),
        "lora_AT": get("L1_ffn_lora_A").reshape(EXPERTS * RANK, D).T,
        "lora_BT": get("L1_ffn_lora_B").transpose(0, 2, 1).reshape(EXPERTS * RANK, FF),
        "c_ident": np.eye(P, dtype=np.float32), "c_blocks": blocks,
        "c_cos": cos, "c_sin": sin,
        "c_rank": np.arange(EXPERTS, 0, -1, dtype=np.float32)[None, :],
    }
    nc = bacc.Bacc("TRN2", target_bir_lowering=False, num_devices=1)
    given, A = {}, {}
    for name, a in arrays.items():
        a = np.ascontiguousarray(a)
        given[f"in_{name}"] = a
        A[name] = nc.dram_tensor(f"in_{name}", a.shape, mybir.dt.from_np(a.dtype), kind="ExternalInput").ap()
    out = nc.dram_tensor("out", (1, N, D), F32, kind="ExternalOutput").ap()
    build(nc, A, out)
    r = run(nc, [given], core_ids=[0])
    return r.results[0]["out"]
```
